# Optimizing a Trainium2 kernel written in Bass

```python
import numpy as np
import jax
import jax.numpy as jnp

def _softmax(x, axis=-1):
    return jax.nn.softmax(x, axis=axis)

def _gelu(x):
    return jax.nn.gelu(x, approximate=True)

def _silu(x):
    return jax.nn.silu(x)

def _sigmoid(x):
    return jax.nn.sigmoid(x)

def _layernorm(x, axis=-1, eps=1e-05):
    m = jnp.mean(x, axis=axis, keepdims=True)
    v = jnp.var(x, axis=axis, keepdims=True)
    return (x - m) / jnp.sqrt(v + eps)

def _scatter_add(tgt, idx, src, axis=0):
    return tgt.at[idx].add(src)

def _segment_sum(src, seg, n):
    return jax.ops.segment_sum(src, seg, n)
kernel_name = 'mk_hybrid_d1_jaxref_r4_dfc40f'

def setup_inputs(seed: int=0):
    np.random.seed(seed)
    _w = jnp.asarray

    def _L0_attn_a_setup():
        import jax, jax.numpy as jnp
        import numpy as np
        B, T, D, H = (8, 1024, 256, 16)
        DK = D // H
        CHUNK = 64
        E, TOPK, MULT, CAPF = (8, 2, 4, 1.25)
        HID = D * MULT
        N = B * T
        CAPACITY = int(CAPF * (N / E))

        def rmsnorm(x, scale):
            return x / jnp.sqrt(jnp.mean(x * x, axis=-1, keepdims=True)) * scale

        def apply_rope(x):
            half = x.shape[-1] // 2
            t = x.shape[2]
            inv = 1.0 / 10000.0 ** (jnp.arange(half, dtype=jnp.float32) / half)
            ang = jnp.arange(t, dtype=jnp.float32)[:, None] * inv[None, :]
            sin, cos = (jnp.sin(ang)[None, None], jnp.cos(ang)[None, None])
            x1, x2 = (x[..., :half], x[..., half:])
            return jnp.concatenate([x1 * cos - x2 * sin, x1 * sin + x2 * cos], axis=-1)

        def phi(x):
            return jax.nn.elu(x) + 1.0

        def attention(x, Wq, bq, Wk, bk, Wv, bv, Wg, bg, Wo, bo):
            b, t, c = x.shape
            heads = lambda y: y.reshape(b, t, H, DK).transpose(0, 2, 1, 3)
            q = phi(apply_rope(heads(x @ Wq + bq)))
            k = phi(apply_rope(heads(x @ Wk + bk)))
            v = heads(x @ Wv + bv)
            g = heads(jax.nn.sigmoid(x @ Wg + bg))
            nc = t // CHUNK
            to_chunks = lambda y: y.reshape(b, H, nc, CHUNK, DK).transpose(2, 0, 1, 3, 4)
            qs, ks_, vs, gs = map(to_chunks, (q, k, v, g))
            S0 = jnp.zeros((b, H, DK, DK), x.dtype)
            Z0 = jnp.zeros((b, H, DK), x.dtype)

            def step(carry, inp):
                S, Z = carry
                qc, kc, vc, gc = inp
                S = S + jnp.einsum('bhtd,bhte->bhde', kc, vc)
                Z = Z + kc.sum(axis=2)
                num = jnp.einsum('bhtd,bhde->bhte', qc, S)
                den = jnp.einsum('bhtd,bhd->bht', qc, Z)[..., None] + 1e-06
                return ((S, Z), gc * (num / den))
            _, outs = jax.lax.scan(step, (S0, Z0), (qs, ks_, vs, gs))
            out = outs.transpose(1, 2, 0, 3, 4).reshape(b, H, t, DK)
            out = out.transpose(0, 2, 1, 3).reshape(b, t, c)
            return out @ Wo + bo

        def moe(x, router_W, router_b, W1, b1, W2, b2):
            b, t, c = x.shape
            n = b * t
            xf = x.reshape(n, c)
            probs = jax.nn.softmax(xf @ router_W + router_b, axis=-1)
            topk_probs, topk_idx = jax.lax.top_k(probs, TOPK)
            topk_probs = topk_probs / topk_probs.sum(axis=-1, keepdims=True)
            out = jnp.zeros_like(xf)
            load = []
            for eid in range(E):
                mask = (topk_idx == eid).reshape(-1)
                idx = jnp.nonzero(mask, size=CAPACITY, fill_value=n * TOPK)[0]
                valid = idx < n * TOPK
                idxc = jnp.minimum(idx, n * TOPK - 1)
                tok, choice = (idxc // TOPK, idxc % TOPK)
                h = jax.nn.gelu(xf[tok] @ W1[eid] + b1[eid], approximate=False) @ W2[eid] + b2[eid]
                gate = jnp.where(valid, topk_probs[tok, choice], 0.0)
                out = out.at[tok].add(gate[:, None] * h)
                load.append(jnp.minimum(mask.sum(), CAPACITY).astype(xf.dtype))
            load = jnp.stack(load)
            importance = probs.sum(axis=0)
            importance = importance / importance.sum()
            load = load / load.sum()
            aux = (importance * load).sum() * E ** 2
            return (out.reshape(b, t, c), aux)

        def _reference_tuple_inner(x, norm1_scale, norm2_scale, Wq, bq, Wk, bk, Wv, bv, Wg, bg, Wo, bo, router_W, router_b, W1, b1, W2, b2):
            x = x + attention(rmsnorm(x, norm1_scale), Wq, bq, Wk, bk, Wv, bv, Wg, bg, Wo, bo)
            moe_out, aux = moe(rmsnorm(x, norm2_scale), router_W, router_b, W1, b1, W2, b2)
            return (x + moe_out, aux)
        key = jax.random.key(seed)
        ks = jax.random.split(key, 16)
        s = 0.02
        r = lambda k, shape: jax.random.normal(k, shape, jnp.float32) * s
        return {'x': jax.random.normal(ks[0], (B, T, D), jnp.float32), 'norm1_scale': jnp.ones((D,), jnp.float32), 'norm2_scale': jnp.ones((D,), jnp.float32), 'Wq': r(ks[1], (D, D)), 'bq': jnp.zeros((D,), jnp.float32), 'Wk': r(ks[2], (D, D)), 'bk': jnp.zeros((D,), jnp.float32), 'Wv': r(ks[3], (D, D)), 'bv': jnp.zeros((D,), jnp.float32), 'Wg': r(ks[4], (D, D)), 'bg': jnp.zeros((D,), jnp.float32), 'Wo': r(ks[5], (D, D)), 'bo': jnp.zeros((D,), jnp.float32), 'router_W': r(ks[6], (D, E)), 'router_b': jnp.zeros((E,), jnp.float32), 'W1': r(ks[7], (E, D, HID)), 'b1': jnp.zeros((E, HID), jnp.float32), 'W2': r(ks[8], (E, HID, D)), 'b2': jnp.zeros((E, D), jnp.float32)}
    _L0_attn_a_in = _L0_attn_a_setup()

    def _L0_attn_b_setup():
        import jax, jax.numpy as jnp
        import numpy as np
        B, N, DIM, H = (8, 1024, 256, 16)
        D = DIM // H
        EPS_NORM = 1e-12
        EPS_PI = 1e-08
        key = jax.random.key(seed)
        k1, k2, k3 = jax.random.split(key, 3)
        x = jax.random.normal(k1, (B, N, DIM), dtype=jnp.float32)
        Wqkv = jax.random.normal(k2, (DIM, DIM), dtype=jnp.float32) * (1.0 / np.sqrt(DIM))
        temp = jnp.ones((H, 1), dtype=jnp.float32)
        Wout = jax.random.normal(k3, (DIM, DIM), dtype=jnp.float32) * (1.0 / np.sqrt(DIM))
        bout = jnp.zeros((DIM,), dtype=jnp.float32)
        return {'x': x, 'Wqkv': Wqkv, 'temp': temp, 'Wout': Wout, 'bout': bout}
    _L0_attn_b_in = _L0_attn_b_setup()

    def _L0_ffn_setup():
        import jax, jax.numpy as jnp
        import numpy as np
        H, HP, NH_M, NH_D = (256, 64, 8, 8)
        B, T = (2, 512)
        SPARSITY = 8
        N_ROT = 32
        BASE = 10000.0

        def _rope(x, pos, n_rot, base):
            half = n_rot // 2
            inv = base ** (-jnp.arange(half, dtype=x.dtype) / half)
            ang = pos[..., None] * inv
            cos, sin = (jnp.cos(ang), jnp.sin(ang))
            x1, x2 = (x[..., :half], x[..., half:n_rot])
            rot = jnp.concatenate([x1 * cos - x2 * sin, x1 * sin + x2 * cos], axis=-1)
            return jnp.concatenate([rot, x[..., n_rot:]], axis=-1)

        def _mosa_branch(X, router_w, wqkv, wo):
            b, t, _ = X.shape
            k = t // SPARSITY
            scores = jnp.einsum('bth,hn->bnt', X, router_w)
            _, idx = jax.lax.top_k(scores, k)
            idx = jnp.sort(idx, axis=-1)
            gates = jax.nn.sigmoid(jnp.take_along_axis(scores, idx, axis=-1))
            Xg = jnp.take_along_axis(X[:, None], idx[..., None], axis=2)
            qkv = jnp.einsum('bnkh,hnd->bnkd', Xg, wqkv)
            Q, K, V = jnp.split(qkv, 3, axis=-1)
            pos = idx.astype(X.dtype)
            Q = _rope(Q, pos, N_ROT, BASE)
            K = _rope(K, pos, N_ROT, BASE)
            att = jnp.einsum('bnqd,bnkd->bnqk', Q, K) / jnp.sqrt(jnp.asarray(HP, X.dtype))
            causal = idx[..., :, None] >= idx[..., None, :]
            att = jnp.where(causal, att, -jnp.inf)
            AV = jnp.einsum('bnqk,bnkd->bnqd', jax.nn.softmax(att, axis=-1), V)
            AV = AV * gates[..., None]
            out = jnp.zeros((b, NH_M, t, HP), X.dtype)
            bi = jnp.arange(b)[:, None, None]
            hi = jnp.arange(NH_M)[None, :, None]
            out = out.at[bi, hi, idx].set(AV)
            out = out.transpose(0, 2, 1, 3).reshape(b, t, NH_M * HP)
            return out @ wo

        def _dense_branch(X, wqkv, wo):
            b, t, _ = X.shape
            qkv = jnp.einsum('bth,hnd->bntd', X, wqkv)
            Q, K, V = jnp.split(qkv, 3, axis=-1)
            pos = jnp.arange(t, dtype=X.dtype)
            Q = _rope(Q, pos, N_ROT, BASE)
            K = _rope(K, pos, N_ROT, BASE)
            att = jnp.einsum('bnqd,bnkd->bnqk', Q, K) / jnp.sqrt(jnp.asarray(HP, X.dtype))
            causal = jnp.tril(jnp.ones((t, t), bool))
            att = jnp.where(causal, att, -jnp.inf)
            AV = jnp.einsum('bnqk,bnkd->bnqd', jax.nn.softmax(att, axis=-1), V)
            return AV.transpose(0, 2, 1, 3).reshape(b, t, NH_D * HP) @ wo
        key = jax.random.key(seed)
        ks = jax.random.split(key, 6)
        s = 0.02
        return {'X': jax.random.normal(ks[0], (B, T, H), jnp.float32), 'mosa_router_w': jax.random.normal(ks[1], (H, NH_M), jnp.float32) * s, 'mosa_wqkv': jax.random.normal(ks[2], (H, NH_M, 3 * HP), jnp.float32) * s, 'mosa_wo': jax.random.normal(ks[3], (NH_M * HP, H), jnp.float32) * s, 'dense_wqkv': jax.random.normal(ks[4], (H, NH_D, 3 * HP), jnp.float32) * s, 'dense_wo': jax.random.normal(ks[5], (NH_D * HP, H), jnp.float32) * s}
    _L0_ffn_in = _L0_ffn_setup()
    _d = {'L0_attn_a_x': _L0_attn_a_in['x'], 'L0_attn_a_norm1_scale': _L0_attn_a_in['norm1_scale'], 'L0_attn_a_norm2_scale': _L0_attn_a_in['norm2_scale'], 'L0_attn_a_Wq': _L0_attn_a_in['Wq'], 'L0_attn_a_bq': _L0_attn_a_in['bq'], 'L0_attn_a_Wk': _L0_attn_a_in['Wk'], 'L0_attn_a_bk': _L0_attn_a_in['bk'], 'L0_attn_a_Wv': _L0_attn_a_in['Wv'], 'L0_attn_a_bv': _L0_attn_a_in['bv'], 'L0_attn_a_Wg': _L0_attn_a_in['Wg'], 'L0_attn_a_bg': _L0_attn_a_in['bg'], 'L0_attn_a_Wo': _L0_attn_a_in['Wo'], 'L0_attn_a_bo': _L0_attn_a_in['bo'], 'L0_attn_a_router_W': _L0_attn_a_in['router_W'], 'L0_attn_a_router_b': _L0_attn_a_in['router_b'], 'L0_attn_a_W1': _L0_attn_a_in['W1'], 'L0_attn_a_b1': _L0_attn_a_in['b1'], 'L0_attn_a_W2': _L0_attn_a_in['W2'], 'L0_attn_a_b2': _L0_attn_a_in['b2'], 'L0_attn_b_Wqkv': _L0_attn_b_in['Wqkv'], 'L0_attn_b_temp': _L0_attn_b_in['temp'], 'L0_attn_b_Wout': _L0_attn_b_in['Wout'], 'L0_attn_b_bout': _L0_attn_b_in['bout'], 'L0_ffn_mosa_router_w': _L0_ffn_in['mosa_router_w'], 'L0_ffn_mosa_wqkv': _L0_ffn_in['mosa_wqkv'], 'L0_ffn_mosa_wo': _L0_ffn_in['mosa_wo'], 'L0_ffn_dense_wqkv': _L0_ffn_in['dense_wqkv'], 'L0_ffn_dense_wo': _L0_ffn_in['dense_wo']}
    _x0 = _d['L0_attn_a_x']
    _d['L0_attn_a_x'] = jax.random.normal(jax.random.fold_in(jax.random.key(seed), 1), (16, 512, 256), dtype=_x0.dtype)
    del _x0
    return _d

def reference(L0_attn_a_x, L0_attn_a_norm1_scale, L0_attn_a_norm2_scale, L0_attn_a_Wq, L0_attn_a_bq, L0_attn_a_Wk, L0_attn_a_bk, L0_attn_a_Wv, L0_attn_a_bv, L0_attn_a_Wg, L0_attn_a_bg, L0_attn_a_Wo, L0_attn_a_bo, L0_attn_a_router_W, L0_attn_a_router_b, L0_attn_a_W1, L0_attn_a_b1, L0_attn_a_W2, L0_attn_a_b2, L0_attn_b_Wqkv, L0_attn_b_temp, L0_attn_b_Wout, L0_attn_b_bout, L0_ffn_mosa_router_w, L0_ffn_mosa_wqkv, L0_ffn_mosa_wo, L0_ffn_dense_wqkv, L0_ffn_dense_wo):

    def _L0_attn_a_ref(x, norm1_scale, norm2_scale, Wq, bq, Wk, bk, Wv, bv, Wg, bg, Wo, bo, router_W, router_b, W1, b1, W2, b2):
        import jax, jax.numpy as jnp
        import numpy as np
        B, T, D, H = (8, 1024, 256, 16)
        DK = D // H
        CHUNK = 64
        E, TOPK, MULT, CAPF = (8, 2, 4, 1.25)
        HID = D * MULT
        N = B * T
        CAPACITY = int(CAPF * (N / E))

        def rmsnorm(x, scale):
            return x / jnp.sqrt(jnp.mean(x * x, axis=-1, keepdims=True)) * scale

        def apply_rope(x):
            half = x.shape[-1] // 2
            t = x.shape[2]
            inv = 1.0 / 10000.0 ** (jnp.arange(half, dtype=jnp.float32) / half)
            ang = jnp.arange(t, dtype=jnp.float32)[:, None] * inv[None, :]
            sin, cos = (jnp.sin(ang)[None, None], jnp.cos(ang)[None, None])
            x1, x2 = (x[..., :half], x[..., half:])
            return jnp.concatenate([x1 * cos - x2 * sin, x1 * sin + x2 * cos], axis=-1)

        def phi(x):
            return jax.nn.elu(x) + 1.0

        def attention(x, Wq, bq, Wk, bk, Wv, bv, Wg, bg, Wo, bo):
            b, t, c = x.shape
            heads = lambda y: y.reshape(b, t, H, DK).transpose(0, 2, 1, 3)
            q = phi(apply_rope(heads(x @ Wq + bq)))
            k = phi(apply_rope(heads(x @ Wk + bk)))
            v = heads(x @ Wv + bv)
            g = heads(jax.nn.sigmoid(x @ Wg + bg))
            nc = t // CHUNK
            to_chunks = lambda y: y.reshape(b, H, nc, CHUNK, DK).transpose(2, 0, 1, 3, 4)
            qs, ks_, vs, gs = map(to_chunks, (q, k, v, g))
            S0 = jnp.zeros((b, H, DK, DK), x.dtype)
            Z0 = jnp.zeros((b, H, DK), x.dtype)

            def step(carry, inp):
                S, Z = carry
                qc, kc, vc, gc = inp
                S = S + jnp.einsum('bhtd,bhte->bhde', kc, vc)
                Z = Z + kc.sum(axis=2)
                num = jnp.einsum('bhtd,bhde->bhte', qc, S)
                den = jnp.einsum('bhtd,bhd->bht', qc, Z)[..., None] + 1e-06
                return ((S, Z), gc * (num / den))
            _, outs = jax.lax.scan(step, (S0, Z0), (qs, ks_, vs, gs))
            out = outs.transpose(1, 2, 0, 3, 4).reshape(b, H, t, DK)
            out = out.transpose(0, 2, 1, 3).reshape(b, t, c)
            return out @ Wo + bo

        def moe(x, router_W, router_b, W1, b1, W2, b2):
            b, t, c = x.shape
            n = b * t
            xf = x.reshape(n, c)
            probs = jax.nn.softmax(xf @ router_W + router_b, axis=-1)
            topk_probs, topk_idx = jax.lax.top_k(probs, TOPK)
            topk_probs = topk_probs / topk_probs.sum(axis=-1, keepdims=True)
            out = jnp.zeros_like(xf)
            load = []
            for eid in range(E):
                mask = (topk_idx == eid).reshape(-1)
                idx = jnp.nonzero(mask, size=CAPACITY, fill_value=n * TOPK)[0]
                valid = idx < n * TOPK
                idxc = jnp.minimum(idx, n * TOPK - 1)
                tok, choice = (idxc // TOPK, idxc % TOPK)
                h = jax.nn.gelu(xf[tok] @ W1[eid] + b1[eid], approximate=False) @ W2[eid] + b2[eid]
                gate = jnp.where(valid, topk_probs[tok, choice], 0.0)
                out = out.at[tok].add(gate[:, None] * h)
                load.append(jnp.minimum(mask.sum(), CAPACITY).astype(xf.dtype))
            load = jnp.stack(load)
            importance = probs.sum(axis=0)
            importance = importance / importance.sum()
            load = load / load.sum()
            aux = (importance * load).sum() * E ** 2
            return (out.reshape(b, t, c), aux)

        def _reference_tuple_inner(x, norm1_scale, norm2_scale, Wq, bq, Wk, bk, Wv, bv, Wg, bg, Wo, bo, router_W, router_b, W1, b1, W2, b2):
            x = x + attention(rmsnorm(x, norm1_scale), Wq, bq, Wk, bk, Wv, bv, Wg, bg, Wo, bo)
            moe_out, aux = moe(rmsnorm(x, norm2_scale), router_W, router_b, W1, b1, W2, b2)
            return (x + moe_out, aux)
        return _reference_tuple_inner(x, norm1_scale, norm2_scale, Wq, bq, Wk, bk, Wv, bv, Wg, bg, Wo, bo, router_W, router_b, W1, b1, W2, b2)[0]

    def _L0_attn_b_ref(x, Wqkv, temp, Wout, bout):
        import jax, jax.numpy as jnp
        import numpy as np
        B, N, DIM, H = (8, 1024, 256, 16)
        D = DIM // H
        EPS_NORM = 1e-12
        EPS_PI = 1e-08
        b, n, dim = x.shape
        h, d = (H, dim // H)
        w = (x @ Wqkv.T).reshape(b, n, h, d).transpose(0, 2, 1, 3)
        norm = jnp.sqrt(jnp.sum(w * w, axis=-2, keepdims=True))
        w_normed = w / jnp.maximum(norm, EPS_NORM)
        logits = jnp.sum(w_normed * w_normed, axis=-1) * temp[None, :, :]
        Pi = jax.nn.softmax(logits, axis=1)
        Pi_norm = Pi / (jnp.sum(Pi, axis=-1, keepdims=True) + EPS_PI)
        dots = jnp.einsum('bhn,bhnd->bhd', Pi_norm, w * w)
        attn = 1.0 / (1.0 + dots)
        out = -(w * Pi[..., None]) * attn[:, :, None, :]
        out = out.transpose(0, 2, 1, 3).reshape(b, n, dim)
        return out @ Wout.T + bout

    def _L0_ffn_ref(X, mosa_router_w, mosa_wqkv, mosa_wo, dense_wqkv, dense_wo):
        import jax, jax.numpy as jnp
        import numpy as np
        H, HP, NH_M, NH_D = (256, 64, 8, 8)
        B, T = (2, 512)
        SPARSITY = 8
        N_ROT = 32
        BASE = 10000.0

        def _rope(x, pos, n_rot, base):
            half = n_rot // 2
            inv = base ** (-jnp.arange(half, dtype=x.dtype) / half)
            ang = pos[..., None] * inv
            cos, sin = (jnp.cos(ang), jnp.sin(ang))
            x1, x2 = (x[..., :half], x[..., half:n_rot])
            rot = jnp.concatenate([x1 * cos - x2 * sin, x1 * sin + x2 * cos], axis=-1)
            return jnp.concatenate([rot, x[..., n_rot:]], axis=-1)

        def _mosa_branch(X, router_w, wqkv, wo):
            b, t, _ = X.shape
            k = t // SPARSITY
            scores = jnp.einsum('bth,hn->bnt', X, router_w)
            _, idx = jax.lax.top_k(scores, k)
            idx = jnp.sort(idx, axis=-1)
            gates = jax.nn.sigmoid(jnp.take_along_axis(scores, idx, axis=-1))
            Xg = jnp.take_along_axis(X[:, None], idx[..., None], axis=2)
            qkv = jnp.einsum('bnkh,hnd->bnkd', Xg, wqkv)
            Q, K, V = jnp.split(qkv, 3, axis=-1)
            pos = idx.astype(X.dtype)
            Q = _rope(Q, pos, N_ROT, BASE)
            K = _rope(K, pos, N_ROT, BASE)
            att = jnp.einsum('bnqd,bnkd->bnqk', Q, K) / jnp.sqrt(jnp.asarray(HP, X.dtype))
            causal = idx[..., :, None] >= idx[..., None, :]
            att = jnp.where(causal, att, -jnp.inf)
            AV = jnp.einsum('bnqk,bnkd->bnqd', jax.nn.softmax(att, axis=-1), V)
            AV = AV * gates[..., None]
            out = jnp.zeros((b, NH_M, t, HP), X.dtype)
            bi = jnp.arange(b)[:, None, None]
            hi = jnp.arange(NH_M)[None, :, None]
            out = out.at[bi, hi, idx].set(AV)
            out = out.transpose(0, 2, 1, 3).reshape(b, t, NH_M * HP)
            return out @ wo

        def _dense_branch(X, wqkv, wo):
            b, t, _ = X.shape
            qkv = jnp.einsum('bth,hnd->bntd', X, wqkv)
            Q, K, V = jnp.split(qkv, 3, axis=-1)
            pos = jnp.arange(t, dtype=X.dtype)
            Q = _rope(Q, pos, N_ROT, BASE)
            K = _rope(K, pos, N_ROT, BASE)
            att = jnp.einsum('bnqd,bnkd->bnqk', Q, K) / jnp.sqrt(jnp.asarray(HP, X.dtype))
            causal = jnp.tril(jnp.ones((t, t), bool))
            att = jnp.where(causal, att, -jnp.inf)
            AV = jnp.einsum('bnqk,bnkd->bnqd', jax.nn.softmax(att, axis=-1), V)
            return AV.transpose(0, 2, 1, 3).reshape(b, t, NH_D * HP) @ wo
        return _mosa_branch(X, mosa_router_w, mosa_wqkv, mosa_wo) + _dense_branch(X, dense_wqkv, dense_wo)
    x = L0_attn_a_x
    x = x + _L0_attn_a_ref(_layernorm(x, axis=-1), L0_attn_a_norm1_scale, L0_attn_a_norm2_scale, L0_attn_a_Wq, L0_attn_a_bq, L0_attn_a_Wk, L0_attn_a_bk, L0_attn_a_Wv, L0_attn_a_bv, L0_attn_a_Wg, L0_attn_a_bg, L0_attn_a_Wo, L0_attn_a_bo, L0_attn_a_router_W, L0_attn_a_router_b, L0_attn_a_W1, L0_attn_a_b1, L0_attn_a_W2, L0_attn_a_b2)
    x = x + _L0_ffn_ref(_layernorm(x, axis=-1), L0_ffn_mosa_router_w, L0_ffn_mosa_wqkv, L0_ffn_mosa_wo, L0_ffn_dense_wqkv, L0_ffn_dense_wo)
    x = x + _L0_attn_b_ref(_layernorm(x, axis=-1), L0_attn_b_Wqkv, L0_attn_b_temp, L0_attn_b_Wout, L0_attn_b_bout)
    x = x + _L0_ffn_ref(_layernorm(x, axis=-1), L0_ffn_mosa_router_w, L0_ffn_mosa_wqkv, L0_ffn_mosa_wo, L0_ffn_dense_wqkv, L0_ffn_dense_wo)
    return x

_drawn_inputs = setup_inputs


def setup_inputs(seed=0):
    import zlib

    import numpy as np

    out = dict(_drawn_inputs(seed))
    spreads = {'L0_attn_a_norm1_scale': (1.0, 0.6),
     'L0_attn_a_norm2_scale': (1.0, 0.6),
     'L0_attn_a_bq': (0.0, 0.8),
     'L0_attn_a_bk': (0.0, 0.8),
     'L0_attn_a_bv': (0.0, 0.638),
     'L0_attn_a_bg': (0.0, 0.8),
     'L0_attn_a_bo': (0.0, 0.1),
     'L0_attn_a_router_b': (0.0, 0.1),
     'L0_attn_a_b1': (0.0, 0.791),
     'L0_attn_a_b2': (0.0, 0.288),
     'L0_attn_b_temp': (1.0, 0.6),
     'L0_attn_b_bout': (0.0, 0.1)}
    factors = {'L0_attn_a_Wq': 8.0,
     'L0_attn_a_Wk': 8.0,
     'L0_attn_a_Wv': 8.0,
     'L0_attn_a_Wg': 8.0,
     'L0_attn_a_Wo': 5.052,
     'L0_attn_b_Wqkv': 3.651,
     'L0_attn_b_Wout': 3.608,
     'L0_ffn_mosa_router_w': 6.081,
     'L0_ffn_mosa_wqkv': 6.039,
     'L0_ffn_mosa_wo': 5.985,
     'L0_ffn_dense_wqkv': 3.017,
     'L0_ffn_dense_wo': 3.039}
    for name, (base, spread) in spreads.items():
        noise = np.random.default_rng([zlib.crc32(name.encode()), seed]).standard_normal(out[name].shape)
        drawn = base * np.exp(spread * noise) if base else spread * noise
        out[name] = jnp.asarray(drawn.astype(out[name].dtype))
    for name, factor in factors.items():
        out[name] = (out[name] * factor).astype(out[name].dtype)
    return out
```

```python
import concourse.bass as bass
from concourse import mybir
from contextlib import ExitStack
import numpy as np

F32 = mybir.dt.float32
BF16 = mybir.dt.bfloat16
F16 = mybir.dt.float16
I32 = mybir.dt.int32
U32 = mybir.dt.uint32
ALU = mybir.AluOpType
ACT = mybir.ActivationFunctionType
AX = mybir.AxisListType.X

P = 128
NB, NT, D = 16, 512, 256
TOK = NB * NT
TILES = NT // P
KC = D // P
HA, DA = 16, 16
CH = 64
NCH = NT // CH
VA = DA + 1
GRP = P // DA
NE, HID, TOPK = 8, 1024, 2
CAP = int(1.25 * (TOK / NE))
MC = HID // P
NH, HP = 8, 64
ROT = 32
SLOTS = NT // 8
PAIRS = NH // 2
HB, DB = 16, 16
LN_EPS = 1e-5
NEG = -1e30


class Sig:

    def __init__(self, ctx, nc, name, per=1, by=1):
        self.sem = ctx.enter_context(nc.semaphore(name))
        self.name, self.per, self.by = name, per, by
        self.up = (self.sem, by)

    def __call__(self, r, n=None):
        return self.sem, ((r.at if isinstance(r, Round) else r) * self.per + (self.per if n is None else n)) * self.by


class Chain:

    def __init__(self, eng, sig, r):
        self.eng, self.sig, self.r, self.n = eng, sig, r, 0

    def inc(self, ins):
        ins.then_inc(*self.sig.up)
        self.n += 1

    def sync(self):
        self.eng.wait_ge(*self.sig(self.r, self.n))

    def link(self, ins):
        self.inc(ins)
        self.sync()

    def end(self):
        assert self.n == self.sig.per, (self.sig.name, self.n, self.sig.per)


def rounds(eng, count, body):
    for k in range(2):
        body(Round(0, k), k, k)
    with eng.Fori(1, count // 2) as i:
        for p in range(2):
            body(Round(i, p), p, None)


class Round:

    def __init__(self, half, parity):
        self.half, self.parity = half, parity
        self.at = half * 2 + parity

    def __sub__(self, n):
        p = self.parity - n
        return Round(self.half + p // 2, p % 2)


def overlapped(eng, count, order, step):
    def pair(r, k, nxt, k_next):
        for name in order:
            if name.startswith("b_"):
                step(name, r, r.parity, k)
            elif nxt is not None:
                step(name, nxt, nxt.parity, k_next)

    for name in order:
        if not name.startswith("b_"):
            step(name, Round(0, 0), 0, 0)
    pair(Round(0, 0), 0, Round(0, 1), 1)
    pair(Round(0, 1), 1, Round(1, 0), None)
    with eng.Fori(1, count // 2 - 1) as i:
        pair(Round(i, 0), None, Round(i, 1), None)
        pair(Round(i, 1), None, Round(i + 1, 0), None)
    last = count // 2 - 1
    pair(Round(last, 0), None, Round(last, 1), None)
    pair(Round(last, 1), None, None, None)


A_ORDER = {
    "sp": "x b_res",
    "pool": "ln b_res sum b_send",
    "pe": "b_o ln t0 t1 b_hn t2 t3 b_rank kv qT num",
    "act": "b_o ln b_square t0 b_hn t1 t2 t3 qT b_gate",
    "dve": "ln b_y b_hn t0 t1 b_route t2 t3 fin sum b_slots o",
}


def settle(eng):
    eng.nop(nofuse=True)


class TwoSig:

    def __init__(self, ctx, nc, name, per=1, by=16):
        self.sig = [Sig(ctx, nc, name + s, per, by) for s in ("_even", "_odd")]

    def up(self, r):
        return self.sig[r.parity].up

    def __call__(self, r, n=None):
        return self.sig[r.parity](r.half, n)


RSQRT_STEPS = 11


def rsqrt(nc, chain, y, v, t, part=None):
    if part != 1:
        chain.link(nc.vector.tensor_scalar(y.bitcast(I32), v.bitcast(I32), 1, None, ALU.logical_shift_right))
        chain.link(nc.vector.tensor_scalar(y.bitcast(I32), y.bitcast(I32), -1.0, 1597463007.0, ALU.mult, ALU.add))
    for _ in range({None: 3, 0: 1, 1: 2}[part]):
        chain.link(nc.vector.scalar_tensor_tensor(t, y, -0.5, y, ALU.mult, ALU.mult))
        chain.link(nc.vector.tensor_tensor(t, t, v, ALU.mult))
        chain.link(nc.vector.scalar_tensor_tensor(y, t, 1.5, y, ALU.add, ALU.mult))


def over(ap, *dims):
    return bass.AP(ap.tensor, ap.offset, [list(ap.ap[0])] + [list(d) for d in dims])


def attention_a_stage(nc, a):
    with ExitStack() as ctx:
        sb = lambda name, shape, dt=F32: ctx.enter_context(nc.sbuf_tensor(name, shape, dt))
        sig = lambda name, per=1, by=1: Sig(ctx, nc, "a_" + name, per, by)
        two = lambda name, per=1: TwoSig(ctx, nc, "a_" + name, per)
        ps = [ctx.enter_context(nc.psum_tensor(f"a_ps{i}", [P, 512], F32)) for i in range(8)]
        ident = sb("a_ident", [P, P])
        wqkvg = sb("a_wqkvg", [P, KC, 4 * D])
        wo = sb("a_wo", [P, KC, D])
        rw = sb("a_rw", [P, KC, NE])
        s1 = sb("a_s1", [P, KC])
        s2b = sb("a_s2b", [P, D])
        bqkvg = sb("a_bqkvg", [P, 4 * D])
        bo = sb("a_bo", [P, D])
        rb = sb("a_rb", [P, NE])
        cosa = sb("a_cos", [P, TILES, DA])
        sina = sb("a_sin", [P, TILES, DA])
        bd = sb("a_bd", [P, 2 * GRP * VA])
        before = sb("a_before", [P, P], BF16)
        ones = sb("a_ones", [P, P], BF16)
        iota8 = sb("a_iota8", [P, TOPK, NE])
        xs = sb("a_x", [P, 2, TILES, D])
        stats = sb("a_stats", [P, TILES, 6])
        mv = sb("a_mv", [P, TILES, 2])
        v2 = sb("a_v2", [P, 2, TILES])
        rs = sb("a_rs", [P, 2, TILES])
        rt = sb("a_rt", [P, 2, TILES])
        h = sb("a_h", [P, TILES, D])
        hb = sb("a_hb", [P, TILES, D])
        u = sb("a_u", [P, TILES, D])
        uT = sb("a_uT", [P, KC, NT])
        qk = sb("a_qk", [P, TILES, 2 * D])
        ra = sb("a_ra", [P, 2 * D])
        rc = sb("a_rc", [P, 2 * D])
        mn = sb("a_mn", [P, TILES, 2 * D])
        va = sb("a_va", [P, TILES, HA, VA])
        z = sb("a_z", [P, TILES, D])
        run = sb("a_run", [P, NCH, 2 * GRP * VA])
        state = sb("a_state", [P, NCH, 2 * GRP * VA])
        qT = sb("a_qT", [P, KC, NT])
        den = sb("a_den", [P, HA])
        dd = sb("a_dd", [P, D])
        o = sb("a_o", [P, TILES, D])
        oT = sb("a_oT", [P, KC, NT])
        y = sb("a_y", [P, TILES, D])
        sq = sb("a_sq", [P, D])
        ssq = sb("a_ssq", [P, TILES])
        ssn = sb("a_ssn", [P, TILES])
        rr = sb("a_rr", [P, TILES])
        rrt = sb("a_rrt", [P, TILES])
        hn = sb("a_hn", [P, 2, TILES, D])
        hnT = sb("a_hnT", [P, KC, NT])
        res = sb("a_res", [P, 2, TILES, D])
        lg = sb("a_lg", [P, TILES, NE])
        top = sb("a_top", [P, TILES, 8])
        topi = sb("a_topi", [P, TILES, 8], U32)
        ef = sb("a_ef", [P, TILES, TOPK])
        oh = sb("a_oh", [P, TILES, TOPK, NE])
        msk = sb("a_msk", [P, TILES, NE], BF16)
        rank = sb("a_rank", [P, TILES, NE])
        carry = sb("a_carry", [P, NE])
        rk = sb("a_rk", [P, TILES, TOPK, NE])
        rsel = sb("a_rsel", [P, TILES, TOPK])
        ok = sb("a_ok", [P, TILES, TOPK])
        slf = sb("a_slf", [P, TILES, TOPK])
        sld = sb("a_sld", [P, TILES, TOPK])
        sli = sb("a_sli", [P, 2, TILES, TOPK], U32)
        ge = sb("a_ge", [P, TILES])
        gd = sb("a_gd", [P, TILES])
        gg = sb("a_gg", [P, TILES, TOPK])
        zero = sb("a_zero", [P, 2560])
        slot_of, gate_of = a["slot_of"], a["gate_of"]

        consts = [(ident[:], a["ident"]), (wqkvg[:], a["wqkvg"].rearrange("(k p) n -> p k n", p=P)),
                  (wo[:], a["wo"].rearrange("(k p) n -> p k n", p=P)),
                  (rw[:], a["rw"].rearrange("(k p) n -> p k n", p=P)), (s1[:], a["s1"]), (s2b[:], a["s2b"]),
                  (bqkvg[:], a["bqkvg"]), (bo[:], a["bo"]), (rb[:], a["rb"]), (cosa[:], a["cosa"]),
                  (sina[:], a["sina"]), (bd[:], a["bd"]), (before[:], a["before"]), (iota8[:], a["iota8"])]
        const_in = sig("const_in", len(consts), 16)
        zeroed = sig("zeroed")
        cleared = sig("cleared", 8, 16)
        ones_set = sig("ones_set", 3)
        w_scaled = sig("w_scaled", KC)
        x_in = two("x_in")
        normed = sig("normed", 18 + RSQRT_STEPS)
        hb_made = sig("hb_made")
        flipped = sig("flipped", 4)
        evac = sig("evac", 4)
        b_flipped = sig("b_flipped", 4)
        b_evac = sig("b_evac", 4)
        proj = sig("proj", 2 * TILES)
        qk_step = sig("qk_step", 5 * TILES)
        vg_step = sig("vg_step", 3 * TILES)
        e_qk = sig("e_qk", TILES)
        e_z = sig("e_z", TILES)
        phi = sig("phi", TILES)
        kv = sig("kv", NCH)
        summed = sig("summed", NCH)
        masked = sig("masked", NCH)
        num = sig("num", TILES)
        o_step = sig("o_step", 4 * TILES)
        ao = sig("ao", TILES)
        y_made = sig("y_made", TILES)
        squared = sig("squared", TILES)
        hn_step = sig("hn_step", 1 + RSQRT_STEPS + TILES)
        res_made = sig("res_made")
        res_out = two("res_out")
        logit = sig("logit")
        route = sig("route", 15)
        ranked = sig("ranked")
        g_exp = sig("g_exp")
        slots = sig("slots", 15)
        gates_sig = sig("gates", 2)
        sent = two("sent", TILES * TOPK)

        with nc.Block() as block:

            @block.sync
            def _(sp):
                for to, of in consts:
                    sp.dma_start(to, of).then_inc(*const_in.up)

                def step(s, r, p, k):
                    if s == "x":
                        if k is None:
                            sp.wait_ge(*res_made(r - 2))
                        sp.dma_start(xs[:, p], a["x"][r.at].rearrange("(t p) n -> p t n", p=P)).then_inc(*x_in.up(r))
                    else:
                        sp.wait_ge(*res_made(r))
                        sp.dma_start(a["resid"][r.at].rearrange("(t p) n -> p t n", p=P), res[:, p]).then_inc(*res_out.up(r))

                overlapped(sp, NB, A_ORDER["sp"].split(), step)
                last = Round(NB // 2 - 1, 1)
                sp.wait_ge(*res_out(last - 1))
                sp.wait_ge(*res_out(last))

            @block.gpsimd
            def _(pool):
                nc.gpsimd.memset(zero[:], 0.0).then_inc(*zeroed.up)
                pool.wait_ge(*zeroed(0))
                n = NE * CAP * D // (8 * 2560)
                cells = a["dispatched"].rearrange("r n -> (r n)").rearrange("(c p n) -> c p n", c=8, p=n)
                for c in range(8):
                    pool.dma_start(cells[c], zero[0:n, :]).then_inc(*cleared.up)
                pool.wait_ge(*const_in(0))

                def step(s_, r, p, k):
                    if s_ == "ln":
                        pool.wait_ge(*normed(r))
                        if k is None or k >= 1:
                            pool.wait_ge(*y_made(r - 1))
                        nc.gpsimd.tensor_tensor(hb[:], h[:], over(bo[:], [0, TILES], [1, D]), ALU.add).then_inc(*hb_made.up)
                    elif s_ == "sum":
                        if k is None or k >= 1:
                            pool.wait_ge(*num(r - 1))
                        for c in range(NCH):
                            pool.wait_ge(*summed(r, c + 1))
                            nc.gpsimd.tensor_tensor(state[:, c, :], run[:, c, :], bd[:], ALU.mult).then_inc(*masked.up)
                    elif s_ == "b_res":
                        pool.wait_ge(*y_made(r))
                        if k is None:
                            pool.wait_ge(*res_out(r - 2))
                        nc.gpsimd.tensor_tensor(res[:, p], xs[:, p], y[:], ALU.add).then_inc(*res_made.up)
                    elif s_ == "b_send":
                        pool.wait_ge(*slots(r))
                        if k == 0:
                            pool.wait_ge(*cleared(0))
                        settle(pool)
                        for t in range(TILES):
                            for c in range(TOPK):
                                pool.indirect_dma_start(
                                    a["dispatched"], bass.IndirectOffsetOnAxis(ap=sli[:, p, t, c:c + 1], axis=0),
                                    hn[:, p, t, :], None, bounds_check=NE * CAP - 1, oob_is_err=False).then_inc(*sent.up(r))

                overlapped(pool, NB, A_ORDER["pool"].split(), step)
                last = Round(NB // 2 - 1, 1)
                pool.wait_ge(*sent(last - 1))
                pool.wait_ge(*sent(last))

            @block.tensor
            def _(pe):
                pe.wait_ge(*const_in(0))
                pe.wait_ge(*w_scaled(0))
                pe.wait_ge(*ones_set(0))

                def flip(src, bank, up):
                    for c in range(KC):
                        for t in range(TILES):
                            ins = nc.tensor.transpose(ps[bank + c][:, t * P:(t + 1) * P], src(t, c), ident[:])
                        ins.then_inc(*up.up)

                def step(s_, r, p, k):
                    if s_ == "ln":
                        pe.wait_ge(*normed(r))
                        if k is None or k >= 1:
                            pe.wait_ge(*evac(r - 1))
                        flip(lambda t, c: u[:, t, c * P:(c + 1) * P], 0, flipped)
                    elif s_[0] == "t":
                        t = int(s_[1])
                        pe.wait_ge(*evac(r, 2))
                        for j in range(2):
                            if t:
                                pe.wait_ge(*(qk_step(r, 5 * t - 4) if j == 0 else vg_step(r, 3 * t - 1)))
                            elif k is None or k >= 1:
                                pe.wait_ge(*(qk_step(r - 1, 5 * TILES - 4) if j == 0 else vg_step(r - 1, 3 * TILES - 1)))
                            for c in range(KC):
                                ins = nc.tensor.matmul(ps[2 + j][:], uT[:, c, t * P:(t + 1) * P],
                                                       wqkvg[:, c, j * 512:(j + 1) * 512], start=c == 0, stop=c == KC - 1)
                            ins.then_inc(*proj.up)
                    elif s_ == "kv":
                        for c in range(NCH):
                            t, q = c // 2, (c % 2) * CH
                            pe.wait_ge(*phi(r, t + 1))
                            if c >= 2:
                                pe.wait_ge(*summed(r, c - 1))
                            elif k is None or k >= 1:
                                pe.wait_ge(*o_step(r - 1))
                            for g in range(2):
                                ins = nc.tensor.matmul(ps[4 + c % 2][:, g * GRP * VA:(g + 1) * GRP * VA],
                                                       qk[q:q + CH, t, D + g * P:D + (g + 1) * P],
                                                       va[q:q + CH, t, g * GRP:(g + 1) * GRP, :].rearrange("p h e -> p (h e)"), start=True, stop=True)
                            ins.then_inc(*kv.up)
                    elif s_ == "qT":
                        flip(lambda t, c: qk[:, t, c * P:(c + 1) * P], 0, flipped)
                        pe.wait_ge(*evac(r, 4))
                    elif s_ == "num":
                        for t in range(TILES):
                            if t >= 2:
                                pe.wait_ge(*o_step(r, 4 * (t - 2) + 4))
                            else:
                                pe.wait_ge(*summed(r, NCH - 1 + t))
                            for c in (2 * t, 2 * t + 1):
                                q = (c % 2) * CH
                                pe.wait_ge(*masked(r, c + 1))
                                for g in range(2):
                                    cols = slice(g * GRP * VA, (g + 1) * GRP * VA)
                                    ins = nc.tensor.matmul(ps[4 + t % 2][q:q + CH, cols], qT[:, g, c * CH:(c + 1) * CH],
                                                           state[:, c, cols], start=True, stop=True)
                            ins.then_inc(*num.up)
                    elif s_ == "b_o":
                        pe.wait_ge(*o_step(r))
                        if k is None or k >= 1:
                            pe.wait_ge(*slots(r - 1, 3))
                        flip(lambda t, c: o[:, t, c * P:(c + 1) * P], 6, b_flipped)
                        pe.wait_ge(*b_evac(r, 2))
                        for t in range(TILES):
                            for c in range(KC):
                                ins = nc.tensor.matmul(ps[6 + t // 2][:, (t % 2) * D:(t % 2 + 1) * D], oT[:, c, t * P:(t + 1) * P],
                                                       wo[:, c, :], start=c == 0, stop=c == KC - 1)
                            ins.then_inc(*ao.up)
                    elif s_ == "b_hn":
                        pe.wait_ge(*hn_step(r))
                        flip(lambda t, c: hn[:, p, t, c * P:(c + 1) * P], 6, b_flipped)
                        pe.wait_ge(*b_evac(r, 4))
                        for t in range(TILES):
                            for c in range(KC):
                                ins = nc.tensor.matmul(ps[6][:, t * NE:(t + 1) * NE], hnT[:, c, t * P:(t + 1) * P], rw[:, c, :],
                                                       start=c == 0, stop=c == KC - 1)
                        ins.then_inc(*logit.up)
                    elif s_ == "b_rank":
                        pe.wait_ge(*route(r))
                        nc.tensor.matmul(ps[7][:, 0:TILES * NE], before[:], msk[:].rearrange("p t e -> p (t e)"), start=True, stop=False)
                        for t in range(TILES - 1):
                            nc.tensor.matmul(ps[7][:, (t + 1) * NE:TILES * NE], ones[:],
                                             over(msk[:, t, :], [0, TILES - 1 - t], [1, NE]), start=False, stop=t == TILES - 2)
                        for t in range(TILES):
                            ins = nc.tensor.matmul(ps[7][:, TILES * NE:(TILES + 1) * NE], ones[:], msk[:, t, :],
                                                   start=t == 0, stop=t == TILES - 1)
                        ins.then_inc(*ranked.up)

                overlapped(pe, NB, A_ORDER["pe"].split(), step)

            @block.scalar
            def _(act):
                def step(s_, r, p, k):
                    def out(dst, n, bank, made, up):
                        for c in range(KC):
                            act.wait_ge(*made(r, n + c + 1))
                            nc.scalar.activation(dst[:, c, :], ps[bank + c][:], ACT.Copy).then_inc(*up.up)

                    if s_ == "ln":
                        if k is None or k >= 1:
                            act.wait_ge(*proj(r - 1))
                        out(uT, 0, 0, flipped, evac)
                    elif s_[0] == "t":
                        t = int(s_[1])
                        act.wait_ge(*qk_step(r, 5 * t + 5))
                        nc.scalar.activation(mn[:, t, :], mn[:, t, :], ACT.Exp).then_inc(*e_qk.up)
                        act.wait_ge(*vg_step(r, 3 * t + 3))
                        nc.scalar.activation(z[:, t, :], z[:, t, :], ACT.Exp).then_inc(*e_z.up)
                    elif s_ == "qT":
                        if k is None or k >= 1:
                            act.wait_ge(*num(r - 1))
                        out(qT, 2, 0, flipped, evac)
                    elif s_ == "b_o":
                        if k is None or k >= 1:
                            act.wait_ge(*ao(r - 1))
                        out(oT, 0, 6, b_flipped, b_evac)
                    elif s_ == "b_square":
                        for t in range(TILES):
                            act.wait_ge(*y_made(r, t + 1))
                            if t:
                                act.wait_ge(*squared(r, t))
                            elif k is None or k >= 1:
                                act.wait_ge(*hn_step(r - 1, 1))
                            nc.scalar.activation(sq[:], y[:, t, :], ACT.Square, accum_out=ssq[:, t:t + 1]).then_inc(*squared.up)
                    elif s_ == "b_hn":
                        if k is None or k >= 1:
                            act.wait_ge(*logit(r - 1))
                        out(hnT, 2, 6, b_flipped, b_evac)
                    elif s_ == "b_gate":
                        act.wait_ge(*slots(r, 1))
                        nc.scalar.activation(ge[:], gd[:], ACT.Exp).then_inc(*g_exp.up)

                overlapped(act, NB, A_ORDER["act"].split(), step)

            @block.vector
            def _(dve):
                nc.vector.memset(ones[:], 1.0).then_inc(*ones_set.up)
                nc.vector.memset(va[:], 1.0).then_inc(*ones_set.up)
                nc.vector.memset(carry[:], 0.0).then_inc(*ones_set.up)
                dve.wait_ge(*ones_set(0))
                dve.wait_ge(*const_in(0))
                for c in range(KC):
                    nc.vector.tensor_scalar(wqkvg[:, c, :], wqkvg[:, c, :], s1[:, c:c + 1], None, ALU.mult).then_inc(*w_scaled.up)

                def step(s_, r, p, k):
                    if s_ == "ln":
                        dve.wait_ge(*x_in(r))
                        n = Chain(dve, normed, r)
                        if k is None or k >= 1:
                            dve.wait_ge(*normed(r - 1))
                        for t in range(TILES):
                            n.inc(nc.vector.bn_stats(stats[:, t, :], xs[:, p, t, :]))
                        n.sync()
                        settle(dve)
                        for t in range(TILES):
                            n.inc(nc.vector.bn_aggr(mv[:, t, :], stats[:, t, :]))
                        n.sync()
                        n.inc(nc.vector.tensor_scalar(v2[:, 0, :], mv[:, :, 1], LN_EPS, None, ALU.add))
                        n.link(nc.vector.tensor_copy(v2[:, 1, :], mv[:, :, 1]))
                        rsqrt(nc, n, rs[:], v2[:], rt[:])
                        if k is None or k >= 1:
                            dve.wait_ge(*hb_made(r - 1))
                        for t in range(TILES):
                            n.inc(nc.vector.tensor_scalar(h[:, t, :], xs[:, p, t, :], mv[:, t, 0:1], rs[:, 0, t:t + 1],
                                                          ALU.subtract, ALU.mult))
                        if k is None or k >= 1:
                            dve.wait_ge(*flipped(r - 1, 2))
                        for t in range(TILES):
                            n.inc(nc.vector.tensor_scalar(u[:, t, :], xs[:, p, t, :], mv[:, t, 0:1], rs[:, 1, t:t + 1],
                                                          ALU.subtract, ALU.mult))
                        n.end()
                    elif s_[0] == "t" or s_ == "fin":
                        def finish(t):
                            dve.wait_ge(*e_qk(r, t + 1))
                            nc.vector.scalar_tensor_tensor(qk[:, t, :], qk[:, t, :], 0.0, mn[:, t, :], ALU.max, ALU.add).then_inc(*phi.up)

                        if s_ == "fin":
                            finish(TILES - 1)
                            return
                        t = int(s_[1])
                        q, w = Chain(dve, qk_step, r), Chain(dve, vg_step, r)
                        q.n, w.n = 5 * t, 3 * t
                        if t == 0 and (k is None or k >= 1):
                            dve.wait_ge(*flipped(r - 1))
                            dve.wait_ge(*kv(r - 1))
                            dve.wait_ge(*o_step(r - 1))
                        dve.wait_ge(*proj(r, 2 * t + 1))
                        q.link(nc.vector.tensor_tensor(qk[:, t, :], ps[2][:], bqkvg[:, 0:512], ALU.add))
                        x3 = qk[:, t, :].rearrange("p (h s d) -> p h s d", s=2, d=DA // 2)
                        q.inc(nc.vector.tensor_tensor(ra[:].rearrange("p (h d) -> p h d", d=DA),
                                                      qk[:, t, :].rearrange("p (h d) -> p h d", d=DA),
                                                      over(cosa[:, t, :], [0, 2 * HA], [1, DA]), ALU.mult))
                        q.link(nc.vector.tensor_tensor(rc[:].rearrange("p (h s d) -> p h s d", s=2, d=DA // 2), x3[:, :, ::-1, :],
                                                       over(sina[:, t, :], [0, 2 * HA], [DA // 2, 2], [1, DA // 2]), ALU.mult))
                        q.link(nc.vector.tensor_tensor(qk[:, t, :], ra[:], rc[:], ALU.add))
                        q.link(nc.vector.tensor_scalar(mn[:, t, :], qk[:, t, :], 0.0, None, ALU.min))
                        dve.wait_ge(*proj(r, 2 * t + 2))
                        w.inc(nc.vector.tensor_tensor(va[:, t, :, 0:DA], ps[3][:, 0:D].rearrange("p (h e) -> p h e", e=DA),
                                                      bqkvg[:, 512:768].rearrange("p (h e) -> p h e", e=DA), ALU.add))
                        w.link(nc.vector.tensor_tensor(z[:, t, :], ps[3][:, D:2 * D], bqkvg[:, 768:1024], ALU.add))
                        w.link(nc.vector.tensor_scalar(z[:, t, :], z[:, t, :], -1.0, 80.0, ALU.mult, ALU.min))
                        if t:
                            finish(t - 1)
                    elif s_ == "sum":
                        if k is None or k >= 1:
                            dve.wait_ge(*masked(r - 1))
                        for c in range(NCH):
                            dve.wait_ge(*kv(r, c + 1))
                            d = ps[4 + c % 2][:, 0:2 * GRP * VA]
                            if c == 0:
                                nc.vector.tensor_copy(run[:, 0, :], d).then_inc(*summed.up)
                            else:
                                dve.wait_ge(*summed(r, c))
                                nc.vector.tensor_tensor(run[:, c, :], d, run[:, c - 1, :], ALU.add).then_inc(*summed.up)
                    elif s_ == "o":
                        s = Chain(dve, o_step, r)
                        if k is None or k >= 1:
                            dve.wait_ge(*b_flipped(r - 1, 2))
                        for t in range(TILES):
                            dve.wait_ge(*num(r, t + 1))
                            dve.wait_ge(*e_z(r, t + 1))
                            nv = ps[4 + t % 2][:, 0:HA * VA].rearrange("p (h e) -> p h e", e=VA)
                            s.link(nc.vector.tensor_scalar(den[:], nv[:, :, DA], 1e-6, None, ALU.add))
                            s.link(nc.vector.scalar_tensor_tensor(dd[:].rearrange("p (h e) -> p h e", e=DA),
                                                                  z[:, t, :].rearrange("p (h e) -> p h e", e=DA), 1.0,
                                                                  over(den[:], [1, HA], [0, DA]), ALU.add, ALU.mult))
                            s.link(nc.vector.reciprocal(dd[:], dd[:]))
                            s.link(nc.vector.tensor_tensor(o[:, t, :].rearrange("p (h e) -> p h e", e=DA), nv[:, :, 0:DA],
                                                           dd[:].rearrange("p (h e) -> p h e", e=DA), ALU.mult))
                        s.end()
                    elif s_ == "b_y":
                        dve.wait_ge(*hb_made(r))
                        if k is None or k >= 1:
                            dve.wait_ge(*res_made(r - 1))
                        for t in range(TILES):
                            dve.wait_ge(*ao(r, t // 2 * 2 + 2))
                            nc.vector.tensor_tensor(y[:, t, :], ps[6 + t // 2][:, (t % 2) * D:(t % 2 + 1) * D], hb[:, t, :],
                                                    ALU.add).then_inc(*y_made.up)
                    elif s_ == "b_hn":
                        s = Chain(dve, hn_step, r)
                        dve.wait_ge(*squared(r))
                        s.link(nc.vector.tensor_scalar(ssn[:], ssq[:], 1.0 / D, None, ALU.mult))
                        rsqrt(nc, s, rr[:], ssn[:], rrt[:])
                        if k is None:
                            dve.wait_ge(*sent(r - 2))
                        for t in range(TILES):
                            dve.wait_ge(*y_made(r, t + 1))
                            s.inc(nc.vector.scalar_tensor_tensor(hn[:, p, t, :], y[:, t, :], rr[:, t:t + 1], s2b[:], ALU.mult, ALU.mult))
                        s.end()
                    elif s_ == "b_route":
                        s = Chain(dve, route, r)
                        dve.wait_ge(*logit(r))
                        s.link(nc.vector.tensor_tensor(lg[:], ps[6][:, 0:TILES * NE].rearrange("p (t e) -> p t e", e=NE),
                                                       over(rb[:], [0, TILES], [1, NE]), ALU.add))
                        settle(dve)
                        for t in range(TILES):
                            s.inc(nc.vector.max(top[:, t, :], lg[:, t, :]))
                        s.sync()
                        settle(dve)
                        for t in range(TILES):
                            s.inc(nc.vector.max_index(topi[:, t, :], top[:, t, :], lg[:, t, :]))
                        s.sync()
                        s.link(nc.vector.tensor_copy(ef[:], topi[:, :, 0:TOPK]))
                        for t in range(TILES):
                            s.inc(nc.vector.tensor_tensor(oh[:, t], iota8[:], over(ef[:, t, :], [1, TOPK], [0, NE]), ALU.is_equal))
                        s.sync()
                        if k is None or k >= 1:
                            dve.wait_ge(*ranked(r - 1))
                        s.link(nc.vector.tensor_tensor(msk[:], oh[:, :, 0, :], oh[:, :, 1, :], ALU.add))
                        s.end()
                    elif s_ == "b_slots":
                        s = Chain(dve, slots, r)
                        if k is None or k >= 1:
                            dve.wait_ge(*g_exp(r - 1))
                        s.inc(nc.vector.tensor_tensor(gd[:], top[:, :, 1], top[:, :, 0], ALU.subtract))
                        dve.wait_ge(*ranked(r))
                        s.link(nc.vector.tensor_tensor(rank[:], ps[7][:, 0:TILES * NE].rearrange("p (t e) -> p t e", e=NE),
                                                       over(carry[:], [0, TILES], [1, NE]), ALU.add))
                        s.link(nc.vector.tensor_tensor(carry[:], ps[7][:, TILES * NE:(TILES + 1) * NE], carry[:], ALU.add))
                        for t in range(TILES):
                            s.inc(nc.vector.tensor_tensor(rk[:, t], oh[:, t], over(rank[:, t, :], [0, TOPK], [1, NE]), ALU.mult))
                        s.sync()
                        s.link(nc.vector.tensor_reduce(rsel[:], rk[:], AX, ALU.add))
                        s.inc(nc.vector.tensor_scalar(ok[:], rsel[:], float(CAP), None, ALU.is_lt))
                        s.link(nc.vector.scalar_tensor_tensor(slf[:], ef[:], float(CAP), rsel[:], ALU.mult, ALU.add))
                        s.inc(nc.vector.tensor_scalar(sld[:], ok[:], -1e6, 1e6, ALU.mult, ALU.add))
                        s.link(nc.vector.tensor_tensor(slot_of[:, bass.ds(r.at * TILES * TOPK, TILES * TOPK)],
                                                       slf[:].rearrange("p t c -> p (t c)"), ok[:].rearrange("p t c -> p (t c)"), ALU.mult))
                        s.inc(nc.vector.tensor_tensor(sli[:, p], slf[:], sld[:], ALU.add))
                        dve.wait_ge(*g_exp(r))
                        s.link(nc.vector.tensor_scalar(gd[:], ge[:], 1.0, None, ALU.add))
                        s.link(nc.vector.reciprocal(gg[:, :, 0], gd[:]))
                        g = Chain(dve, gates_sig, r)
                        g.link(nc.vector.tensor_tensor(gg[:, :, 1], gg[:, :, 0], ge[:], ALU.mult))
                        g.inc(nc.vector.tensor_tensor(gate_of[:, bass.ds(r.at * TILES * TOPK, TILES * TOPK)],
                                                      gg[:].rearrange("p t c -> p (t c)"), ok[:].rearrange("p t c -> p (t c)"), ALU.mult))
                        g.end()
                        s.end()

                overlapped(dve, NB, A_ORDER["dve"].split(), step)


def expert_stage(nc, a):
    with ExitStack() as ctx:
        sb = lambda name, shape, dt=F32: ctx.enter_context(nc.sbuf_tensor("e_" + name, shape, dt))
        sig = lambda name, per=1, by=1: Sig(ctx, nc, "e_" + name, per, by)
        two = lambda name, per=1: TwoSig(ctx, nc, "e_" + name, per)
        ps = [ctx.enter_context(nc.psum_tensor(f"e_ps{i}", [P, 512], F32)) for i in range(8)]
        ST = CAP // P
        SPANS = [(s, min(512, CAP - s)) for s in range(0, CAP, 512)]
        NS = len(SPANS)
        ident = sb("ident", [P, P])
        b1 = sb("b1", [P, NE, MC])
        b2 = sb("b2", [P, NE, D])
        b2e = sb("b2e", [P, D])
        b1e = sb("b1e", [P, MC])
        w1 = sb("w1", [P, 2, KC, HID])
        w2 = sb("w2", [P, 2, MC, D])
        xt = sb("xt", [P, 2, ST, D])
        xT = sb("xT", [P, KC, CAP])
        hid = sb("hid", [P, 2, MC, 512])
        yt = sb("yt", [P, 2, ST, D])

        const_in = sig("const_in", 3, 16)
        loaded = two("loaded", 3)
        bias_set = sig("bias_set", 2)
        flipped = sig("flipped", KC * NS)
        copied = sig("copied", KC * NS)
        up = sig("up", MC * NS)
        act_done = sig("act_done", MC * NS)
        down = sig("down", ST)
        y_set = sig("y_set", ST)
        stored = two("stored")

        with nc.Block() as block:

            @block.sync
            def _(sp):
                sp.dma_start(ident[:], a["ident"]).then_inc(*const_in.up)
                sp.dma_start(b1[:], a["b1"]).then_inc(*const_in.up)
                sp.dma_start(b2[:], a["b2"]).then_inc(*const_in.up)

                def store(r, p):
                    sp.wait_ge(*y_set(r))
                    sp.dma_start(a["expert_out"].rearrange("(e t p) n -> e p t n", e=NE, p=P)[r.at], yt[:, p]).then_inc(*stored.up(r))

                def body(r, p, k):
                    if k is None:
                        sp.wait_ge(*down(r - 2))
                    sp.dma_start(xt[:, p], a["dispatched"].rearrange("(e t p) n -> e p t n", e=NE, p=P)[r.at]).then_inc(*loaded.up(r))
                    sp.dma_start(w1[:, p], a["w1"][r.at].rearrange("(k p) n -> p k n", p=P)).then_inc(*loaded.up(r))
                    sp.dma_start(w2[:, p], a["w2"][r.at].rearrange("(m p) n -> p m n", p=P)).then_inc(*loaded.up(r))
                    if k != 0:
                        store(r - 1, 1 - p)

                rounds(sp, NE, body)
                last = Round(NE // 2 - 1, 1)
                store(last, 1)
                sp.wait_ge(*stored(last - 1))
                sp.wait_ge(*stored(last))

            @block.tensor
            def _(pe):
                pe.wait_ge(*const_in(0))

                def body(r, p, k):
                    pe.wait_ge(*loaded(r))
                    for s, (at, n) in enumerate(SPANS):
                        for c in range(KC):
                            i = s * KC + c
                            if i >= 2:
                                pe.wait_ge(*copied(r, i - 1))
                            elif k is None or k >= 1:
                                pe.wait_ge(*copied(r - 1, KC * NS - 1 + i))
                            for t in range(n // P):
                                ins = nc.tensor.transpose(ps[c][:, t * P:(t + 1) * P], xt[:, p, at // P + t, c * P:(c + 1) * P], ident[:])
                            ins.then_inc(*flipped.up)

                    def upward(s):
                        at, n = SPANS[s]
                        pe.wait_ge(*copied(r, (s + 1) * KC))
                        for m in range(MC):
                            i = s * MC + m
                            if i >= 3:
                                pe.wait_ge(*act_done(r, i - 2))
                            elif k is None or k >= 1:
                                pe.wait_ge(*act_done(r - 1))
                            for c in range(KC):
                                ins = nc.tensor.matmul(ps[2 + i % 3][:, 0:n], w1[:, p, c, m * P:(m + 1) * P], xT[:, c, at:at + n],
                                                       start=c == 0, stop=c == KC - 1)
                            ins.then_inc(*up.up)

                    def downward(s):
                        at, n = SPANS[s]
                        pe.wait_ge(*act_done(r, (s + 1) * MC))
                        for t in range(at // P, (at + n) // P):
                            if t >= 3:
                                pe.wait_ge(*y_set(r, t - 2))
                            elif k is None or k >= 1:
                                pe.wait_ge(*y_set(r - 1))
                            for m in range(MC):
                                ins = nc.tensor.matmul(ps[5 + t % 3][:, 0:D], hid[:, s % 2, m, t * P - at:(t + 1) * P - at], w2[:, p, m, :],
                                                       start=m == 0, stop=m == MC - 1)
                            ins.then_inc(*down.up)

                    upward(0)
                    for s in range(1, NS):
                        upward(s)
                        downward(s - 1)
                    downward(NS - 1)

                rounds(pe, NE, body)

            @block.scalar
            def _(act):
                def body(r, p, k):
                    act.wait_ge(*bias_set(r))
                    for s, (at, n) in enumerate(SPANS):
                        for m in range(MC):
                            i = s * MC + m
                            act.wait_ge(*up(r, i + 1))
                            if s >= 2:
                                act.wait_ge(*down(r, (SPANS[s - 2][0] + SPANS[s - 2][1]) // P))
                            elif k is None or k >= 1:
                                act.wait_ge(*down(r - 1))
                            nc.scalar.activation(hid[:, s % 2, m, 0:n], ps[2 + i % 3][:, 0:n], ACT.Gelu, bias=b1e[:, m:m + 1]).then_inc(*act_done.up)

                rounds(act, NE, body)

            @block.vector
            def _(dve):
                dve.wait_ge(*const_in(0))

                def body(r, p, k):
                    if k is None or k >= 1:
                        dve.wait_ge(*act_done(r - 1))
                        dve.wait_ge(*y_set(r - 1))
                    nc.vector.tensor_copy(b1e[:], b1[:, bass.ds(r.at, 1), :].rearrange("p a m -> p (a m)")).then_inc(*bias_set.up)
                    nc.vector.tensor_copy(b2e[:], b2[:, bass.ds(r.at, 1), :].rearrange("p a m -> p (a m)")).then_inc(*bias_set.up)
                    if k is None or k >= 1:
                        dve.wait_ge(*up(r - 1))
                    for s, (at, n) in enumerate(SPANS):
                        for c in range(KC):
                            dve.wait_ge(*flipped(r, s * KC + c + 1))
                            nc.vector.tensor_copy(xT[:, c, at:at + n], ps[c][:, 0:n]).then_inc(*copied.up)
                    dve.wait_ge(*bias_set(r))
                    if k is None:
                        dve.wait_ge(*stored(r - 2))
                    for t in range(ST):
                        dve.wait_ge(*down(r, t + 1))
                        nc.vector.tensor_tensor(yt[:, p, t, :], ps[5 + t % 3][:, 0:D], b2e[:], ALU.add).then_inc(*y_set.up)

                rounds(dve, NE, body)


class Fills:

    def __init__(self, order, first_bank):
        assert len(order) % 2 == 0
        self.order, self.first = order, first_bank
        self.index = {name: j for j, (name, _) in enumerate(order)}
        self.reader = dict(order)

    def count(self, reader):
        return sum(r == reader for _, r in self.order)

    def bank(self, name):
        return self.first + self.index[name] % 2

    def filled(self, name):
        return self.index[name] + 1

    def read(self, name):
        return sum(r == self.reader[name] for _, r in self.order[:self.index[name] + 1])

    def before(self, name):
        j = self.index[name] - 2
        return self.order[j][0], int(j < 0)


def front_back(eng, count, front, back):
    front(Round(0, 0), 0, None)
    nxt = lambda r, k: (lambda i: front(r, k, i))
    back(Round(0, 0), nxt(Round(0, 1), 1), 0)
    with eng.Fori(0, count // 2 - 1) as i:
        back(Round(i, 1), nxt(Round(i + 1, 0), None), None)
        back(Round(i + 1, 0), nxt(Round(i + 1, 1), None), None)
    back(Round(count // 2 - 1, 1), lambda i: None, count - 1)


ENGINES = ("pe", "act", "dve", "pool", "sp")


def turns(text):
    parts = [p.split(":") for p in text.split(";")]
    return {int(i): names.split() for i, names in parts}


TURNS = {
    True: ({
        "pe": turns("2: bm0; 3: bm1; 4: gt0 gt1; 5: gt2 gt3"),
        "dve": turns("4: bm0 bm1 gt0; 5: gt1; 6: gt2 gt3"),
    }, {
        "pe": turns("7: hT0 hT1; 9: score; 10: q0 k0; 12: v0; 15: q1 k1; 16: qT0 kT0; 18: sel; 19: q2; 20: v1 xg1; "
                     "21: xg0 k2; 22: aux; 23: mq0 mq1; 24: qT1 kT1; 25: v2; 26: q3 k3; 27: mqT mkT; 28: kT2 qT2; 29: ms; "
                     "30: v3; 31: mpT; 32: qT3 kT3; 33: am"),
        "act": turns("6: h; 7: hT0 hT1; 9: score; 11: q0 k0; 13: v0 ropeB0; 16: q1 k1; 17: qT0 kT0; 18: sel; 19: ropeB1; "
                     "20: q2 v1; 21: xg1 xg0; 22: k2 aux; 24: mq0 mq1 ropeB2; 25: qT1 mrope kT1; 26: v2; "
                     "27: q3 k3 mqT mkT; 29: kT2 qT2 ms ropeB3; 31: v3 mpT; 33: qT3 kT3; 34: am"),
        "dve": turns("3: x1; 4: lnA lnB; 5: lnC lnD; 10: top0; 12: top2 ropeA0 top3; 13: v0 ropeB0; 14: top1; "
                     "15: top4 top5; 16: top6; 17: top7 ropeA1; 18: topend sel; 19: ropeB1 G; 20: v1; 21: xg1 xg0; "
                     "22: aux; 23: ropeA2; 24: ropeB2; 25: mrope; 26: v2; 28: ropeA3 ropeB3; 29: ms; 31: v3 mpT; 34: am"),
        "pool": turns("2: x; 6: h; 12: ropeA0; 13: ropeB0; 17: ropeA1; 18: ropeB1; 23: ropeA2; 24: ropeB2; "
                     "29: ropeA3 ropeB3"),
        "sp": turns("3: x; 35: swap"),
    }),
    False: ({
        "pe": turns("1: gt1; 2: bm0; 3: bm1 gt2; 4: gt0; 5: gt3"),
        "dve": turns("2: gt1 bm0; 4: bm1 gt2; 5: gt0; 6: gt3"),
    }, {
        "pe": turns("6: bT0 bT1; 7: bw0 bw1; 8: bss; 11: bdot; 12: oT0 oT1; 13: bo0 bo1; 16: hT0 hT1; 17: score; "
                     "18: q0 k0; 19: v0; 20: q1; 21: k1; 22: sel; 23: qT0 kT0; 24: xg0; 25: q2 v1; 26: xg1 k2 aux; "
                     "27: mq0 mq1; 28: kT1; 29: qT1 q3 k3; 30: mqT mkT; 31: ms v2; 32: mpT v3 kT2; 34: qT2 am; 35: qT3 kT3"),
        "act": turns("3: bh; 6: bT0 bT1; 7: bw0 bw1; 9: bexp; 12: oT0 oT1; 14: h; 16: hT0 hT1; 17: score; 19: q0 k0; "
                     "20: v0; 22: ropeB0 q1 k1 sel; 24: qT0 kT0 ropeB1; 25: xg0; 26: q2 v1 xg1 k2 aux; "
                     "28: mq0 ropeB2 mq1; 29: kT1 qT1 mrope; 30: q3 k3 mqT mkT; 31: ms; 32: v2 mpT v3; 33: ropeB3 kT2; "
                     "35: qT2 am qT3 kT3"),
        "dve": turns("1: b_lnA b_lnB; 2: b_lnC; 3: b_lnD; 8: bss; 10: bpi; 11: bdot res; 12: oT0 oT1; 13: bo0 bo1; "
                     "14: lnA lnB lnC; 15: lnD; 17: top0; 18: top1; 19: top3 top2; 20: v0 ropeA0; 21: top4 top6 top7; "
                     "22: ropeB0 top5 topend sel; 23: ropeA1 G; 24: ropeB1; 25: xg0; 26: v1 xg1 aux; 27: ropeA2; "
                     "28: ropeB2; 29: mrope; 31: ropeA3; 32: ms v2 mpT; 33: ropeB3 v3; 35: am"),
        "pool": turns("3: bh; 14: h; 20: ropeA0; 21: ropeB0; 23: ropeA1; 24: ropeB1; 27: ropeA2 ropeB2; 31: ropeA3 ropeB3"),
        "sp": turns("3: x; 27: swap"),
    }),
}


W_UP = 64.0


def mixing_stage(nc, a, first):
    with ExitStack() as ctx:
        pre = "m1_" if first else "m2_"
        sb = lambda name, shape, dt=F32: ctx.enter_context(nc.sbuf_tensor(pre + name, shape, dt))
        sig = lambda name, per=1, by=1: Sig(ctx, nc, pre + name, per, by)
        two = lambda name, per=1: TwoSig(ctx, nc, pre + name, per)
        ps = [ctx.enter_context(nc.psum_tensor(f"{pre}ps{i}", [P, 512], F32)) for i in range(8)]
        ps16 = [b[:].bitcast(F16) for b in ps]
        HW = NH * HP
        SCALE = HP ** -0.5
        HALF = ROT // 2
        TW = ROT + NH
        ident = sb("ident", [P, P])
        ident16 = sb("ident16", [P, P], F16)
        causal = sb("causal", [P, P], BF16)
        causal2 = sb("causal2", [P, P], BF16)
        identb = sb("identb", [P, P], BF16)
        headrow = sb("headrow", [NH, PAIRS, P], BF16)
        slot1 = sb("slot1", [P, SLOTS])
        slotcol = sb("slotcol", [P, 1])
        onesf = sb("onesf", [P, P])
        cosd = sb("cosd", [P, TILES, ROT])
        sind = sb("sind", [P, TILES, ROT])
        dwqkv = sb("dwqkv", [P, 2, KC, 3 * HW], F16)
        mwqkv = sb("mwqkv", [P, 2, KC, 3 * HW], F16)
        dwo = sb("dwo", [P, 2, PAIRS, D], F16)
        mwo = sb("mwo", [P, 2, PAIRS, D], F16)
        mrw = sb("mrw", [P, 2, KC, NH], F16)
        mrw32 = sb("mrw32", [P, KC, NH])
        tb32 = sb("tb32", [P, TILES, ROT])
        x = sb("x", [P, 2, TILES, D])
        xo = sb("xo", [P, TILES, D])
        stats = sb("stats", [P, TILES, 6])
        mv = sb("mv", [P, TILES, 2])
        ve = sb("ve", [P, TILES])
        rs = sb("rs", [P, TILES])
        rt = sb("rt", [P, TILES])
        h = sb("h", [P, 2, TILES, D], F16)
        hT = sb("hT", [P, KC, 2, NT], F16)
        raw = sb("raw", [P, 2 * HW])
        ra = sb("ra", [P, 2 * NH, ROT])
        rc = sb("rc", [P, 2 * NH, ROT])
        qk2 = sb("qk2", [P, 2, 2 * NH, 2, HP], F16)
        v = sb("v", [P, 2, 2, TILES, HW], F16)
        qkT = sb("qkT", [P, 2, 2, NH, NT], F16)
        kS = sb("kS", [P, 2, NH, NT], F16)
        nmax = sb("nmax", [P, 4])
        rsum = sb("rsum", [P, TILES * NH])
        rinv = sb("rinv", [P, NH])
        prob = sb("prob", [P, 2, NT])
        pT = sb("pT", [P, 3, 2, NT], F16)
        av32 = sb("av32", [P, HW])
        av = sb("av", [P, 2, HW], F16)
        avT = sb("avT", [P, 2, PAIRS, P], F16)
        scT = sb("scT", [NH, NT])
        wk = sb("wk", [NH, NT])
        m8 = sb("m8", [NH, 8])
        selT = sb("selT", [NH, NT])
        sel16 = sb("sel16", [NH, 2, NT], BF16)
        sel = sb("sel", [P, TILES, NH])
        tb = sb("tb", [P, TILES, 2, TW], F16)
        G = sb("G", [P, TILES, NH * SLOTS], F16)
        GT = sb("GT", [P, PAIRS, NT], F16)
        xgT = sb("xgT", [P, KC, 2, NH * SLOTS], F16)
        aux = sb("aux", [P, PAIRS * TW])
        gsc = sb("gsc", [P, PAIRS])
        gex = sb("gex", [P, PAIRS])
        gr = sb("gr", [P, PAIRS])
        r4 = sb("r4", [P, 4, PAIRS, 2, HALF])
        big = sb("big", [P, 5 * 256])
        h32 = big[:, 0:TILES * D].rearrange("p (t n) -> p t n", n=D)
        mq = big[:, 0:PAIRS * 192].rearrange("p (m n) -> p m n", n=192)
        mp = big[:, PAIRS * 192:PAIRS * (192 + P)].rearrange("p (m n) -> p m n", n=P)
        mq2 = sb("mq2", [P, 2, PAIRS, 192], F16)
        PW = D + HB
        mqTb = sb("mqT", [P, TILES * PW])
        mqT = mqTb[0:HP, 0:1024].bitcast(F16).rearrange("p (j s n) -> p j s n", j=2, s=2)
        mmax = sb("mmax", [P, PAIRS])
        msum = sb("msum", [P, PAIRS])
        mpT = sb("mpT", [P, 2, PAIRS, P], F16)
        am = sb("am", [P, 2, PAIRS * SLOTS], F16)
        bm = sb("bm", [P, 2, PAIRS, D], F16)
        if first:
            idx = sb("idx", [P, TILES * TOPK], U32)
            gcur = sb("gcur", [P, TILES * TOPK])
            gy = sb("gy", [P, TILES, TOPK, D])
        else:
            bw = sb("bw", [P, 2, KC, D], F16)
            bwout = sb("bwout", [P, 2, KC, D], F16)
            btemp = sb("btemp", [P, HB])
            bbout = sb("bbout", [P, D])
            w = xgT[:].rearrange("p c s n -> p (c s n)").bitcast(F32).rearrange("p (t n) -> p t n", n=D)
            w2 = G[:].rearrange("p t n -> p (t n)").bitcast(F32).rearrange("p (t n) -> p t n", n=D)
            pw = mqTb[:].rearrange("p (t n) -> p t n", n=PW)
            x2 = sb("x2", [P, TILES, D])
            inv = sb("inv", [P, D])
            attn = inv
            bl = sb("bl", [P, TILES, HB])
            bmx = sb("bmx", [P, TILES])
            bsm = sb("bsm", [P, TILES])
            bden = sb("bden", [P, HB])
            dot = r4[:].rearrange("p j m s n -> p (j m s n)")[:, 0:PW]

        st = qkT[:].rearrange("p r j n t -> p (r j n t)").bitcast(F32)
        st2 = kS[:].rearrange("p r n t -> p (r n t)").bitcast(F32)
        chunked = [(st[:, 0:KC * 3 * HW], "dwqkv", dwqkv, 3 * HW), (st[:, 4096:4096 + KC * 3 * HW], "mwqkv", mwqkv, 3 * HW),
                   (st2[:, 0:PAIRS * D], "dwo", dwo, D), (st2[:, PAIRS * D:2 * PAIRS * D], "mwo", mwo, D),
                   (mrw32[:].rearrange("p k n -> p (k n)"), "mrw", mrw, NH)]
        consts = [(ident, "ident"), (ident16, "ident16"), (identb, "identb"), (causal, "causal"), (causal2, "causal_pair"),
                  (headrow, "headrow"), (slot1, "slot1"), (slotcol, "slotcol"), (cosd, "cosd"), (sind, "sind"), (tb32, "rope_rows")]
        if not first:
            consts += [(btemp, "btemp"), (bbout, "bbout")]
            chunked += [(st2[:, 2048:2048 + KC * D], "bw", bw, D), (st2[:, 2560:2560 + KC * D], "bwout", bwout, D)]

        NI = TILES * NH
        AV_LAG = 3
        SLOT_N = NI + AV_LAG + 1
        QORDER = [3, 2, 1, 0]
        item = lambda i: (QORDER[i // NH], i % NH)

        def due(i, k):
            late = [(TILES - 1, part, 1) for part in (1, 2) if i == part and not k == 0]
            return late + [(g, part, 0) for g in range(TILES) for part, after in enumerate((0, 2, 3))
                           if i == (g + 1) * NH + AV_LAG - 1 + after]

        own, ahead = TURNS[first]
        own = {e: dict(own.get(e, {})) for e in ENGINES}
        ahead = {e: dict(ahead.get(e, {})) for e in ENGINES}
        names = lambda *ps, n: {f"{p}{i}" for p in ps for i in range(n)}
        by_scalar = {"score", "ms", "mqT", "mkT"} | names("hT", "bT", "bw", "mq", n=2) | names("q", "k", "qT", "kT", n=TILES)
        in_order = lambda turns: [s for i in sorted(turns) for s in turns[i]]
        fills = in_order(ahead["pe"]) + in_order(own["pe"])
        fl = Fills([(s, "act" if s in by_scalar else "dve") for s in fills], 6)
        order = fl.order
        for e in ("act", "dve"):
            mine = [s for s in in_order(ahead[e]) + in_order(own[e]) if s in fl.index]
            assert mine == [s for s in fills if s in mine], (e, mine)
        for e in ENGINES:
            assert not own[e] or max(own[e]) < min([i for i in ahead[e] for s in ahead[e][i] if s in fl.index] + [SLOT_N]), e
            assert max(ahead[e]) < SLOT_N

        const_in = sig("const_in", len(consts) + len(chunked), 16)
        ones_set = sig("ones_set")
        split = sig("split", 2 * len(chunked) + 6)
        filled = sig("filled", len(order))
        read = {"act": sig("read_by_scalar", fl.count("act")), "dve": sig("read_by_vector", fl.count("dve"))}
        hi = sig("hi", TILES + 1 + 5 + (4 if not first else 0))
        HI = ([] if first else ["bw0", "bw1", "oT0", "oT1"]) + [f"v{t}" for t in range(TILES)] + ["sel", "xg0", "xg1", "mpT", "am"]
        x_in = two("x_in")
        x_made = sig("x_made", 2 * TILES) if first else None
        x_ready = lambda r: x_made(r) if first else read["dve"](r, fl.read("bo1"))
        out_made = sig("out_made", TILES)
        out_done = sig("out_done", 1, 16)
        ln = sig("ln", 2 * TILES + 1 + RSQRT_STEPS + TILES)
        h_hi = sig("h_hi")
        h_lo = sig("h_lo")
        pick = sig("pick", 16 + 3 + 1)
        rope_a = sig("rope_a", TILES)
        rope_b = sig("rope_b", TILES)
        rope = sig("rope", TILES)
        qk_hi = sig("qk_hi", TILES)
        qk_lo = sig("qk_lo", TILES)
        swapped = sig("swapped", 2, 16)
        g_set = sig("g_set", TILES)
        aux_hi = sig("aux_hi")
        aux_step = sig("aux_step", 2)
        gate_exp = sig("gate_exp")
        mrope = sig("mrope", 6)
        mq_hi = sig("mq_hi")
        mq_lo = sig("mq_lo")
        m_max = sig("m_max")
        m_exp = sig("m_exp", PAIRS - 1)
        bm_step = sig("bm_step", 3 + 6)
        s_ps = sig("s_ps", TILES * NH)
        s_max = sig("s_max", TILES * NH)
        s_exp = sig("s_exp", TILES * NH)
        p_flip = sig("p_flip", TILES * NH)
        p_hi = sig("p_hi", TILES * NH)
        p_lo = sig("p_lo", TILES * NH)
        av_ps = sig("av_ps", TILES * NH)
        av_set = sig("av_set", 2 * TILES)
        av_lo = sig("av_lo", TILES)
        av_hi = sig("av_hi", TILES)
        av_flip = sig("av_flip", TILES)
        avT_set = sig("avT_set", TILES)
        o_ps = sig("o_ps", TILES)
        if first:
            idx_set = sig("idx_set", 2)
            gathered = sig("gathered", TILES * TOPK, 16)
        else:
            b_ln = sig("b_ln", 2 * TILES + 1 + RSQRT_STEPS + TILES)
            bh_hi = sig("bh_hi")
            bh_lo = sig("bh_lo")
            xb_set = sig("xb_set")
            pi = sig("pi", 10)
            pi_exp = sig("pi_exp")
            res = sig("res", 7)

        with nc.Block() as block:

            def run_front(step, slots):
                def front(r, k, i):
                    for s in ([s for j in sorted(slots) for s in slots[j]] if i is None else slots.get(i, ())):
                        step(r, r.parity, k, s)
                return front

            @block.sync
            def _(sp):
                for to, name in consts:
                    sp.dma_start(to[:], a[name]).then_inc(*const_in.up)
                for to, name, _, n in chunked:
                    sp.dma_start(to.rearrange("p (k n) -> p k n", n=n), a[name].rearrange("(k p) n -> p k n", p=P)).then_inc(*const_in.up)
                sp.wait_ge(*split(0))

                def step(r, p, k, s):
                    if s == "x":
                        if first:
                            if k is None or k >= 1:
                                sp.wait_ge(*filled(r - 1, fl.filled("mpT")))
                            sp.dma_start(h32, a["resid"][r.at].rearrange("(t p) n -> p t n", p=P)).then_inc(*x_in.up(r))
                        else:
                            if k is None or k >= 1:
                                sp.wait_ge(*x_ready(r - 1))
                            sp.dma_start(x2[:], a["mid"][r.at].rearrange("(t p) n -> p t n", p=P)).then_inc(*x_in.up(r))
                    elif s == "swap":
                        sp.wait_ge(*read["act"](r, fl.read(f"kT{TILES - 1}")))
                        if k is None:
                            sp.wait_ge(*s_ps(r - 2))
                        sp.dma_start(kS[0:HP, p], qkT[HP:P, p, 1]).then_inc(*swapped.up)
                        sp.dma_start(kS[HP:P, p], qkT[0:HP, p, 1]).then_inc(*swapped.up)

                def back(r, side, k):
                    for i in range(SLOT_N):
                        side(i)
                        if i == 3 and not k == 0:
                            end(r - 1)

                def end(r):
                    sp.wait_ge(*out_made(r))
                    sp.dma_start(a["mid" if first else "out"][r.at].rearrange("(t p) n -> p t n", p=P), xo[:]).then_inc(*out_done.up)

                front_back(sp, NB, run_front(step, ahead["sp"]), back)
                end(Round(NB // 2 - 1, 1))
                sp.wait_ge(*out_done(NB - 1))

            @block.gpsimd
            def _(pool):
                nc.gpsimd.memset(onesf[:], 1.0).then_inc(*ones_set.up)
                pool.wait_ge(*const_in(0))

                def step(r, p, k, s):
                    if s == "x" and first:
                        if k is None or k >= 1:
                            pool.wait_ge(*x_made(r - 1))
                            pool.wait_ge(*gathered(r - 1))
                        cols = bass.ds(r.at * TILES * TOPK, TILES * TOPK)
                        nc.gpsimd.tensor_copy(idx[:], a["slot_of"][:, cols]).then_inc(*idx_set.up)
                        nc.gpsimd.tensor_copy(gcur[:], a["gate_of"][:, cols]).then_inc(*idx_set.up)
                        pool.wait_ge(*idx_set(r))
                        settle(pool)
                        for t in range(TILES):
                            for c in range(TOPK):
                                pool.indirect_dma_start(gy[:, t, c, :], None, a["expert_out"],
                                                        bass.IndirectOffsetOnAxis(ap=idx[:, t * TOPK + c:t * TOPK + c + 1], axis=0),
                                                        bounds_check=NE * CAP - 1, oob_is_err=False).then_inc(*gathered.up)
                    elif s in ("h", "bh"):
                        pool.wait_ge(*(h_hi if s == "h" else bh_hi)(r))
                        nc.gpsimd.tensor_tensor(h[:, 1], h32, h[:, 0], ALU.subtract).then_inc(*(h_lo if s == "h" else bh_lo).up)
                    if s == "bh":
                        nc.gpsimd.tensor_tensor(x2[:], x2[:], over(bbout[:], [0, TILES], [1, D]), ALU.add).then_inc(*xb_set.up)
                    elif s[:5] == "ropeA":
                        t = int(s[5:])
                        pool.wait_ge(*read["act"](r, fl.read(f"k{t}")))
                        if t:
                            pool.wait_ge(*rope(r, t))
                        elif k is None or k >= 1:
                            pool.wait_ge(*rope(r - 1))
                        x2d = raw[:].rearrange("p (h d) -> p h d", d=HP)[:, :, 0:ROT]
                        nc.gpsimd.tensor_tensor(rc[:].rearrange("p h (s d) -> p h s d", s=2), x2d.rearrange("p h (s d) -> p h s d", s=2)[:, :, ::-1, :],
                                                over(sind[:, t, :], [0, 2 * NH], [HALF, 2], [1, HALF]), ALU.mult).then_inc(*rope_b.up)
                    elif s[:5] == "ropeB":
                        t = int(s[5:])
                        pool.wait_ge(*qk_hi(r, t + 1))
                        nc.gpsimd.tensor_tensor(qk2[:, t % 2, :, 1, :], raw[:].rearrange("p (h d) -> p h d", d=HP), qk2[:, t % 2, :, 0, :],
                                                ALU.subtract).then_inc(*qk_lo.up)

                def end(r, g, part, k):
                    if part == 0:
                        pool.wait_ge(*av_hi(r, g + 1))
                        nc.gpsimd.tensor_tensor(av[:, 1], av32[:], av[:, 0], ALU.subtract).then_inc(*av_lo.up)

                def back(r, side, k):
                    for i in range(SLOT_N):
                        for g, part, ago in due(i, k):
                            end(r - ago, g, part, k)
                        side(i)

                front_back(pool, NB, run_front(step, ahead["pool"]), back)
                end(Round(NB // 2 - 1, 1), TILES - 1, 1, None)
                end(Round(NB // 2 - 1, 1), TILES - 1, 2, None)

            @block.tensor
            def _(pe):
                pe.wait_ge(*const_in(0))
                pe.wait_ge(*ones_set(0))
                pe.wait_ge(*split(0))

                def begin(r, k, name, after=None):
                    was, ago = fl.before(name)
                    eng = fl.reader[was]
                    if after and fl.reader[after] == eng:
                        if ago or fl.index[after] > fl.index[was]:
                            was, ago = after, 0
                    elif after:
                        pe.wait_ge(*read[fl.reader[after]](r, fl.read(after)))
                    if not (ago and k == 0):
                        pe.wait_ge(*read[eng](r - ago, fl.read(was)))
                    return fl.bank(name)

                def products(to, pairs):
                    for n, (l, m) in enumerate(pairs):
                        ins = nc.tensor.matmul(to, l, m, start=n == 0, stop=n == len(pairs) - 1)
                    return ins

                parts = lambda l, m: [(l(i), m(j)) for i, j in ((0, 0), (0, 1), (1, 0))]

                def step(r, p, k, s):
                    if s not in fl.index:
                        return
                    if s in ("hT0", "hT1", "bT0", "bT1"):
                        c = int(s[2])
                        if c == 0:
                            pe.wait_ge(*(h_lo if s[0] == "h" else bh_lo)(r))
                        b = begin(r, k, s)
                        for j in range(2):
                            for t in range(TILES):
                                ins = nc.tensor.transpose(ps16[b][:, (j * TILES + t) * P:(j * TILES + t + 1) * P], h[:, j, t, c * P:(c + 1) * P], ident16[:])
                    elif s == "score":
                        b = begin(r, k, s, after="hT1")
                        ins = products(ps[b][0:NH, :], [q for c in range(KC) for q in parts(lambda i: mrw[:, i, c, :], lambda j: hT[:, c, j, :])])
                    elif s[0] in "qkv" and len(s) == 2:
                        t, j = int(s[1]), "qkv".index(s[0])
                        b = begin(r, k, s)
                        ins = products(ps[b][:], [q for c in range(KC) for q in parts(
                            lambda i: hT[:, c, i, t * P:(t + 1) * P], lambda i: dwqkv[:, i, c, j * HW:(j + 1) * HW])])
                    elif s[0:2] in ("qT", "kT"):
                        t, j = int(s[2]), "qk".index(s[0])
                        pe.wait_ge(*qk_lo(r, t + 1))
                        b = begin(r, k, s)
                        for n in range(NH):
                            ins = nc.tensor.transpose(ps16[b][:, n * P:(n + 1) * P], qk2[:, t % 2, j * NH + n].rearrange("p s d -> p (s d)"), ident16[:])
                    elif s == "sel":
                        pe.wait_ge(*pick(r))
                        b = begin(r, k, s)
                        settle(pe)
                        for j, src in enumerate((selT, scT)):
                            for t in range(TILES):
                                ins = nc.tensor.transpose(ps[b][:, (j * TILES + t) * NH:(j * TILES + t + 1) * NH],
                                                          src[:, t * P:(t + 1) * P], ident[0:NH, 0:NH])
                    elif s[:2] == "xg":
                        c = int(s[2])
                        pe.wait_ge(*g_set(r))
                        b = begin(r, k, s)
                        ins = products(ps[b][:], [(h[:, i, t, c * P:(c + 1) * P], G[:, t, :]) for t in range(TILES) for i in range(2)])
                    elif s == "aux":
                        b = begin(r, k, s, after="sel")
                        for m in range(PAIRS):
                            ins = products(ps[b][:, m * 2 * TW:(m + 1) * 2 * TW],
                                           [(G[:, t, m * P:(m + 1) * P], tb[:, t].rearrange("p s n -> p (s n)")) for t in range(TILES)])
                    elif s[:2] == "mq" and s != "mqT":
                        g = int(s[2])
                        b = begin(r, k, s, after="xg1")
                        for n in range(4 * g, 4 * g + 4):
                            q, m = n % 2 * SLOTS, n // 2 % 2
                            ins = products(ps[b][q:q + SLOTS, m * 192:(m + 1) * 192], [z for c in range(KC) for z in parts(
                                lambda i: xgT[:, c, i, n * SLOTS:(n + 1) * SLOTS], lambda i: mwqkv[:, i, c, n * 192:(n + 1) * 192])])
                    elif s in ("mqT", "mkT"):
                        j = "qk".index(s[1])
                        pe.wait_ge(*mq_lo(r))
                        b = begin(r, k, s)
                        settle(pe)
                        for i in range(2):
                            for m in range(PAIRS):
                                ins = nc.tensor.transpose(ps16[b][0:HP, (i * PAIRS + m) * P:(i * PAIRS + m + 1) * P], mq2[:, i, m, j * HP:(j + 1) * HP], ident16[:])
                    elif s == "ms":
                        b = begin(r, k, s, after="mkT")
                        for m in range(PAIRS):
                            cols = slice(m * P, (m + 1) * P)
                            ins = products(ps[b][:, cols], parts(lambda i: mqT[:, 0, i, cols], lambda i: mqT[:, 1, i, cols]) + [(identb[:], causal2[:])])
                    elif s == "mpT":
                        b = begin(r, k, s, after="ms")
                        for m in range(PAIRS):
                            ins = nc.tensor.transpose(ps[b][:, m * P:(m + 1) * P], mp[:, m, :], ident[:])
                    elif s == "am":
                        b = begin(r, k, s, after="mpT")
                        for n in range(NH):
                            q, m = n % 2 * SLOTS, n // 2
                            ins = products(ps[b][q:q + HP, m * SLOTS:(m + 1) * SLOTS],
                                           parts(lambda i: mq2[:, i, m, 2 * HP:3 * HP], lambda i: mpT[:, i, m, q:q + SLOTS]))
                    elif s[:2] == "bm":
                        g = int(s[2])
                        b = begin(r, k, s, after="am")
                        settle(pe)
                        for n in range(4 * g, 4 * g + 4):
                            q, m = n % 2 * SLOTS, n // 2
                            ins = products(ps[b][q:q + SLOTS, m % 2 * D:(m % 2 + 1) * D],
                                           parts(lambda i: am[q:q + HP, i, m * SLOTS:(m + 1) * SLOTS], lambda i: mwo[q:q + HP, i, m, :]))
                    elif s[:2] == "gt":
                        m = int(s[2])
                        b = begin(r, k, s)
                        ins = nc.tensor.matmul(ps[b][:], headrow[:, m, :], sel16[:, p, :], start=True, stop=True)
                    elif s in ("bw0", "bw1"):
                        g = int(s[2])
                        b = begin(r, k, s, after="bT1")
                        for t in (2 * g, 2 * g + 1):
                            ins = products(ps[b][:, t % 2 * D:(t % 2 + 1) * D], [z for c in range(KC) for z in parts(
                                lambda i: hT[:, c, i, t * P:(t + 1) * P], lambda i: bw[:, i, c, :])])
                    elif s == "bss":
                        b = begin(r, k, s, after="bw1")
                        ins = products(ps[b][:, 0:D], [(onesf[:], w2[:, t, :]) for t in range(TILES)])
                    elif s == "bdot":
                        pe.wait_ge(*pi(r))
                        b = begin(r, k, s)
                        ins = products(ps[b][:, 0:PW], [(onesf[:], pw[:, t, :]) for t in range(TILES)])
                    elif s in ("oT0", "oT1"):
                        c = int(s[2])
                        pe.wait_ge(*res(r))
                        b = begin(r, k, s)
                        for t in range(TILES):
                            ins = nc.tensor.transpose(ps[b][:, t * P:(t + 1) * P], w[:, t, c * P:(c + 1) * P], ident[:])
                    elif s in ("bo0", "bo1"):
                        g = int(s[2])
                        b = begin(r, k, s, after="oT1")
                        for t in (2 * g, 2 * g + 1):
                            ins = products(ps[b][:, t % 2 * D:(t % 2 + 1) * D], [z for c in range(KC) for z in parts(
                                lambda i: hT[:, c, i, t * P:(t + 1) * P], lambda i: bwout[:, i, c, :])])
                    ins.then_inc(*filled.up)

                def end(r, g, part, k):
                    if part == 1:
                        pe.wait_ge(*av_lo(r, g + 1))
                        if g:
                            pe.wait_ge(*out_made(r, g))
                        elif k is None or k >= 1:
                            pe.wait_ge(*out_made(r - 1))
                        for s_ in range(2):
                            for m in range(PAIRS):
                                ins = nc.tensor.transpose(ps16[5][:, (s_ * PAIRS + m) * P:(s_ * PAIRS + m + 1) * P], av[:, s_, m * P:(m + 1) * P], ident16[:])
                        ins.then_inc(*av_flip.up)
                    elif part == 2:
                        qt = QORDER[g]
                        pe.wait_ge(*read["dve"](r, fl.read("gt3")))
                        pe.wait_ge(*avT_set(r, g + 1))
                        ins = products(ps[5][:, 0:D], [(GT[:, m, qt * P:(qt + 1) * P], bm[:, i_, m, :]) for m in range(PAIRS) for i_ in range(2)]
                                       + [z for m in range(PAIRS) for z in parts(lambda i_: avT[:, i_, m, :], lambda i_: dwo[:, i_, m, :])])
                        ins.then_inc(*o_ps.up)

                def back(r, side, k):
                    p = r.parity
                    pe.wait_ge(*swapped(r))
                    pe.wait_ge(*read["act"](r, fl.read(f"kT{TILES - 1}")))
                    pe.wait_ge(*read["dve"](r, fl.read(f"v{TILES - 1}")))
                    for i in range(SLOT_N):
                        if i < NI:
                            qt, n = item(i)
                            nk = (qt + 1) * P
                            if i >= 2:
                                pe.wait_ge(*s_exp(r, i - 1))
                            elif k is None or k >= 1:
                                pe.wait_ge(*s_exp(r - 1))
                            to = ps[i % 2]
                            qs = qkT[:, p, 0, n, qt * P:(qt + 1) * P]
                            nc.tensor.matmul(to[:, 0:nk], qs, qkT[:, p, 1, n, 0:nk], start=True, stop=False)
                            nc.tensor.matmul(to[:, 0:nk], qs, kS[:, p, n, 0:nk], start=False, stop=False)
                            nc.tensor.matmul(to[:, nk - P:nk], identb[:], causal[:], start=False, stop=True).then_inc(*s_ps.up)
                        if 1 <= i <= NI:
                            j = i - 1
                            qt, n = item(j)
                            pe.wait_ge(*s_exp(r, j + 1))
                            if j >= 2:
                                pe.wait_ge(*p_lo(r, j - 1))
                            elif k is None or k >= 1:
                                pe.wait_ge(*p_lo(r - 1))
                            for c in range(qt + 1):
                                ins = nc.tensor.transpose(ps[2 + j % 2][:, c * P:(c + 1) * P], prob[:, j % 2, c * P:(c + 1) * P], ident[:])
                            ins.then_inc(*p_flip.up)
                        if AV_LAG <= i < NI + AV_LAG:
                            j = i - AV_LAG
                            qt, n = item(j)
                            pe.wait_ge(*p_lo(r, j + 1))
                            if n == 0 and j:
                                pe.wait_ge(*av_set(r, 2 * (j // NH)))
                            elif n == 0 and (k is None or k >= 1):
                                pe.wait_ge(*av_set(r - 1, 2 * TILES))
                            ins = products(ps[4][:, n * HP:(n + 1) * HP], [z for c in range(qt + 1) for z in parts(
                                lambda i_: pT[:, j % 3, i_, c * P:(c + 1) * P], lambda i_: v[:, p, i_, c, n * HP:(n + 1) * HP])])
                            ins.then_inc(*av_ps.up)
                        for g, part, ago in due(i, k):
                            end(r - ago, g, part, k)
                        for s in own["pe"].get(i, ()):
                            step(r, p, k, s)
                        side(i)

                front_back(pe, NB, run_front(step, ahead["pe"]), back)
                end(Round(NB // 2 - 1, 1), TILES - 1, 1, None)
                end(Round(NB // 2 - 1, 1), TILES - 1, 2, None)

            @block.scalar
            def _(act):
                def copy(dst, src, up, scale=1.0):
                    nc.scalar.activation(dst, src, ACT.Copy, scale=scale).then_inc(*up.up)

                def step(r, p, k, s):
                    if s in fl.index and s in HI + ["hT0", "hT1", "bT0", "bT1", "score", "mq0", "mq1", "mqT", "mkT", "ms"] or s in fl.index and s[0] in "qk":
                        act.wait_ge(*filled(r, fl.filled(s)))
                        b = fl.bank(s)
                    last = read["act"]
                    if s in ("h", "bh"):
                        act.wait_ge(*(ln if s == "h" else b_ln)(r))
                        if s == "h" and not first:
                            act.wait_ge(*filled(r, fl.filled("bT1")))
                        elif k is None or k >= 1:
                            act.wait_ge(*filled(r - 1, fl.filled("xg1")))
                        copy(h[:, 0], h32, h_hi if s == "h" else bh_hi)
                    elif s in ("hT0", "hT1", "bT0", "bT1"):
                        copy(hT[:, int(s[2])], ps16[b].rearrange("p (s n) -> p s n", s=2), last)
                    elif s == "score":
                        if k is None or k >= 1:
                            act.wait_ge(*pick(r - 1))
                        copy(scT[:], ps[b][0:NH, :], last, 1 / W_UP)
                    elif s[0] in "qk" and len(s) == 2:
                        t, j = int(s[1]), "qk".index(s[0])
                        if t:
                            act.wait_ge(*qk_lo(r, t))
                        elif k is None or k >= 1:
                            act.wait_ge(*qk_lo(r - 1))
                        copy(raw[:, j * HW:(j + 1) * HW], ps[b][:], last, 1 / W_UP)
                    elif s[0] == "v":
                        if k is None:
                            act.wait_ge(*av_ps(r - 2))
                        copy(v[:, p, 0, int(s[1]), :], ps[b][:], hi, 1 / W_UP)
                    elif s[:5] == "ropeB":
                        t = int(s[5:])
                        act.wait_ge(*rope(r, t + 1))
                        if t >= 2:
                            act.wait_ge(*filled(r, fl.filled(f"kT{t - 2}")))
                        elif k is None or k >= 1:
                            act.wait_ge(*filled(r - 1, fl.filled(f"kT{TILES - 2 + t}")))
                        copy(qk2[:, t % 2, :, 0, :], raw[:].rearrange("p (h d) -> p h d", d=HP), qk_hi)
                    elif s[0:2] in ("qT", "kT"):
                        t, j = int(s[2]), "qk".index(s[0])
                        if k is None:
                            act.wait_ge(*s_ps(r - 2))
                        copy(qkT[:, p, j, :, t * P:(t + 1) * P], ps16[b].rearrange("p (n q) -> p n q", n=NH), last)
                    elif s == "sel":
                        n4 = TILES * NH
                        if k is None or k >= 1:
                            act.wait_ge(*g_set(r - 1))
                        copy(sel[:], ps[b][:, 0:n4].rearrange("p (t n) -> p t n", n=NH), hi)
                        copy(tb[:, :, 0, ROT:], ps[b][:, n4:2 * n4].rearrange("p (t n) -> p t n", n=NH), hi)
                    elif s in ("xg0", "xg1"):
                        copy(xgT[:, int(s[2]), 0, :], ps[b][:], hi)
                    elif s == "aux":
                        act.wait_ge(*aux_step(r))
                        if k is None or k >= 1:
                            act.wait_ge(*bm_step(r - 1, 1))
                        nc.scalar.activation(gex[:], gsc[:], ACT.Exp).then_inc(*gate_exp.up)
                    elif s in ("mq0", "mq1"):
                        g = int(s[2])
                        copy(mq[:, 2 * g:2 * g + 2, :], ps[b][:, 0:2 * 192].rearrange("p (m n) -> p m n", m=2), last, 1 / W_UP)
                    elif s == "mrope":
                        act.wait_ge(*mrope(r))
                        if k is None or k >= 1:
                            act.wait_ge(*filled(r - 1, fl.filled("am")))
                        copy(mq2[:, 0], mq, mq_hi)
                    elif s in ("mqT", "mkT"):
                        copy(mqT[:, "qk".index(s[1])], ps16[b][0:HP, :].rearrange("p (s n) -> p s n", s=2), last)
                    elif s == "ms":
                        act.wait_ge(*m_max(r))
                        if k is None or k >= 1:
                            act.wait_ge(*bm_step(r - 1, 2))
                        for m in range(PAIRS):
                            nc.scalar.activation(mp[:, m, :], ps[b][:, m * P:(m + 1) * P], ACT.Exp, bias=mmax[:, m:m + 1],
                                                 accum_out=msum[:, m:m + 1]).then_inc(*(last if m == PAIRS - 1 else m_exp).up)
                    elif s == "mpT":
                        copy(mpT[:, 0], ps[b][:].rearrange("p (m n) -> p m n", m=PAIRS), hi)
                    elif s == "am":
                        copy(am[:, 0], ps[b][:, 0:PAIRS * SLOTS], hi)
                    elif s in ("bw0", "bw1"):
                        g = int(s[2])
                        src = ps[b][:].rearrange("p (t n) -> p t n", n=D)
                        copy(w[:, 2 * g:2 * g + 2, :], src, hi, 1 / W_UP)
                        nc.scalar.activation(w2[:, 2 * g:2 * g + 2, :], src, ACT.Square, scale=1 / W_UP).then_inc(*last.up)
                    elif s == "bexp":
                        act.wait_ge(*pi(r, 6))
                        nc.scalar.activation(bl[:], bl[:], ACT.Exp).then_inc(*pi_exp.up)
                    elif s in ("oT0", "oT1"):
                        copy(hT[:, int(s[2]), 0], ps[b][:], hi)

                def end(r, g, part, k):
                    if part == 0:
                        act.wait_ge(*av_set(r, 2 * g + 2))
                        if g:
                            act.wait_ge(*av_flip(r, g))
                        elif k is None or k >= 1:
                            act.wait_ge(*av_flip(r - 1))
                        copy(av[:, 0], av32[:], av_hi)
                    elif part == 1:
                        act.wait_ge(*av_flip(r, g + 1))
                        if g:
                            act.wait_ge(*o_ps(r, g))
                        elif k is None or k >= 1:
                            act.wait_ge(*o_ps(r - 1))
                        copy(avT[:], ps16[5].rearrange("p (s m n) -> p s m n", s=2, m=PAIRS), avT_set)

                def back(r, side, k):
                    for i in range(SLOT_N):
                        if i < NI:
                            qt, n = item(i)
                            nk = (qt + 1) * P
                            act.wait_ge(*s_max(r, i + 1))
                            if i >= 2:
                                act.wait_ge(*p_flip(r, i - 1))
                            elif k is None or k >= 1:
                                act.wait_ge(*p_flip(r - 1))
                            if i == 0 and (k is None or k >= 1):
                                act.wait_ge(*av_set(r - 1))
                            nc.scalar.activation(prob[:, i % 2, 0:nk], ps[i % 2][:, 0:nk], ACT.Exp, bias=nmax[:, i % 4:i % 4 + 1],
                                                 accum_out=rsum[:, qt * NH + n:qt * NH + n + 1]).then_inc(*s_exp.up)
                        if 1 <= i <= NI:
                            j = i - 1
                            nk = (item(j)[0] + 1) * P
                            act.wait_ge(*p_flip(r, j + 1))
                            if j >= 3:
                                act.wait_ge(*av_ps(r, j - 2))
                            elif k is None or k >= 1:
                                act.wait_ge(*av_ps(r - 1))
                            copy(pT[:, j % 3, 0, 0:nk], ps[2 + j % 2][:, 0:nk], p_hi)
                        for g, part, ago in due(i, k):
                            end(r - ago, g, part, k)
                        for s in own["act"].get(i, ()):
                            step(r, r.parity, k, s)
                        side(i)

                front_back(act, NB, run_front(step, ahead["act"]), back)
                end(Round(NB // 2 - 1, 1), TILES - 1, 1, None)
                end(Round(NB // 2 - 1, 1), TILES - 1, 2, None)

            @block.vector
            def _(dve):
                V = nc.vector
                dve.wait_ge(*const_in(0))
                dve.wait_ge(*ones_set(0))
                s0 = Chain(dve, split, 0)
                for src, name, to, n in chunked:
                    src = src.rearrange("p (k n) -> p k n", n=n)
                    if name == "dwqkv":
                        s0.link(V.tensor_scalar(src[:, :, 0:HW], src[:, :, 0:HW], SCALE, None, ALU.mult))
                    if name == "mwqkv":
                        for c in range(KC):
                            qs = src[:, c, :].rearrange("p (h n) -> p h n", n=3 * HP)[:, :, 0:HP]
                            s0.inc(V.tensor_scalar(qs, qs, SCALE, None, ALU.mult))
                        s0.sync()
                    s0.link(V.tensor_scalar(to[:, 0], src, W_UP, None, ALU.mult))
                    s0.inc(V.scalar_tensor_tensor(to[:, 1], src, W_UP, to[:, 0], ALU.mult, ALU.subtract))
                s0.link(V.tensor_copy(tb[:, :, 0, 0:ROT], tb32[:]))
                s0.inc(V.tensor_tensor(tb[:, :, 1, 0:ROT], tb32[:], tb[:, :, 0, 0:ROT], ALU.subtract))
                s0.inc(V.memset(m8[:], 0.0))
                s0.end()
                dve.wait_ge(*split(0))

                def layernorm(part, up, r, src):
                    if part == "A":
                        c = open_["ln"] = Chain(dve, up, r)
                        for t in range(TILES):
                            c.inc(V.bn_stats(stats[:, t, :], src[:, t, :]))
                        c.sync()
                        settle(dve)
                        for t in range(TILES):
                            c.inc(V.bn_aggr(mv[:, t, :], stats[:, t, :]))
                        c.sync()
                        c.link(V.tensor_scalar(ve[:], mv[:, :, 1], LN_EPS, None, ALU.add))
                        return
                    c = open_["ln"]
                    if part in "BC":
                        rsqrt(nc, c, rs[:], ve[:], rt[:], "BC".index(part))
                    else:
                        for t in range(TILES):
                            c.inc(V.tensor_scalar(h32[:, t, :], src[:, t, :], mv[:, t, 0:1], rs[:, t:t + 1], ALU.subtract, ALU.mult))
                        c.end()

                heads = lambda z: z.rearrange("p t (h d) -> p t h d", d=DB)
                last = read["dve"]
                open_ = {}

                def low(r, s, to, src, high, n_hi, op_scale=None):
                    dve.wait_ge(*hi(r, n_hi))
                    if op_scale is None:
                        V.tensor_tensor(to, src, high, ALU.subtract).then_inc(*last.up)
                    else:
                        V.scalar_tensor_tensor(to, src, op_scale, high, ALU.mult, ALU.subtract).then_inc(*last.up)

                HN, count = {}, 0
                for s_ in in_order(ahead["act"]):
                    if s_ in HI:
                        count += 2 if s_ == "sel" else 1
                        HN[s_] = count
                assert count == hi.per, (count, hi.per)

                def step(r, p, k, s):
                    if fl.reader.get(s) == "dve" or s == "ms":
                        dve.wait_ge(*filled(r, fl.filled(s)))
                        b = fl.bank(s)
                    if s == "x1":
                        c_ = Chain(dve, x_made, r)
                        if k is None:
                            dve.wait_ge(*out_made(r - 2))
                        dve.wait_ge(*x_in(r))
                        dve.wait_ge(*gathered(r))
                        for c in range(TOPK):
                            for t in range(TILES):
                                c_.inc(V.scalar_tensor_tensor(x[:, p, t, :], gy[:, t, c, :], gcur[:, t * TOPK + c:t * TOPK + c + 1],
                                                              x[:, p, t, :] if c else h32[:, t, :], ALU.mult, ALU.add))
                            c_.sync()
                        c_.end()
                    elif s[:4] == "b_ln":
                        if s[4] == "A":
                            dve.wait_ge(*x_in(r))
                        layernorm(s[4], b_ln, r, x2)
                    elif s[:2] == "ln":
                        if s[2] == "A":
                            dve.wait_ge(*x_ready(r))
                        if s[2] == "D" and not first:
                            dve.wait_ge(*bh_lo(r))
                        layernorm(s[2], ln, r, x[:, p])
                    elif s[:3] == "top" and s != "topend":
                        i = int(s[3])
                        if i == 0:
                            open_["pick"] = Chain(dve, pick, r)
                            dve.wait_ge(*read["act"](r, fl.read("score")))
                        c_ = open_["pick"]
                        src = scT[:] if i == 0 else wk[:]
                        settle(dve)
                        c_.link(V.max(m8[:], src))
                        settle(dve)
                        c_.link(V.match_replace(wk[:], m8[:], src, NEG))
                    elif s == "topend":
                        c_ = open_["pick"]
                        if k is None or k >= 1:
                            dve.wait_ge(*filled(r - 1, fl.filled("sel")))
                        c_.link(V.tensor_tensor(wk[:], wk[:], scT[:], ALU.not_equal))
                        c_.link(V.tensor_tensor_scan(selT[:], over(onesf[0:NH, 0:1], [0, NT]), wk[:], 0.0, ALU.mult, ALU.add))
                        c_.link(V.tensor_tensor(selT[:], wk[:], selT[:], ALU.mult))
                        c_.inc(V.tensor_copy(sel16[:, p, :], selT[:]))
                        c_.end()
                    elif s[0] == "v" and len(s) == 2:
                        t = int(s[1])
                        low(r, s, v[:, p, 1, t, :], ps[b][:], v[:, p, 0, t, :], HN[s], 1 / W_UP)
                    elif s[:4] == "rope":
                        t = int(s[5:])
                        x2d = raw[:].rearrange("p (h d) -> p h d", d=HP)[:, :, 0:ROT]
                        if s[4] == "A":
                            dve.wait_ge(*read["act"](r, fl.read(f"k{t}")))
                            V.tensor_tensor(ra[:], x2d, over(cosd[:, t, :], [0, 2 * NH], [1, ROT]), ALU.mult).then_inc(*rope_a.up)
                        else:
                            dve.wait_ge(*rope_a(r, t + 1))
                            dve.wait_ge(*rope_b(r, t + 1))
                            V.tensor_tensor(x2d, ra[:], rc[:], ALU.add).then_inc(*rope.up)
                    elif s == "sel":
                        low(r, s, tb[:, :, 1, ROT:], ps[b][:, TILES * NH:2 * TILES * NH].rearrange("p (t n) -> p t n", n=NH), tb[:, :, 0, ROT:], HN[s])
                    elif s == "G":
                        for t in range(TILES):
                            V.tensor_tensor(G[:, t, :].rearrange("p (n k) -> p n k", k=SLOTS), over(slot1[:], [0, NH], [1, SLOTS]),
                                            over(sel[:, t, :], [1, NH], [0, SLOTS]), ALU.is_equal).then_inc(*g_set.up)
                    elif s in ("xg0", "xg1"):
                        c = int(s[2])
                        low(r, s, xgT[:, c, 1, :], ps[b][:], xgT[:, c, 0, :], HN[s])
                    elif s == "aux":
                        sums = ps[b][:, 0:PAIRS * 2 * TW].rearrange("p (m s n) -> p m s n", m=PAIRS, s=2)
                        V.tensor_copy(aux[:].rearrange("p (m n) -> p m n", m=PAIRS), sums[:, :, 0, :]).then_inc(*aux_hi.up)
                        dve.wait_ge(*aux_hi(r))
                        V.tensor_tensor(aux[:].rearrange("p (m n) -> p m n", m=PAIRS), aux[:].rearrange("p (m n) -> p m n", m=PAIRS), sums[:, :, 1, :],
                                        ALU.add).then_inc(*last.up)
                        dve.wait_ge(*last(r, fl.read("aux")))
                        for q in range(2):
                            V.tensor_scalar(gsc[q * SLOTS:(q + 1) * SLOTS, :], over(aux[q * SLOTS:(q + 1) * SLOTS, ROT + q:ROT + q + 1], [TW + 2, PAIRS]),
                                            -1.0, 80.0, ALU.mult, ALU.min).then_inc(*aux_step.up)
                    elif s == "mrope":
                        c_ = Chain(dve, mrope, r)
                        dve.wait_ge(*read["act"](r, fl.read("mq1")))
                        qk_ = mq[:, :, 0:2 * HP].rearrange("p m (j d) -> p m j d", j=2)
                        x1, x2_ = qk_[:, :, :, 0:HALF], qk_[:, :, :, HALF:ROT]
                        cc, ss = (over(aux[:, o:o + 1], [TW, PAIRS], [0, 2], [1, HALF]) for o in (0, HALF))
                        c_.inc(V.tensor_tensor(r4[:, 0], x1, cc, ALU.mult))
                        c_.inc(V.tensor_tensor(r4[:, 1], x2_, ss, ALU.mult))
                        c_.inc(V.tensor_tensor(r4[:, 2], x1, ss, ALU.mult))
                        c_.link(V.tensor_tensor(r4[:, 3], x2_, cc, ALU.mult))
                        c_.inc(V.tensor_tensor(x1, r4[:, 0], r4[:, 1], ALU.subtract))
                        c_.inc(V.tensor_tensor(x2_, r4[:, 2], r4[:, 3], ALU.add))
                        c_.end()
                        dve.wait_ge(*mq_hi(r))
                        V.tensor_tensor(mq2[:, 1], mq, mq2[:, 0], ALU.subtract).then_inc(*mq_lo.up)
                    elif s == "ms":
                        V.tensor_reduce(mmax[:], ps[b][:].rearrange("p (m n) -> p m n", m=PAIRS), AX, ALU.max, negate=True).then_inc(*m_max.up)
                    elif s == "mpT":
                        low(r, s, mpT[:, 1], ps[b][:].rearrange("p (m n) -> p m n", m=PAIRS), mpT[:, 0], HN[s])
                    elif s == "am":
                        low(r, s, am[:, 1], ps[b][:, 0:PAIRS * SLOTS], am[:, 0], HN[s])
                    elif s in ("bm0", "bm1"):
                        g = int(s[2])
                        if g == 0:
                            open_["bm"] = c_ = Chain(dve, bm_step, r)
                            dve.wait_ge(*gate_exp(r))
                            dve.wait_ge(*read["act"](r, fl.read("ms")))
                            c_.link(V.tensor_scalar(gr[:], gex[:], 1.0, None, ALU.add))
                            c_.link(V.tensor_tensor(gr[:], gr[:], msum[:], ALU.mult))
                            c_.link(V.reciprocal(gr[:], gr[:]))
                            if k is None or k >= 1:
                                dve.wait_ge(*o_ps(r - 1))
                        c_ = open_["bm"]
                        for m in (2 * g, 2 * g + 1):
                            src = ps[b][:, m % 2 * D:(m % 2 + 1) * D]
                            c_.inc(V.tensor_scalar(bm[:, 0, m, :], src, gr[:, m:m + 1], None, ALU.mult))
                        c_.sync()
                        for m in (2 * g, 2 * g + 1):
                            src = ps[b][:, m % 2 * D:(m % 2 + 1) * D]
                            ins = V.scalar_tensor_tensor(bm[:, 1, m, :], src, gr[:, m:m + 1], bm[:, 0, m, :], ALU.mult, ALU.subtract)
                            ins.then_inc(*last.up) if m % 2 else c_.inc(ins)
                    elif s[:2] == "gt":
                        m = int(s[2])
                        V.tensor_scalar(GT[:, m, :], ps[b][:], slotcol[:], None, ALU.is_equal).then_inc(*last.up)
                    elif s == "bss":
                        c_ = Chain(dve, pi, r)
                        V.tensor_scalar(inv[:], ps[b][:, 0:D], 1e-24, None, ALU.max).then_inc(*last.up)
                        dve.wait_ge(*last(r, fl.read("bss")))
                        c_.link(V.reciprocal(inv[:], inv[:]))
                        c_.link(V.tensor_tensor(pw[:, :, 0:D], w2, over(inv[:], [0, TILES], [1, D]), ALU.mult))
                        c_.link(V.tensor_reduce(bl[:], heads(pw[:, :, 0:D]), AX, ALU.add))
                        c_.link(V.tensor_tensor(bl[:], bl[:], over(btemp[:], [0, TILES], [1, HB]), ALU.mult))
                        c_.link(V.tensor_reduce(bmx[:], bl[:], AX, ALU.max))
                        c_.link(V.tensor_tensor(bl[:], bl[:], over(bmx[:], [1, TILES], [0, HB]), ALU.subtract))
                        open_["pi"] = c_
                    elif s == "bpi":
                        c_ = open_["pi"]
                        dve.wait_ge(*pi_exp(r))
                        c_.link(V.tensor_reduce(bsm[:], bl[:], AX, ALU.add))
                        c_.link(V.reciprocal(bsm[:], bsm[:]))
                        c_.link(V.tensor_tensor(pw[:, :, D:], bl[:], over(bsm[:], [1, TILES], [0, HB]), ALU.mult))
                        c_.link(V.tensor_tensor(heads(pw[:, :, 0:D]), heads(w2), over(pw[:, 0, D:], [PW, TILES], [1, HB], [0, DB]), ALU.mult))
                        c_.end()
                    elif s == "bdot":
                        V.tensor_copy(dot, ps[b][:, 0:PW]).then_inc(*last.up)
                    elif s == "res":
                        c_ = Chain(dve, res, r)
                        dve.wait_ge(*last(r, fl.read("bdot")))
                        c_.link(V.tensor_scalar(bden[:], dot[:, D:PW], 1e-8, None, ALU.add))
                        c_.link(V.reciprocal(bden[:], bden[:]))
                        c_.link(V.tensor_tensor(attn[:].rearrange("p (h d) -> p h d", d=DB), dot[:, 0:D].rearrange("p (h d) -> p h d", d=DB),
                                                over(bden[:], [1, HB], [0, DB]), ALU.mult))
                        c_.link(V.tensor_scalar(attn[:], attn[:], 1.0, None, ALU.add))
                        c_.link(V.reciprocal(attn[:], attn[:]))
                        c_.link(V.scalar_tensor_tensor(w, w, -1.0, over(attn[:], [0, TILES], [1, D]), ALU.mult, ALU.mult))
                        c_.link(V.tensor_tensor(heads(w), heads(w), over(pw[:, 0, D:], [PW, TILES], [1, HB], [0, DB]), ALU.mult))
                        c_.end()
                    elif s in ("oT0", "oT1"):
                        c = int(s[2])
                        low(r, s, hT[:, c, 1], ps[b][:], hT[:, c, 0], HN[s])
                    elif s in ("bo0", "bo1"):
                        g = int(s[2])
                        dve.wait_ge(*xb_set(r))
                        if k is None and g == 0:
                            dve.wait_ge(*out_made(r - 2))
                        src = ps[b][:].rearrange("p (t n) -> p t n", n=D)
                        V.scalar_tensor_tensor(x[:, p, 2 * g:2 * g + 2, :], src, 1 / W_UP, x2[:, 2 * g:2 * g + 2, :], ALU.mult, ALU.add).then_inc(*last.up)

                def end(r, g, part, k):
                    if part == 0:
                        qt = QORDER[g]
                        dve.wait_ge(*s_exp(r, (g + 1) * NH))
                        V.reciprocal(rinv[:], rsum[:, qt * NH:(qt + 1) * NH]).then_inc(*av_set.up)
                        dve.wait_ge(*av_set(r, 2 * g + 1))
                        dve.wait_ge(*av_ps(r, (g + 1) * NH))
                        if g:
                            dve.wait_ge(*av_lo(r, g))
                        elif k is None or k >= 1:
                            dve.wait_ge(*av_lo(r - 1))
                        V.tensor_tensor(av32[:].rearrange("p (n d) -> p n d", d=HP), ps[4][:].rearrange("p (n d) -> p n d", d=HP),
                                        over(rinv[:], [1, NH], [0, HP]), ALU.mult).then_inc(*av_set.up)
                    elif part == 2:
                        qt = QORDER[g]
                        dve.wait_ge(*o_ps(r, g + 1))
                        if g == 0 and (k is None or k >= 1):
                            dve.wait_ge(*out_done(r - 1))
                        V.scalar_tensor_tensor(xo[:, qt, :], ps[5][:, 0:D], 1 / W_UP, x[:, r.parity, qt, :], ALU.mult, ALU.add).then_inc(*out_made.up)

                def back(r, side, k):
                    p = r.parity
                    for i in range(SLOT_N):
                        if i < NI:
                            nk = (item(i)[0] + 1) * P
                            dve.wait_ge(*s_ps(r, i + 1))
                            if i >= 4:
                                dve.wait_ge(*s_exp(r, i - 3))
                            elif k is None or k >= 1:
                                dve.wait_ge(*s_exp(r - 1))
                            V.tensor_reduce(nmax[:, i % 4:i % 4 + 1], ps[i % 2][:, 0:nk], AX, ALU.max, negate=True).then_inc(*s_max.up)
                        if 2 <= i <= NI + 1:
                            j = i - 2
                            nk = (item(j)[0] + 1) * P
                            dve.wait_ge(*p_hi(r, j + 1))
                            V.tensor_tensor(pT[:, j % 3, 1, 0:nk], ps[2 + j % 2][:, 0:nk], pT[:, j % 3, 0, 0:nk], ALU.subtract).then_inc(*p_lo.up)
                        for g, part, ago in due(i, k):
                            end(r - ago, g, part, k)
                        for s in own["dve"].get(i, ()):
                            step(r, p, k, s)
                        side(i)

                front_back(dve, NB, run_front(step, ahead["dve"]), back)
                end(Round(NB // 2 - 1, 1), TILES - 1, 1, None)
                end(Round(NB // 2 - 1, 1), TILES - 1, 2, None)


def hybrid_block_program(nc, a):
    a["resid"] = nc.dram_tensor("resid", (NB, NT, D), F32, kind="Internal").ap()
    a["dispatched"] = nc.dram_tensor("dispatched", (NE * CAP, D), F32, kind="Internal").ap()
    a["expert_out"] = nc.dram_tensor("expert_out", (NE * CAP, D), F32, kind="Internal").ap()
    a["mid"] = nc.dram_tensor("mid", (NB, NT, D), F32, kind="Internal").ap()
    with ExitStack() as ctx:
        a["slot_of"] = ctx.enter_context(nc.sbuf_tensor("slot_of", [P, NB * TILES * TOPK], U32))
        a["gate_of"] = ctx.enter_context(nc.sbuf_tensor("gate_of", [P, NB * TILES * TOPK], F32))
        attention_a_stage(nc, a)
        expert_stage(nc, a)
        mixing_stage(nc, a, True)
        mixing_stage(nc, a, False)


def host_layout(inputs):
    f = np.float32
    inp = {k: np.ascontiguousarray(np.asarray(v)) for k, v in inputs.items()}
    rep = lambda v: np.ascontiguousarray(np.broadcast_to(v.reshape(1, -1), (P, v.size)))
    A = "L0_attn_a_"
    d = {
        "x": inp[A + "x"],
        "wqkvg": np.concatenate([inp[A + w] for w in ("Wq", "Wk", "Wv", "Wg")], axis=1),
        "wo": inp[A + "Wo"], "rw": inp[A + "router_W"],
        "s1": np.ascontiguousarray(inp[A + "norm1_scale"].reshape(KC, P).T),
        "s2b": rep(inp[A + "norm2_scale"]),
        "bqkvg": rep(np.concatenate([inp[A + b] for b in ("bq", "bk", "bv", "bg")])),
        "bo": rep(inp[A + "bo"]), "rb": rep(inp[A + "router_b"]),
        "w1": inp[A + "W1"], "w2": inp[A + "W2"],
        "b1": np.ascontiguousarray(inp[A + "b1"].reshape(NE, MC, P).transpose(2, 0, 1)),
        "b2": rep(inp[A + "b2"]).reshape(P, NE, D),
        "bw": np.ascontiguousarray(inp["L0_attn_b_Wqkv"].T), "bwout": np.ascontiguousarray(inp["L0_attn_b_Wout"].T),
        "btemp": rep(inp["L0_attn_b_temp"]), "bbout": rep(inp["L0_attn_b_bout"]),
        "mrw": inp["L0_ffn_mosa_router_w"],
        "mwqkv": inp["L0_ffn_mosa_wqkv"].reshape(D, NH * 3 * HP),
        "mwo": inp["L0_ffn_mosa_wo"],
        "dwqkv": np.ascontiguousarray(inp["L0_ffn_dense_wqkv"].reshape(D, NH, 3, HP).transpose(0, 2, 1, 3)).reshape(D, 3 * NH * HP),
        "dwo": inp["L0_ffn_dense_wo"],
    }
    pos = np.arange(NT, dtype=f).reshape(TILES, P).T
    half = DA // 2
    inv = (f(1.0) / np.power(f(10000.0), np.arange(half, dtype=f) / f(half))).astype(f)
    ang = pos[..., None] * inv
    sin, cos = np.sin(ang).astype(f), np.cos(ang).astype(f)
    d["cosa"] = np.concatenate([cos, cos], axis=-1)
    d["sina"] = np.concatenate([-sin, sin], axis=-1)
    half = ROT // 2
    inv = np.power(f(10000.0), -np.arange(half, dtype=f) / f(half)).astype(f)
    ang = pos[..., None] * inv
    sin, cos = np.sin(ang).astype(f), np.cos(ang).astype(f)
    d["cosd"] = np.concatenate([cos, cos], axis=-1)
    d["sind"] = np.concatenate([-sin, sin], axis=-1)
    d["rope_rows"] = np.concatenate([cos, sin], axis=-1)
    part = np.arange(P)
    d["ident"] = np.eye(P, dtype=f)
    d["bd"] = rep(np.zeros(2 * GRP * VA, f))
    d["bd"] = np.ascontiguousarray(np.tile((part[:, None] // DA == np.arange(GRP)[None, :]).astype(f)[:, None, :, None], (1, 2, 1, VA)).reshape(P, -1))
    bf = mybir.dt.np(BF16)
    d["before"] = (part[:, None] < part[None, :]).astype(f).astype(bf)
    d["iota8"] = np.ascontiguousarray(np.broadcast_to(np.arange(NE, dtype=f), (P, TOPK, NE)))
    d["ident16"] = np.eye(P, dtype=mybir.dt.np(F16))
    d["identb"] = np.eye(P, dtype=f).astype(bf)
    d["causal"] = np.where(part[:, None] >= part[None, :], 0.0, NEG).astype(bf)
    d["causal_pair"] = np.where((part[:, None] >= part[None, :]) & (part[:, None] // SLOTS == part[None, :] // SLOTS), 0.0, NEG).astype(bf)
    d["slot1"] = np.ascontiguousarray(np.broadcast_to(np.arange(1, SLOTS + 1, dtype=f), (P, SLOTS)))
    d["slotcol"] = (part % SLOTS + 1).astype(f).reshape(P, 1)
    d["headrow"] = (np.arange(NH)[:, None, None] == 2 * np.arange(PAIRS)[None, :, None] + part[None, None, :] // SLOTS).astype(f).astype(bf)
    return {k: np.ascontiguousarray(v) for k, v in d.items()}


def kernel(**inputs):
    import concourse.bacc as bacc
    from concourse.bass_utils import run_bass_kernel_spmd

    nc = bacc.Bacc("TRN2", target_bir_lowering=False, num_devices=1)
    arrays = host_layout(inputs)
    a = {name: nc.dram_tensor(name, v.shape, mybir.dt.from_np(v.dtype), kind="ExternalInput").ap() for name, v in arrays.items()}
    a["out"] = nc.dram_tensor("out", (NB, NT, D), F32, kind="ExternalOutput").ap()
    hybrid_block_program(nc, a)
    got = run_bass_kernel_spmd(nc, [arrays], core_ids=[0])
    return got.results[0]["out"]
```

```python
import concourse.bass as bass
from concourse import mybir
from contextlib import ExitStack
import numpy as np

F32 = mybir.dt.float32
BF16 = mybir.dt.bfloat16
F16 = mybir.dt.float16
I32 = mybir.dt.int32
U32 = mybir.dt.uint32
ALU = mybir.AluOpType
ACT = mybir.ActivationFunctionType
AX = mybir.AxisListType.X

P = 128
NB, NT, D = 16, 512, 256
TOK = NB * NT
TILES = NT // P
KC = D // P
HA, DA = 16, 16
CH = 64
NCH = NT // CH
VA = DA + 1
GRP = P // DA
NE, HID, TOPK = 8, 1024, 2
CAP = int(1.25 * (TOK / NE))
MC = HID // P
NH, HP = 8, 64
ROT = 32
SLOTS = NT // 8
PAIRS = NH // 2
HB, DB = 16, 16
LN_EPS = 1e-5
NEG = -1e30
W_UP = 64.0


class Sig:

    def __init__(self, ctx, nc, name, per=1, by=1):
        self.sem = ctx.enter_context(nc.semaphore(name))
        self.name, self.per, self.by = name, per, by
        self.up = (self.sem, by)

    def __call__(self, r, n=None):
        return self.sem, ((r.at if isinstance(r, Round) else r) * self.per + (self.per if n is None else n)) * self.by


class Chain:

    def __init__(self, eng, sig, r):
        self.eng, self.sig, self.r, self.n = eng, sig, r, 0

    def inc(self, ins):
        ins.then_inc(*self.sig.up)
        self.n += 1

    def sync(self):
        self.eng.wait_ge(*self.sig(self.r, self.n))

    def link(self, ins):
        self.inc(ins)
        self.sync()

    def end(self):
        assert self.n == self.sig.per, (self.sig.name, self.n, self.sig.per)


class Round:

    def __init__(self, half, parity):
        self.half, self.parity = half, parity
        self.at = half * 2 + parity

    def __sub__(self, n):
        p = self.parity - n
        return Round(self.half + p // 2, p % 2)


def overlapped(eng, count, order, step):
    def pair(r, k, nxt, k_next):
        for name in order:
            if name.startswith("b_"):
                step(name, r, r.parity, k)
            elif nxt is not None:
                step(name, nxt, nxt.parity, k_next)

    for name in order:
        if not name.startswith("b_"):
            step(name, Round(0, 0), 0, 0)
    pair(Round(0, 0), 0, Round(0, 1), 1)
    pair(Round(0, 1), 1, Round(1, 0), None)
    with eng.Fori(1, count // 2 - 1) as i:
        pair(Round(i, 0), None, Round(i, 1), None)
        pair(Round(i, 1), None, Round(i + 1, 0), None)
    last = count // 2 - 1
    pair(Round(last, 0), None, Round(last, 1), None)
    pair(Round(last, 1), None, None, None)


A_ORDER = {
    "sp": "x b_res",
    "pool": "b_res ln sum0 sum1 sum2 sum3 b_send",
    "pe": "b_o ln t0 t1 b_hn t2 kv0 t3 kv1 kv2 kv3 qT b_rank num",
    "act": "b_o b_square ln t0 b_hn t1 t2 t3 b_gate qT",
    "dve": "ln b_y b_hn t0 t1 b_route t2 sum0 t3 sum1 fin sum2 sum3 b_slots o",
}


def settle(eng):
    eng.nop(nofuse=True)


class TwoSig:

    def __init__(self, ctx, nc, name, per=1, by=16):
        self.sig = [Sig(ctx, nc, name + s, per, by) for s in ("_even", "_odd")]

    def up(self, r):
        return self.sig[r.parity].up

    def __call__(self, r, n=None):
        return self.sig[r.parity](r.half, n)


RSQRT_STEPS = 11


def rsqrt(nc, chain, y, v, t, part=None):
    if part != 1:
        chain.link(nc.vector.tensor_scalar(y.bitcast(I32), v.bitcast(I32), 1, None, ALU.logical_shift_right))
        chain.link(nc.vector.tensor_scalar(y.bitcast(I32), y.bitcast(I32), -1.0, 1597463007.0, ALU.mult, ALU.add))
    for _ in range({None: 3, 0: 1, 1: 2}[part]):
        chain.link(nc.vector.scalar_tensor_tensor(t, y, -0.5, y, ALU.mult, ALU.mult))
        chain.link(nc.vector.tensor_tensor(t, t, v, ALU.mult))
        chain.link(nc.vector.scalar_tensor_tensor(y, t, 1.5, y, ALU.add, ALU.mult))


def over(ap, *dims):
    return bass.AP(ap.tensor, ap.offset, [list(ap.ap[0])] + [list(d) for d in dims])


def attention_a_stage(nc, a):
    with ExitStack() as ctx:
        sb = lambda name, shape, dt=F32: ctx.enter_context(nc.sbuf_tensor(name, shape, dt))
        sig = lambda name, per=1, by=1: Sig(ctx, nc, "a_" + name, per, by)
        two = lambda name, per=1: TwoSig(ctx, nc, "a_" + name, per)
        ps = [ctx.enter_context(nc.psum_tensor(f"a_ps{i}", [P, 512], F32)) for i in range(8)]
        ident = sb("a_ident", [P, P])
        wqkvg = sb("a_wqkvg", [P, KC, 4 * D])
        wo = sb("a_wo", [P, KC, D])
        rw = sb("a_rw", [P, KC, NE])
        s1 = sb("a_s1", [P, KC])
        s2b = sb("a_s2b", [P, D])
        bqkvg = sb("a_bqkvg", [P, 4 * D])
        bo = sb("a_bo", [P, D])
        rb = sb("a_rb", [P, NE])
        cosa = sb("a_cos", [P, TILES, DA])
        sina = sb("a_sin", [P, TILES, DA])
        bd = sb("a_bd", [P, 2 * GRP * VA])
        before = sb("a_before", [P, P], BF16)
        ones = sb("a_ones", [P, P], BF16)
        iota8 = sb("a_iota8", [P, TOPK, NE])
        xs = sb("a_x", [P, 2, TILES, D])
        stats = sb("a_stats", [P, TILES, 6])
        mv = sb("a_mv", [P, TILES, 2])
        v2 = sb("a_v2", [P, 2, TILES])
        rs = sb("a_rs", [P, 2, TILES])
        rt = sb("a_rt", [P, 2, TILES])
        h = sb("a_h", [P, TILES, D])
        hb = sb("a_hb", [P, TILES, D])
        u = sb("a_u", [P, TILES, D])
        uT = sb("a_uT", [P, KC, NT])
        qk = sb("a_qk", [P, TILES, 2 * D])
        ra = sb("a_ra", [P, 2 * D])
        rc = sb("a_rc", [P, 2 * D])
        mn = sb("a_mn", [P, TILES, 2 * D])
        va = sb("a_va", [P, TILES, HA, VA])
        z = sb("a_z", [P, TILES, D])
        run = sb("a_run", [P, NCH, 2 * GRP * VA])
        state = sb("a_state", [P, NCH, 2 * GRP * VA])
        qT = sb("a_qT", [P, KC, NT])
        den = sb("a_den", [P, TILES, HA])
        dd = sb("a_dd", [P, TILES, D])
        o = sb("a_o", [P, TILES, D])
        oT = sb("a_oT", [P, KC, NT])
        y = sb("a_y", [P, TILES, D])
        sq = sb("a_sq", [P, D])
        ssq = sb("a_ssq", [P, TILES])
        ssn = sb("a_ssn", [P, TILES])
        rr = sb("a_rr", [P, TILES])
        rrt = sb("a_rrt", [P, TILES])
        hn = sb("a_hn", [P, 2, TILES, D])
        hnT = sb("a_hnT", [P, KC, NT])
        res = sb("a_res", [P, 2, TILES, D])
        lg = sb("a_lg", [P, TILES, NE])
        top = sb("a_top", [P, TILES, 8])
        topi = sb("a_topi", [P, TILES, 8], U32)
        ef = sb("a_ef", [P, TILES, TOPK])
        oh = sb("a_oh", [P, TILES, TOPK, NE])
        msk = sb("a_msk", [P, TILES, NE], BF16)
        rank = sb("a_rank", [P, TILES, NE])
        carry = sb("a_carry", [P, NE])
        rk = sb("a_rk", [P, TILES, TOPK, NE])
        rsel = sb("a_rsel", [P, TILES, TOPK])
        ok = sb("a_ok", [P, TILES, TOPK])
        slf = sb("a_slf", [P, TILES, TOPK])
        sld = sb("a_sld", [P, TILES, TOPK])
        sli = sb("a_sli", [P, 2, TILES, TOPK], U32)
        ge = sb("a_ge", [P, TILES])
        gd = sb("a_gd", [P, TILES])
        gg = sb("a_gg", [P, TILES, TOPK])
        zero = sb("a_zero", [P, 2560])
        slot_of, gate_of = a["slot_of"], a["gate_of"]

        consts = [(ident[:], a["ident"]), (wqkvg[:], a["wqkvg"].rearrange("(k p) n -> p k n", p=P)),
                  (wo[:], a["wo"].rearrange("(k p) n -> p k n", p=P)),
                  (rw[:], a["rw"].rearrange("(k p) n -> p k n", p=P)), (s1[:], a["s1"]), (s2b[:], a["s2b"]),
                  (bqkvg[:], a["bqkvg"]), (bo[:], a["bo"]), (rb[:], a["rb"]), (cosa[:], a["cosa"]),
                  (sina[:], a["sina"]), (bd[:], a["bd"]), (before[:], a["before"]), (iota8[:], a["iota8"])]
        const_in = sig("const_in", len(consts), 16)
        zeroed = sig("zeroed")
        cleared = Sig(a["lasting"], nc, "a_cleared", 8, 16)
        ones_set = sig("ones_set", 3)
        w_scaled = sig("w_scaled", KC)
        x_in = two("x_in")
        normed = sig("normed", 18 + RSQRT_STEPS)
        hb_made = sig("hb_made")
        flipped = sig("flipped", 4)
        evac = sig("evac", 4)
        b_flipped = sig("b_flipped", 4)
        b_evac = sig("b_evac", 4)
        proj = sig("proj", 2 * TILES)
        qk_step = sig("qk_step", 5 * TILES)
        vg_step = sig("vg_step", 3 * TILES)
        e_qk = sig("e_qk", TILES)
        e_z = sig("e_z", TILES)
        phi = sig("phi", TILES)
        kv = sig("kv", NCH)
        summed = sig("summed", NCH)
        masked = sig("masked", NCH)
        num = sig("num", TILES)
        o_step = sig("o_step", 4 * TILES)
        ao = sig("ao", TILES)
        y_made = sig("y_made", TILES)
        squared = sig("squared", TILES)
        hn_step = sig("hn_step", 1 + RSQRT_STEPS + TILES)
        res_made = sig("res_made")
        res_out = two("res_out")
        logit = sig("logit")
        route = sig("route", 15)
        ranked = sig("ranked")
        g_exp = sig("g_exp")
        slots = sig("slots", 17)
        sent = TwoSig(a["lasting"], nc, "a_sent", TILES * TOPK)

        with nc.Block() as block:

            @block.sync
            def _(sp):
                for to, of in consts:
                    sp.dma_start(to, of).then_inc(*const_in.up)

                def step(s, r, p, k):
                    if s == "x":
                        if k is None:
                            sp.wait_ge(*res_made(r - 2))
                        sp.dma_start(xs[:, p], a["x"][r.at].rearrange("(t p) n -> p t n", p=P)).then_inc(*x_in.up(r))
                    else:
                        sp.wait_ge(*res_made(r))
                        sp.dma_start(a["resid"][r.at].rearrange("(t p) n -> p t n", p=P), res[:, p]).then_inc(*res_out.up(r))

                overlapped(sp, NB, A_ORDER["sp"].split(), step)
                last = Round(NB // 2 - 1, 1)
                sp.wait_ge(*res_out(last - 1))
                sp.wait_ge(*res_out(last))

            @block.gpsimd
            def _(pool):
                nc.gpsimd.memset(zero[:], 0.0).then_inc(*zeroed.up)
                pool.wait_ge(*zeroed(0))
                n = NE * CAP * D // (8 * 2560)
                cells = a["dispatched"].rearrange("r n -> (r n)").rearrange("(c p n) -> c p n", c=8, p=n)
                for c in range(8):
                    pool.dma_start(cells[c], zero[0:n, :]).then_inc(*cleared.up)
                pool.wait_ge(*const_in(0))

                def step(s_, r, p, k):
                    if s_ == "ln":
                        pool.wait_ge(*normed(r))
                        if k is None or k >= 1:
                            pool.wait_ge(*y_made(r - 1))
                        nc.gpsimd.tensor_tensor(hb[:], h[:], over(bo[:], [0, TILES], [1, D]), ALU.add).then_inc(*hb_made.up)
                    elif s_[:3] == "sum":
                        if s_ == "sum0" and (k is None or k >= 1):
                            pool.wait_ge(*num(r - 1))
                        for c in (2 * int(s_[3]), 2 * int(s_[3]) + 1):
                            pool.wait_ge(*summed(r, c + 1))
                            nc.gpsimd.tensor_tensor(state[:, c, :], run[:, c, :], bd[:], ALU.mult).then_inc(*masked.up)
                    elif s_ == "b_res":
                        pool.wait_ge(*y_made(r))
                        if k is None:
                            pool.wait_ge(*res_out(r - 2))
                        nc.gpsimd.tensor_tensor(res[:, p], xs[:, p], y[:], ALU.add).then_inc(*res_made.up)
                    elif s_ == "b_send":
                        pool.wait_ge(*slots(r))
                        if k == 0:
                            pool.wait_ge(*cleared(0))
                        settle(pool)
                        for t in range(TILES):
                            for c in range(TOPK):
                                pool.indirect_dma_start(
                                    a["dispatched"], bass.IndirectOffsetOnAxis(ap=sli[:, p, t, c:c + 1], axis=0),
                                    hn[:, p, t, :], None, bounds_check=NE * CAP - 1, oob_is_err=False).then_inc(*sent.up(r))

                overlapped(pool, NB, A_ORDER["pool"].split(), step)
                last = Round(NB // 2 - 1, 1)
                pool.wait_ge(*sent(last - 1))
                pool.wait_ge(*sent(last))

            @block.tensor
            def _(pe):
                pe.wait_ge(*const_in(0))
                pe.wait_ge(*w_scaled(0))
                pe.wait_ge(*ones_set(0))

                def flip(src, bank, up):
                    for c in range(KC):
                        for t in range(TILES):
                            ins = nc.tensor.transpose(ps[bank + c][:, t * P:(t + 1) * P], src(t, c), ident[:])
                        ins.then_inc(*up.up)

                def step(s_, r, p, k):
                    if s_ == "ln":
                        pe.wait_ge(*normed(r))
                        if k is None or k >= 1:
                            pe.wait_ge(*o_step(r - 1))
                        flip(lambda t, c: u[:, t, c * P:(c + 1) * P], 0, flipped)
                    elif s_[0] == "t":
                        t = int(s_[1])
                        pe.wait_ge(*evac(r, 2))
                        for j in range(2):
                            if t:
                                pe.wait_ge(*(qk_step(r, 5 * t - 4) if j == 0 else vg_step(r, 3 * t - 1)))
                            elif k is None or k >= 1:
                                pe.wait_ge(*(qk_step(r - 1, 5 * TILES - 4) if j == 0 else vg_step(r - 1, 3 * TILES - 1)))
                            for c in range(KC):
                                ins = nc.tensor.matmul(ps[2 + j][:], uT[:, c, t * P:(t + 1) * P],
                                                       wqkvg[:, c, j * 512:(j + 1) * 512], start=c == 0, stop=c == KC - 1)
                            ins.then_inc(*proj.up)
                    elif s_[:2] == "kv":
                        for c in (2 * int(s_[2]), 2 * int(s_[2]) + 1):
                            t, q = c // 2, (c % 2) * CH
                            pe.wait_ge(*phi(r, t + 1))
                            if c >= 2:
                                pe.wait_ge(*summed(r, c - 1))
                            elif k is None or k >= 1:
                                pe.wait_ge(*o_step(r - 1))
                            for g in range(2):
                                ins = nc.tensor.matmul(ps[4 + c % 2][:, g * GRP * VA:(g + 1) * GRP * VA],
                                                       qk[q:q + CH, t, D + g * P:D + (g + 1) * P],
                                                       va[q:q + CH, t, g * GRP:(g + 1) * GRP, :].rearrange("p h e -> p (h e)"), start=True, stop=True)
                            ins.then_inc(*kv.up)
                    elif s_ == "qT":
                        flip(lambda t, c: qk[:, t, c * P:(c + 1) * P], 0, flipped)
                        pe.wait_ge(*evac(r, 4))
                    elif s_ == "num":
                        for t in range(TILES):
                            if t < 2:
                                pe.wait_ge(*summed(r, NCH - 1 + t))
                            for c in (2 * t, 2 * t + 1):
                                q = (c % 2) * CH
                                pe.wait_ge(*masked(r, c + 1))
                                for g in range(2):
                                    cols = slice(g * GRP * VA, (g + 1) * GRP * VA)
                                    ins = nc.tensor.matmul(ps[(4 + t) % 6][q:q + CH, cols], qT[:, g, c * CH:(c + 1) * CH],
                                                           state[:, c, cols], start=True, stop=True)
                            ins.then_inc(*num.up)
                    elif s_ == "b_o":
                        pe.wait_ge(*o_step(r))
                        if k is None or k >= 1:
                            pe.wait_ge(*slots(r - 1, 3))
                        flip(lambda t, c: o[:, t, c * P:(c + 1) * P], 6, b_flipped)
                        pe.wait_ge(*b_evac(r, 2))
                        for t in range(TILES):
                            for c in range(KC):
                                ins = nc.tensor.matmul(ps[6 + t // 2][:, (t % 2) * D:(t % 2 + 1) * D], oT[:, c, t * P:(t + 1) * P],
                                                       wo[:, c, :], start=c == 0, stop=c == KC - 1)
                            ins.then_inc(*ao.up)
                    elif s_ == "b_hn":
                        pe.wait_ge(*hn_step(r))
                        flip(lambda t, c: hn[:, p, t, c * P:(c + 1) * P], 6, b_flipped)
                        pe.wait_ge(*b_evac(r, 4))
                        for t in range(TILES):
                            for c in range(KC):
                                ins = nc.tensor.matmul(ps[6][:, t * NE:(t + 1) * NE], hnT[:, c, t * P:(t + 1) * P], rw[:, c, :],
                                                       start=c == 0, stop=c == KC - 1)
                        ins.then_inc(*logit.up)
                    elif s_ == "b_rank":
                        pe.wait_ge(*route(r))
                        nc.tensor.matmul(ps[7][:, 0:TILES * NE], before[:], msk[:].rearrange("p t e -> p (t e)"), start=True, stop=False)
                        for t in range(TILES - 1):
                            nc.tensor.matmul(ps[7][:, (t + 1) * NE:TILES * NE], ones[:],
                                             over(msk[:, t, :], [0, TILES - 1 - t], [1, NE]), start=False, stop=t == TILES - 2)
                        for t in range(TILES):
                            ins = nc.tensor.matmul(ps[7][:, TILES * NE:(TILES + 1) * NE], ones[:], msk[:, t, :],
                                                   start=t == 0, stop=t == TILES - 1)
                        ins.then_inc(*ranked.up)

                overlapped(pe, NB, A_ORDER["pe"].split(), step)

            @block.scalar
            def _(act):
                def step(s_, r, p, k):
                    def out(dst, n, bank, made, up):
                        for c in range(KC):
                            act.wait_ge(*made(r, n + c + 1))
                            nc.scalar.activation(dst[:, c, :], ps[bank + c][:], ACT.Copy).then_inc(*up.up)

                    if s_ == "ln":
                        if k is None or k >= 1:
                            act.wait_ge(*proj(r - 1))
                        out(uT, 0, 0, flipped, evac)
                    elif s_[0] == "t":
                        t = int(s_[1])
                        act.wait_ge(*qk_step(r, 5 * t + 5))
                        nc.scalar.activation(mn[:, t, :], mn[:, t, :], ACT.Exp).then_inc(*e_qk.up)
                        act.wait_ge(*vg_step(r, 3 * t + 3))
                        nc.scalar.activation(z[:, t, :], z[:, t, :], ACT.Exp).then_inc(*e_z.up)
                    elif s_ == "qT":
                        if k is None or k >= 1:
                            act.wait_ge(*num(r - 1))
                        out(qT, 2, 0, flipped, evac)
                    elif s_ == "b_o":
                        if k is None or k >= 1:
                            act.wait_ge(*ao(r - 1))
                        out(oT, 0, 6, b_flipped, b_evac)
                    elif s_ == "b_square":
                        for t in range(TILES):
                            act.wait_ge(*y_made(r, t + 1))
                            if t:
                                act.wait_ge(*squared(r, t))
                            elif k is None or k >= 1:
                                act.wait_ge(*hn_step(r - 1, 1))
                            nc.scalar.activation(sq[:], y[:, t, :], ACT.Square, accum_out=ssq[:, t:t + 1]).then_inc(*squared.up)
                    elif s_ == "b_hn":
                        if k is None or k >= 1:
                            act.wait_ge(*logit(r - 1))
                        out(hnT, 2, 6, b_flipped, b_evac)
                    elif s_ == "b_gate":
                        act.wait_ge(*slots(r, 1))
                        nc.scalar.activation(ge[:], gd[:], ACT.Exp).then_inc(*g_exp.up)

                overlapped(act, NB, A_ORDER["act"].split(), step)

            @block.vector
            def _(dve):
                nc.vector.memset(ones[:], 1.0).then_inc(*ones_set.up)
                nc.vector.memset(va[:], 1.0).then_inc(*ones_set.up)
                nc.vector.memset(carry[:], 0.0).then_inc(*ones_set.up)
                dve.wait_ge(*ones_set(0))
                dve.wait_ge(*const_in(0))
                for c in range(KC):
                    nc.vector.tensor_scalar(wqkvg[:, c, :], wqkvg[:, c, :], s1[:, c:c + 1], None, ALU.mult).then_inc(*w_scaled.up)

                def step(s_, r, p, k):
                    if s_ == "ln":
                        dve.wait_ge(*x_in(r))
                        n = Chain(dve, normed, r)
                        if k is None or k >= 1:
                            dve.wait_ge(*normed(r - 1))
                        for t in range(TILES):
                            n.inc(nc.vector.bn_stats(stats[:, t, :], xs[:, p, t, :]))
                        n.sync()
                        settle(dve)
                        for t in range(TILES):
                            n.inc(nc.vector.bn_aggr(mv[:, t, :], stats[:, t, :]))
                        n.sync()
                        n.inc(nc.vector.tensor_scalar(v2[:, 0, :], mv[:, :, 1], LN_EPS, None, ALU.add))
                        n.link(nc.vector.tensor_copy(v2[:, 1, :], mv[:, :, 1]))
                        rsqrt(nc, n, rs[:], v2[:], rt[:])
                        if k is None or k >= 1:
                            dve.wait_ge(*hb_made(r - 1))
                        for t in range(TILES):
                            n.inc(nc.vector.tensor_scalar(h[:, t, :], xs[:, p, t, :], mv[:, t, 0:1], rs[:, 0, t:t + 1],
                                                          ALU.subtract, ALU.mult))
                        if k is None or k >= 1:
                            dve.wait_ge(*flipped(r - 1, 2))
                        for t in range(TILES):
                            n.inc(nc.vector.tensor_scalar(u[:, t, :], xs[:, p, t, :], mv[:, t, 0:1], rs[:, 1, t:t + 1],
                                                          ALU.subtract, ALU.mult))
                        n.end()
                    elif s_[0] == "t" or s_ == "fin":
                        def finish(t):
                            dve.wait_ge(*e_qk(r, t + 1))
                            nc.vector.scalar_tensor_tensor(qk[:, t, :], qk[:, t, :], 0.0, mn[:, t, :], ALU.max, ALU.add).then_inc(*phi.up)

                        if s_ == "fin":
                            finish(TILES - 1)
                            return
                        t = int(s_[1])
                        q, w = Chain(dve, qk_step, r), Chain(dve, vg_step, r)
                        q.n, w.n = 5 * t, 3 * t
                        if t == 0 and (k is None or k >= 1):
                            dve.wait_ge(*flipped(r - 1))
                            dve.wait_ge(*kv(r - 1))
                            dve.wait_ge(*o_step(r - 1))
                        dve.wait_ge(*proj(r, 2 * t + 1))
                        q.inc(nc.vector.tensor_tensor(qk[:, t, :], ps[2][:], bqkvg[:, 0:512], ALU.add))
                        dve.wait_ge(*proj(r, 2 * t + 2))
                        w.inc(nc.vector.tensor_tensor(va[:, t, :, 0:DA], ps[3][:, 0:D].rearrange("p (h e) -> p h e", e=DA),
                                                      bqkvg[:, 512:768].rearrange("p (h e) -> p h e", e=DA), ALU.add))
                        w.inc(nc.vector.tensor_tensor(z[:, t, :], ps[3][:, D:2 * D], bqkvg[:, 768:1024], ALU.add))
                        q.sync()
                        x3 = qk[:, t, :].rearrange("p (h s d) -> p h s d", s=2, d=DA // 2)
                        q.inc(nc.vector.tensor_tensor(ra[:].rearrange("p (h d) -> p h d", d=DA),
                                                      qk[:, t, :].rearrange("p (h d) -> p h d", d=DA),
                                                      over(cosa[:, t, :], [0, 2 * HA], [1, DA]), ALU.mult))
                        q.inc(nc.vector.tensor_tensor(rc[:].rearrange("p (h s d) -> p h s d", s=2, d=DA // 2), x3[:, :, ::-1, :],
                                                      over(sina[:, t, :], [0, 2 * HA], [DA // 2, 2], [1, DA // 2]), ALU.mult))
                        w.sync()
                        w.inc(nc.vector.tensor_scalar(z[:, t, :], z[:, t, :], -1.0, 80.0, ALU.mult, ALU.min))
                        q.sync()
                        q.inc(nc.vector.tensor_tensor(qk[:, t, :], ra[:], rc[:], ALU.add))
                        if t:
                            finish(t - 1)
                        q.sync()
                        q.inc(nc.vector.tensor_scalar(mn[:, t, :], qk[:, t, :], 0.0, None, ALU.min))
                    elif s_[:3] == "sum":
                        if s_ == "sum0" and (k is None or k >= 1):
                            dve.wait_ge(*masked(r - 1))
                        for c in (2 * int(s_[3]), 2 * int(s_[3]) + 1):
                            dve.wait_ge(*kv(r, c + 1))
                            d = ps[4 + c % 2][:, 0:2 * GRP * VA]
                            if c == 0:
                                nc.vector.tensor_copy(run[:, 0, :], d).then_inc(*summed.up)
                            else:
                                dve.wait_ge(*summed(r, c))
                                nc.vector.tensor_tensor(run[:, c, :], d, run[:, c - 1, :], ALU.add).then_inc(*summed.up)
                    elif s_ == "o":
                        s = Chain(dve, o_step, r)
                        if k is None or k >= 1:
                            dve.wait_ge(*b_flipped(r - 1, 2))
                        heads = lambda v: v.rearrange("p (h e) -> p h e", e=DA)
                        nv = [ps[(4 + t) % 6][:, 0:HA * VA].rearrange("p (h e) -> p h e", e=VA) for t in range(TILES)]
                        for t in range(TILES):
                            dve.wait_ge(*num(r, t + 1))
                            s.inc(nc.vector.tensor_scalar(den[:, t], nv[t][:, :, DA], 1e-6, None, ALU.add))
                        s.sync()
                        dve.wait_ge(*e_z(r))
                        for t in range(TILES):
                            s.inc(nc.vector.scalar_tensor_tensor(heads(dd[:, t]), heads(z[:, t, :]), 1.0, over(den[:, t], [1, HA], [0, DA]),
                                                                 ALU.add, ALU.mult))
                        s.sync()
                        for t in range(TILES):
                            s.inc(nc.vector.reciprocal(dd[:, t], dd[:, t]))
                        s.sync()
                        for t in range(TILES):
                            s.inc(nc.vector.tensor_tensor(heads(o[:, t, :]), nv[t][:, :, 0:DA], heads(dd[:, t]), ALU.mult))
                        s.end()
                    elif s_ == "b_y":
                        dve.wait_ge(*hb_made(r))
                        if k is None or k >= 1:
                            dve.wait_ge(*res_made(r - 1))
                        for t in range(TILES):
                            dve.wait_ge(*ao(r, t // 2 * 2 + 2))
                            nc.vector.tensor_tensor(y[:, t, :], ps[6 + t // 2][:, (t % 2) * D:(t % 2 + 1) * D], hb[:, t, :],
                                                    ALU.add).then_inc(*y_made.up)
                    elif s_ == "b_hn":
                        s = Chain(dve, hn_step, r)
                        dve.wait_ge(*squared(r))
                        s.link(nc.vector.tensor_scalar(ssn[:], ssq[:], 1.0 / D, None, ALU.mult))
                        rsqrt(nc, s, rr[:], ssn[:], rrt[:])
                        if k is None:
                            dve.wait_ge(*sent(r - 2))
                        for t in range(TILES):
                            dve.wait_ge(*y_made(r, t + 1))
                            s.inc(nc.vector.scalar_tensor_tensor(hn[:, p, t, :], y[:, t, :], rr[:, t:t + 1], s2b[:], ALU.mult, ALU.mult))
                        s.end()
                    elif s_ == "b_route":
                        s = Chain(dve, route, r)
                        dve.wait_ge(*logit(r))
                        s.link(nc.vector.tensor_tensor(lg[:], ps[6][:, 0:TILES * NE].rearrange("p (t e) -> p t e", e=NE),
                                                       over(rb[:], [0, TILES], [1, NE]), ALU.add))
                        settle(dve)
                        for t in range(TILES):
                            s.inc(nc.vector.max(top[:, t, :], lg[:, t, :]))
                        s.sync()
                        settle(dve)
                        for t in range(TILES):
                            s.inc(nc.vector.max_index(topi[:, t, :], top[:, t, :], lg[:, t, :]))
                        s.sync()
                        s.link(nc.vector.tensor_copy(ef[:], topi[:, :, 0:TOPK]))
                        for t in range(TILES):
                            s.inc(nc.vector.tensor_tensor(oh[:, t], iota8[:], over(ef[:, t, :], [1, TOPK], [0, NE]), ALU.is_equal))
                        s.sync()
                        if k is None or k >= 1:
                            dve.wait_ge(*ranked(r - 1))
                        s.link(nc.vector.tensor_tensor(msk[:], oh[:, :, 0, :], oh[:, :, 1, :], ALU.add))
                        s.end()
                    elif s_ == "b_slots":
                        s = Chain(dve, slots, r)
                        if k is None or k >= 1:
                            dve.wait_ge(*g_exp(r - 1))
                        s.inc(nc.vector.tensor_tensor(gd[:], top[:, :, 1], top[:, :, 0], ALU.subtract))
                        dve.wait_ge(*ranked(r))
                        s.link(nc.vector.tensor_tensor(rank[:], ps[7][:, 0:TILES * NE].rearrange("p (t e) -> p t e", e=NE),
                                                       over(carry[:], [0, TILES], [1, NE]), ALU.add))
                        s.link(nc.vector.tensor_tensor(carry[:], ps[7][:, TILES * NE:(TILES + 1) * NE], carry[:], ALU.add))
                        for t in range(TILES):
                            s.inc(nc.vector.tensor_tensor(rk[:, t], oh[:, t], over(rank[:, t, :], [0, TOPK], [1, NE]), ALU.mult))
                        s.sync()
                        s.link(nc.vector.tensor_reduce(rsel[:], rk[:], AX, ALU.add))
                        s.inc(nc.vector.tensor_scalar(ok[:], rsel[:], float(CAP), None, ALU.is_lt))
                        s.link(nc.vector.scalar_tensor_tensor(slf[:], ef[:], float(CAP), rsel[:], ALU.mult, ALU.add))
                        s.inc(nc.vector.tensor_scalar(sld[:], ok[:], -1e6, 1e6, ALU.mult, ALU.add))
                        s.link(nc.vector.tensor_tensor(slot_of[:, bass.ds(r.at * TILES * TOPK, TILES * TOPK)],
                                                       slf[:].rearrange("p t c -> p (t c)"), ok[:].rearrange("p t c -> p (t c)"), ALU.mult))
                        s.inc(nc.vector.tensor_tensor(sli[:, p], slf[:], sld[:], ALU.add))
                        dve.wait_ge(*g_exp(r))
                        s.link(nc.vector.tensor_scalar(gd[:], ge[:], 1.0, None, ALU.add))
                        s.link(nc.vector.reciprocal(gg[:, :, 0], gd[:]))
                        s.link(nc.vector.tensor_tensor(gg[:, :, 1], gg[:, :, 0], ge[:], ALU.mult))
                        s.inc(nc.vector.tensor_tensor(gate_of[:, bass.ds(r.at * TILES * TOPK, TILES * TOPK)],
                                                      gg[:].rearrange("p t c -> p (t c)"), ok[:].rearrange("p t c -> p (t c)"), ALU.mult))
                        s.end()

                overlapped(dve, NB, A_ORDER["dve"].split(), step)


E_ORDER = {
    "sp": "load b_store",
    "pe": "b_span0 b_span1 x0 b_span2 x1 x2",
    "act": "b_span0 b_span1 w1 x0 b_span2 w2 x1 x2",
    "dve": "b_span0 b_span1 w1 x0 b_span2 w2 x1 x2",
}


def expert_stage(nc, a):
    with ExitStack() as ctx:
        sb = lambda name, shape, dt=F32: ctx.enter_context(nc.sbuf_tensor("e_" + name, shape, dt))
        sig = lambda name, per=1, by=1: Sig(ctx, nc, "e_" + name, per, by)
        two = lambda name, per=1: TwoSig(ctx, nc, "e_" + name, per)
        ps = [ctx.enter_context(nc.psum_tensor(f"e_ps{i}", [P, 512], F32)) for i in range(8)]
        ST = CAP // P
        SPANS = [(s, min(512, CAP - s)) for s in range(0, CAP, 512)]
        NS = len(SPANS)
        ident = sb("ident", [P, P])
        b1 = sb("b1", [P, NE, MC])
        b2 = sb("b2", [P, NE, D])
        b2e = sb("b2e", [P, D])
        b1e = sb("b1e", [P, MC])
        w1 = sb("w1", [P, 2, KC, HID])
        w2 = sb("w2", [P, 2, MC, D])
        w1s = sb("w1s", [P, 2, 2, KC, HID], F16)
        w2s = sb("w2s", [P, 2, 2, MC, D], F16)
        xt = sb("xt", [P, 2, ST, D])
        xT = sb("xT", [P, 2, 2, KC, CAP], F16)
        hid32 = sb("hid32", [P, 3, 512])
        hid = sb("hid", [P, 2, 2, MC, 512], F16)
        yt = sb("yt", [P, 2, ST, D])

        const_in = sig("const_in", 3, 16)
        loaded = two("loaded", 3)
        bias_set = sig("bias_set", 2)
        w_hi = sig("w_hi", 2)
        w_lo = sig("w_lo", 2)
        flipped = sig("flipped", KC * NS)
        x_hi = sig("x_hi", KC * NS)
        x_lo = sig("x_lo", KC * NS)
        up = sig("up", MC * NS)
        act_done = sig("act_done", MC * NS)
        hid_hi = sig("hid_hi", MC * NS)
        hid_lo = sig("hid_lo", MC * NS)
        down = sig("down", ST)
        y_set = sig("y_set", ST)
        stored = two("stored")

        with nc.Block() as block:

            @block.sync
            def _(sp):
                sp.dma_start(ident[:], a["ident"]).then_inc(*const_in.up)
                sp.dma_start(b1[:], a["b1"]).then_inc(*const_in.up)
                sp.dma_start(b2[:], a["b2"]).then_inc(*const_in.up)

                def step(s, r, p, k):
                    if s == "load":
                        if k is None:
                            sp.wait_ge(*flipped(r - 2))
                            sp.wait_ge(*w_lo(r - 2))
                        sp.dma_start(w1[:, p], a["w1"][r.at].rearrange("(k p) n -> p k n", p=P)).then_inc(*loaded.up(r))
                        sp.dma_start(w2[:, p], a["w2"][r.at].rearrange("(m p) n -> p m n", p=P)).then_inc(*loaded.up(r))
                        sp.dma_start(xt[:, p], a["dispatched"].rearrange("(e t p) n -> e p t n", e=NE, p=P)[r.at]).then_inc(*loaded.up(r))
                    else:
                        sp.wait_ge(*y_set(r))
                        sp.dma_start(a["expert_out"].rearrange("(e t p) n -> e p t n", e=NE, p=P)[r.at], yt[:, p]).then_inc(*stored.up(r))

                overlapped(sp, NE, E_ORDER["sp"].split(), step)
                last = Round(NE // 2 - 1, 1)
                sp.wait_ge(*stored(last - 1))
                sp.wait_ge(*stored(last))

            @block.tensor
            def _(pe):
                pe.wait_ge(*const_in(0))

                def products(to, n, left, right):
                    for c in range(n):
                        for i, j in ((0, 0), (0, 1), (1, 0)):
                            ins = nc.tensor.matmul(to, left(i, c), right(j, c), start=c + i + j == 0, stop=c == n - 1 and i == 1)
                    return ins

                def step(name, r, p, k):
                    def upward(s):
                        at, n = SPANS[s]
                        pe.wait_ge(*x_lo(r, (s + 1) * KC))
                        pe.wait_ge(*w_lo(r, 1))
                        for m in range(MC):
                            i = s * MC + m
                            if i >= 3:
                                pe.wait_ge(*act_done(r, i - 2))
                            elif k is None or k >= 1:
                                pe.wait_ge(*act_done(r - 1))
                            products(ps[2 + i % 3][:, 0:n], KC, lambda i_, c: w1s[:, p, i_, c, m * P:(m + 1) * P],
                                     lambda j, c: xT[:, p, j, c, at:at + n]).then_inc(*up.up)

                    def downward(s):
                        at, n = SPANS[s]
                        pe.wait_ge(*hid_lo(r, (s + 1) * MC))
                        pe.wait_ge(*w_lo(r))
                        for t in range(at // P, (at + n) // P):
                            if t >= 3:
                                pe.wait_ge(*y_set(r, t - 2))
                            elif k is None or k >= 1:
                                pe.wait_ge(*y_set(r - 1))
                            products(ps[5 + t % 3][:, 0:D], MC, lambda i, m: hid[:, s % 2, i, m, t * P - at:(t + 1) * P - at],
                                     lambda j, m: w2s[:, p, j, m, :]).then_inc(*down.up)

                    s = int(name[-1])
                    if name[0] == "x":
                        pe.wait_ge(*loaded(r))
                        at, n = SPANS[s]
                        for c in range(KC):
                            i = s * KC + c
                            if i >= 2:
                                pe.wait_ge(*x_lo(r, i - 1))
                            elif k is None or k >= 1:
                                pe.wait_ge(*x_lo(r - 1, KC * NS - 1 + i))
                            for t in range(n // P):
                                ins = nc.tensor.transpose(ps[c][:, t * P:(t + 1) * P], xt[:, p, at // P + t, c * P:(c + 1) * P], ident[:])
                            ins.then_inc(*flipped.up)
                    else:
                        upward(s)
                        if s:
                            downward(s - 1)
                        if s == NS - 1:
                            downward(s)

                overlapped(pe, NE, E_ORDER["pe"].split(), step)

            @block.scalar
            def _(act):
                def step(name, r, p, k):
                    if name[0] == "w":
                        act.wait_ge(*loaded(r))
                        if k is None:
                            act.wait_ge(*down(r - 2))
                        parts, whole = (w1s, w1) if name == "w1" else (w2s, w2)
                        nc.scalar.activation(parts[:, p, 0], whole[:, p], ACT.Copy, scale=W_UP).then_inc(*w_hi.up)
                        return
                    s = int(name[-1])
                    at, n = SPANS[s]
                    if name[0] == "x":
                        if k is None:
                            act.wait_ge(*up(r - 2))
                        for c in range(KC):
                            act.wait_ge(*flipped(r, s * KC + c + 1))
                            nc.scalar.activation(xT[:, p, 0, c, at:at + n], ps[c][:, 0:n], ACT.Copy).then_inc(*x_hi.up)
                    else:
                        if s == 0:
                            act.wait_ge(*bias_set(r))
                        for m in range(MC + 1):
                            i = s * MC + m
                            if m < MC:
                                act.wait_ge(*up(r, i + 1))
                                if i >= 3:
                                    act.wait_ge(*hid_lo(r, i - 2))
                                elif k is None or k >= 1:
                                    act.wait_ge(*hid_lo(r - 1))
                                nc.scalar.activation(hid32[:, i % 3, 0:n], ps[2 + i % 3][:, 0:n], ACT.Gelu, bias=b1e[:, m:m + 1],
                                                     scale=1 / W_UP).then_inc(*act_done.up)
                            if m:
                                act.wait_ge(*act_done(r, i))
                                if s >= 2:
                                    act.wait_ge(*down(r, (SPANS[s - 2][0] + SPANS[s - 2][1]) // P))
                                elif k is None or k >= 1:
                                    act.wait_ge(*down(r - 1))
                                nc.scalar.activation(hid[:, s % 2, 0, m - 1, 0:n], hid32[:, (i - 1) % 3, 0:n], ACT.Copy).then_inc(*hid_hi.up)

                overlapped(act, NE, E_ORDER["act"].split(), step)

            @block.vector
            def _(dve):
                V = nc.vector
                dve.wait_ge(*const_in(0))

                def step(name, r, p, k):
                    def outputs(s):
                        at, n = SPANS[s]
                        for t in range(at // P, (at + n) // P):
                            dve.wait_ge(*down(r, t + 1))
                            V.scalar_tensor_tensor(yt[:, p, t, :], ps[5 + t % 3][:, 0:D], 1 / W_UP, b2e[:], ALU.mult, ALU.add).then_inc(*y_set.up)

                    if name[0] == "w":
                        dve.wait_ge(*w_hi(r, int(name[1])))
                        parts, whole = (w1s, w1) if name == "w1" else (w2s, w2)
                        V.scalar_tensor_tensor(parts[:, p, 1], whole[:, p], W_UP, parts[:, p, 0], ALU.mult, ALU.subtract).then_inc(*w_lo.up)
                        return
                    s = int(name[-1])
                    at, n = SPANS[s]
                    if name[0] == "x":
                        for c in range(KC):
                            dve.wait_ge(*x_hi(r, s * KC + c + 1))
                            V.tensor_tensor(xT[:, p, 1, c, at:at + n], ps[c][:, 0:n], xT[:, p, 0, c, at:at + n], ALU.subtract).then_inc(*x_lo.up)
                    else:
                        if s == 0:
                            if k is None or k >= 1:
                                dve.wait_ge(*act_done(r - 1))
                                dve.wait_ge(*y_set(r - 1))
                            V.tensor_copy(b1e[:], b1[:, bass.ds(r.at, 1), :].rearrange("p a m -> p (a m)")).then_inc(*bias_set.up)
                            V.tensor_copy(b2e[:], b2[:, bass.ds(r.at, 1), :].rearrange("p a m -> p (a m)")).then_inc(*bias_set.up)
                        for m in range(MC):
                            i = s * MC + m
                            dve.wait_ge(*hid_hi(r, i + 1))
                            V.tensor_tensor(hid[:, s % 2, 1, m, 0:n], hid32[:, i % 3, 0:n], hid[:, s % 2, 0, m, 0:n], ALU.subtract).then_inc(*hid_lo.up)
                        if s == 1:
                            dve.wait_ge(*bias_set(r))
                            if k is None:
                                dve.wait_ge(*stored(r - 2))
                        if s:
                            outputs(s - 1)
                        if s == NS - 1:
                            outputs(s)

                overlapped(dve, NE, E_ORDER["dve"].split(), step)


class Fills:

    def __init__(self, order, first_bank):
        assert len(order) % 2 == 0
        self.order, self.first = order, first_bank
        self.index = {name: j for j, (name, _) in enumerate(order)}
        self.reader = dict(order)

    def count(self, reader):
        return sum(r == reader for _, r in self.order)

    def bank(self, name):
        return self.first + self.index[name] % 2

    def filled(self, name):
        return self.index[name] + 1

    def read(self, name):
        return sum(r == self.reader[name] for _, r in self.order[:self.index[name] + 1])

    def before(self, name):
        j = self.index[name] - 2
        return self.order[j][0], int(j < 0)


def front_back(eng, count, front, back):
    front(Round(0, 0), 0, None)
    nxt = lambda r, k: (lambda i: front(r, k, i))
    back(Round(0, 0), nxt(Round(0, 1), 1), 0)
    with eng.Fori(0, count // 2 - 1) as i:
        back(Round(i, 1), nxt(Round(i + 1, 0), None), None)
        back(Round(i + 1, 0), nxt(Round(i + 1, 1), None), None)
    back(Round(count // 2 - 1, 1), lambda i: None, count - 1)


ENGINES = ("pe", "act", "dve", "pool", "sp")


def turns(text):
    parts = [p.split(":") for p in text.split(";")]
    return {int(i): names.split() for i, names in parts}


TURNS = {
    True: ({
        "pe": turns("1: gt1; 2: bm0; 5: gt0; 7: bm1"),
        "act": turns("5: gt1; 6: gt0"),
        "dve": turns("4: bm0; 8: bm1"),
    }, {
        "pe": turns("8: hT0 hT1; 10: score; 11: q0 k0; 13: v0; 15: q1 k1; 16: qT0 kT0; 18: sel; 19: v1 q2; 20: xg1; "
                     "21: xg0 k2; 23: aux mq0 mq1; 24: qT1; 25: kT1 v2; 27: q3 k3 mkT mqT; 28: kT2 qT2; 30: ms v3; "
                     "32: qT3 kT3; 33: mpT; 34: am"),
        "act": turns("7: h; 8: hT0 hT1; 10: score; 12: q0 k0; 13: ropeB0; 14: v0; 16: q1 k1 qT0; 17: kT0; 18: sel; "
                     "19: ropeB1 v1; 20: q2; 21: xg1 xg0; 22: k2; 23: aux mq0; 24: mq1 ropeB2; 25: qT1 mrope kT1; "
                     "27: v2 q3 k3 mkT mqT; 29: kT2 qT2 ropeB3; 30: ms; 31: v3; 33: qT3 kT3 mpT; 34: am"),
        "dve": turns("4: x1b lnA; 6: lnB lnC; 7: lnD; 10: top0 top1; 11: top2; 12: ropeA0 top3; 13: ropeB0 top4; "
                     "14: v0 top5; 15: top6; 16: top7; 17: ropeA1; 18: rank0 rank1 rank2 sel; 19: ropeB1 G0 G1 G2 G3 v1; "
                     "21: xg1 xg0; 23: aux ropeA2 ropeB2; 25: mrope mlow; 27: v2; 28: ropeA3 ropeB3; 30: ms; 31: v3; "
                     "33: mpT; 34: am"),
        "pool": turns("1: x; 3: x1 h; 12: ropeA0; 13: ropeB0; 17: ropeA1; 20: ropeB1; 22: ropeA2; 24: ropeB2; 30: ropeA3; "
                     "31: ropeB3"),
        "sp": turns("1: x; 30: swap"),
    }),
    False: ({
        "pe": turns("2: bm0; 3: bm1; 4: gt1; 5: gt0"),
        "act": turns("5: gt1 gt0"),
        "dve": turns("2: bm0; 4: bm1"),
    }, {
        "pe": turns("6: bT0 bT1; 7: bw0 bw1; 8: bss; 11: bdot; 12: oT0 oT1; 13: bo0 bo1; 16: hT0 hT1; 17: score; "
                     "18: q0 k0; 19: v0; 20: q1; 21: k1; 22: sel; 23: qT0; 24: kT0; 25: xg1 xg0 q2; 26: k2 aux v1; "
                     "27: mq0 mq1; 28: kT1; 29: qT1 q3 k3; 30: mqT mkT; 31: ms v2; 32: mpT v3 kT2; 34: qT2 am; 35: qT3 kT3"),
        "act": turns("4: bh; 6: bT0 bT1; 7: bw0 bw1; 9: bexp; 12: oT0 oT1; 14: h; 16: hT0 hT1; 17: score; 19: q0 k0; "
                     "20: v0; 22: ropeB0 q1 k1 sel; 24: qT0 ropeB1; 25: kT0 xg1 xg0 q2; 26: k2 aux v1; "
                     "28: mq0 ropeB2 mq1; 29: kT1 qT1 mrope; 30: q3 k3 mqT mkT; 31: ms; 32: v2 mpT v3; 33: ropeB3 kT2; "
                     "35: qT2 am qT3 kT3"),
        "dve": turns("0: b_lnA; 1: b_lnB; 2: b_lnC; 3: b_lnD; 8: bss bnorm blog; 10: bpi bpiw; 11: bdot res resw; "
                     "12: oT0 oT1; 13: bo0 bo1 lnA; 14: lnB lnC; 15: lnD; 17: top0; 18: top1; 19: top3 top2 ropeA0; "
                     "20: v0 top4; 21: top7 top6; 22: ropeB0 top5 rank0 rank1 rank2 sel G0 G1 G3; 23: G2; "
                     "24: ropeA1 ropeB1; 25: xg1 xg0; 26: aux v1; 27: ropeA2; 28: ropeB2; 29: mrope mlow; 31: ropeA3; "
                     "32: ms v2 mpT; 33: ropeB3 v3; 35: am"),
        "pool": turns("3: bh; 8: wpi; 17: h; 20: ropeA0; 21: ropeB0; 23: ropeA1; 25: ropeB1; 27: ropeA2 ropeB2; "
                     "31: ropeA3 ropeB3"),
        "sp": turns("1: x; 27: swap"),
    }),
}


def mixing_weights(nc, ctx):
    HW = NH * HP
    shapes = {"dwqkv": [P, 2, KC, 3 * HW], "mwqkv": [P, 2, KC, 3 * HW], "dwo": [P, 2, PAIRS, D], "mwo": [P, 2, PAIRS, D],
              "mrw": [P, 2, KC, NH]}
    return {name: ctx.enter_context(nc.sbuf_tensor("m_" + name, shape, F16)) for name, shape in shapes.items()}


def mixing_stage(nc, a, first):
    with ExitStack() as ctx:
        pre = "m1_" if first else "m2_"
        sb = lambda name, shape, dt=F32: ctx.enter_context(nc.sbuf_tensor(pre + name, shape, dt))
        sig = lambda name, per=1, by=1: Sig(ctx, nc, pre + name, per, by)
        two = lambda name, per=1: TwoSig(ctx, nc, pre + name, per)
        ps = [ctx.enter_context(nc.psum_tensor(f"{pre}ps{i}", [P, 512], F32)) for i in range(8)]
        ps16 = [b[:].bitcast(F16) for b in ps]
        HW = NH * HP
        SCALE = HP ** -0.5
        HALF = ROT // 2
        TW = ROT + NH
        ident = sb("ident", [P, P])
        ident16 = sb("ident16", [P, P], F16)
        causal = sb("causal", [P, P], BF16)
        causal2 = sb("causal2", [P, P], BF16)
        identb = sb("identb", [P, P], BF16)
        slot1 = sb("slot1", [P, SLOTS])
        onesf = sb("onesf", [P, P])
        cosd = sb("cosd", [P, TILES, ROT])
        sind = sb("sind", [P, TILES, ROT])
        dwqkv, mwqkv, dwo, mwo, mrw = (a["mixing"][n] for n in ("dwqkv", "mwqkv", "dwo", "mwo", "mrw"))
        mrw32 = sb("mrw32", [P, KC, NH])
        tb32 = sb("tb32", [P, TILES, ROT])
        x = sb("x", [P, 2, TILES, D])
        xo = sb("xo", [P, TILES, D])
        stats = sb("stats", [P, TILES, 6])
        mv = sb("mv", [P, TILES, 2])
        ve = sb("ve", [P, TILES])
        rs = sb("rs", [P, TILES])
        rt = sb("rt", [P, TILES])
        h = sb("h", [P, 2, TILES, D], F16)
        hT = sb("hT", [P, KC, 2, NT], F16)
        raw = sb("raw", [P, 2 * HW])
        ra = sb("ra", [P, 2 * NH, ROT])
        rc = sb("rc", [P, 2 * NH, ROT])
        qk2 = sb("qk2", [P, 2, 2 * NH, 2, HP], F16)
        v = sb("v", [P, 2, 2, TILES, HW], F16)
        qkT = sb("qkT", [P, 2, 2, NH, NT], F16)
        kS = sb("kS", [P, 2, NH, NT], F16)
        nmax = sb("nmax", [P, 4])
        rsum = sb("rsum", [P, TILES * NH])
        rinv = sb("rinv", [P, NH])
        prob = sb("prob", [P, 2, NT])
        pT = sb("pT", [P, 3, 2, NT], F16)
        av32 = sb("av32", [P, HW])
        av = sb("av", [P, 2, HW], F16)
        avT = sb("avT", [P, 2, PAIRS, P], F16)
        scT = sb("scT", [NH, NT])
        wk = sb("wk", [NH, NT])
        m8 = sb("m8", [NH, 8])
        selT = sb("selT", [NH, NT])
        sel = sb("sel", [P, TILES, NH])
        tb = sb("tb", [P, TILES, 2, TW], F16)
        G = sb("G", [P, TILES, NH * SLOTS], F16)
        GT = sb("GT", [P, PAIRS, NT], F16)
        xgT = sb("xgT", [P, KC, 2, NH * SLOTS], F16)
        aux = sb("aux", [P, PAIRS * TW])
        gsc = sb("gsc", [P, PAIRS])
        gex = sb("gex", [P, PAIRS])
        gr = sb("gr", [P, PAIRS])
        r4 = sb("r4", [P, 4, PAIRS, 2, HALF])
        big = sb("big", [P, 5 * 256])
        h32 = big[:, 0:TILES * D].rearrange("p (t n) -> p t n", n=D)
        mq = big[:, 0:PAIRS * 192].rearrange("p (m n) -> p m n", n=192)
        mp = big[:, PAIRS * 192:PAIRS * (192 + P)].rearrange("p (m n) -> p m n", n=P)
        mq2 = sb("mq2", [P, 2, PAIRS, 192], F16)
        PW = D + HB
        mqTb = sb("mqT", [P, TILES * PW])
        mqT = mqTb[0:HP, 0:1024].bitcast(F16).rearrange("p (j s n) -> p j s n", j=2, s=2)
        mmax = sb("mmax", [P, PAIRS])
        msum = sb("msum", [P, PAIRS])
        mpT = sb("mpT", [P, 2, PAIRS, P], F16)
        am = sb("am", [P, 2, PAIRS * SLOTS], F16)
        bm = sb("bm", [P, 2, PAIRS, D], F16)
        if first:
            idx = sb("idx", [P, TILES * TOPK], U32)
            gcur = sb("gcur", [P, TILES * TOPK])
            gy = sb("gy", [P, TILES, TOPK, D])
        else:
            bw = sb("bw", [P, 2, KC, D], F16)
            bwout = sb("bwout", [P, 2, KC, D], F16)
            btemp = sb("btemp", [P, HB])
            bbout = sb("bbout", [P, D])
            w = xgT[:].rearrange("p c s n -> p (c s n)").bitcast(F32).rearrange("p (t n) -> p t n", n=D)
            w2 = G[:].rearrange("p t n -> p (t n)").bitcast(F32).rearrange("p (t n) -> p t n", n=D)
            pw = mqTb[:].rearrange("p (t n) -> p t n", n=PW)
            x2 = sb("x2", [P, TILES, D])
            inv = sb("inv", [P, D])
            attn = inv
            bl = sb("bl", [P, TILES, HB])
            bmx = sb("bmx", [P, TILES])
            bsm = sb("bsm", [P, TILES])
            bden = sb("bden", [P, HB])
            dot = r4[:].rearrange("p j m s n -> p (j m s n)")[:, 0:PW]

        st = qkT[:].rearrange("p r j n t -> p (r j n t)").bitcast(F32)
        st2 = kS[:].rearrange("p r n t -> p (r n t)").bitcast(F32)
        chunked = [(st[:, 0:KC * 3 * HW], "dwqkv", dwqkv, 3 * HW), (st[:, 4096:4096 + KC * 3 * HW], "mwqkv", mwqkv, 3 * HW),
                   (st2[:, 0:PAIRS * D], "dwo", dwo, D), (st2[:, PAIRS * D:2 * PAIRS * D], "mwo", mwo, D),
                   (mrw32[:].rearrange("p k n -> p (k n)"), "mrw", mrw, NH)]
        consts = [(ident, "ident"), (ident16, "ident16"), (identb, "identb"), (causal, "causal"), (causal2, "causal_pair"),
                  (slot1, "slot1"), (cosd, "cosd"), (sind, "sind"), (tb32, "rope_rows")]
        if not first:
            consts += [(btemp, "btemp"), (bbout, "bbout")]
            chunked = [(st2[:, 2048:2048 + KC * D], "bw", bw, D), (st2[:, 2560:2560 + KC * D], "bwout", bwout, D)]

        NI = TILES * NH
        AV_LAG = 3
        SLOT_N = NI + AV_LAG + 1
        QORDER = [3, 2, 1, 0]
        item = lambda i: (QORDER[i // NH], i % NH)

        def due(i, k):
            late = [(TILES - 1, part, 1) for part in (1, 2) if i == part and not k == 0]
            return late + [(g, part, 0) for g in range(TILES) for part, after in enumerate((0, 2, 3))
                           if i == (g + 1) * NH + AV_LAG - 1 + after]

        own, ahead = TURNS[first]
        own = {e: dict(own.get(e, {})) for e in ENGINES}
        ahead = {e: dict(ahead.get(e, {})) for e in ENGINES}
        names = lambda *ps, n: {f"{p}{i}" for p in ps for i in range(n)}
        by_scalar = {"score", "ms", "mqT", "mkT"} | names("hT", "bT", "bw", "mq", "gt", n=2) | names("q", "k", "qT", "kT", n=TILES)
        in_order = lambda turns: [s for i in sorted(turns) for s in turns[i]]
        fills = in_order(ahead["pe"]) + in_order(own["pe"])
        fl = Fills([(s, "act" if s in by_scalar else "dve") for s in fills], 6)
        order = fl.order
        for e in ("act", "dve"):
            mine = [s for s in in_order(ahead[e]) + in_order(own[e]) if s in fl.index]
            assert mine == [s for s in fills if s in mine], (e, mine)
        for e in ENGINES:
            assert not own[e] or max(own[e]) < min([i for i in ahead[e] for s in ahead[e][i] if s in fl.index] + [SLOT_N]), e
            assert max(ahead[e]) < SLOT_N

        const_in = sig("const_in", len(consts) + len(chunked), 16)
        ones_set = sig("ones_set")
        split = sig("split", 2 * len(chunked) + (6 if first else 3))
        filled = sig("filled", len(order))
        read = {"act": sig("read_by_scalar", fl.count("act")), "dve": sig("read_by_vector", fl.count("dve"))}
        hi = sig("hi", TILES + 1 + 5 + (4 if not first else 0))
        HI = ([] if first else ["bw0", "bw1", "oT0", "oT1"]) + [f"v{t}" for t in range(TILES)] + ["sel", "xg0", "xg1", "mpT", "am"]
        HN, count = {}, 0
        for s in in_order(ahead["act"]):
            if s in HI:
                count += 2 if s == "sel" else 1
                HN[s] = count
        assert count == hi.per, (count, hi.per)
        x_in = two("x_in")
        x_part = sig("x_part", 2)
        x_made = sig("x_made")
        x_ready = lambda r: x_made(r) if first else read["dve"](r, fl.read("bo1"))
        out_made = sig("out_made", TILES)
        out_done = sig("out_done", 1, 16)
        ln = sig("ln", 2 * TILES + 1 + RSQRT_STEPS + TILES)
        h_hi = sig("h_hi")
        h_lo = sig("h_lo")
        pick = sig("pick", 16 + 3)
        rope_a = sig("rope_a", TILES)
        rope_b = sig("rope_b", TILES)
        rope = sig("rope", TILES)
        qk_hi = sig("qk_hi", TILES)
        qk_lo = sig("qk_lo", TILES)
        swapped = sig("swapped", 2, 16)
        g_set = sig("g_set", TILES)
        aux_hi = sig("aux_hi")
        aux_step = sig("aux_step", 2)
        gate_exp = sig("gate_exp")
        mrope = sig("mrope", 6)
        mq_hi = sig("mq_hi")
        mq_lo = sig("mq_lo")
        m_max = sig("m_max")
        m_exp = sig("m_exp", PAIRS - 1)
        bm_step = sig("bm_step", 3 + 6)
        s_ps = sig("s_ps", TILES * NH)
        s_max = sig("s_max", TILES * NH)
        s_exp = sig("s_exp", TILES * NH)
        p_flip = sig("p_flip", TILES * NH)
        p_hi = sig("p_hi", TILES * NH)
        p_lo = sig("p_lo", TILES * NH)
        av_ps = sig("av_ps", TILES * NH)
        av_set = sig("av_set", 2 * TILES)
        av_lo = sig("av_lo", TILES)
        av_hi = sig("av_hi", TILES)
        av_flip = sig("av_flip", TILES)
        avT_set = sig("avT_set", TILES)
        o_ps = sig("o_ps", TILES)
        if first:
            idx_set = sig("idx_set", 2)
            gathered = Sig(a["lasting"], nc, pre + "gathered", TILES * TOPK, 16)
        else:
            b_ln = sig("b_ln", 2 * TILES + 1 + RSQRT_STEPS + TILES)
            bh_hi = sig("bh_hi")
            bh_lo = sig("bh_lo")
            xb_set = sig("xb_set")
            pi = sig("pi", 10)
            pi_exp = sig("pi_exp")
            res = sig("res", 6)
            w_pi = sig("w_pi")

        with nc.Block() as block:

            def run_front(step, slots):
                def front(r, k, i):
                    for s in ([s for j in sorted(slots) for s in slots[j]] if i is None else slots.get(i, ())):
                        step(r, r.parity, k, s)
                return front

            @block.sync
            def _(sp):
                for to, name in consts:
                    sp.dma_start(to[:], a[name]).then_inc(*const_in.up)
                for to, name, _, n in chunked:
                    sp.dma_start(to.rearrange("p (k n) -> p k n", n=n), a[name].rearrange("(k p) n -> p k n", p=P)).then_inc(*const_in.up)
                sp.wait_ge(*split(0))

                def step(r, p, k, s):
                    if s == "x":
                        if first:
                            if k is None or k >= 1:
                                sp.wait_ge(*filled(r - 1, fl.filled("mpT")))
                            sp.dma_start(h32, a["resid"][r.at].rearrange("(t p) n -> p t n", p=P)).then_inc(*x_in.up(r))
                        else:
                            if k is None or k >= 1:
                                sp.wait_ge(*x_ready(r - 1))
                            sp.dma_start(x2[:], a["mid"][r.at].rearrange("(t p) n -> p t n", p=P)).then_inc(*x_in.up(r))
                    elif s == "swap":
                        sp.wait_ge(*read["act"](r, fl.read(f"kT{TILES - 1}")))
                        if k is None:
                            sp.wait_ge(*s_ps(r - 2))
                        sp.dma_start(kS[0:HP, p], qkT[HP:P, p, 1]).then_inc(*swapped.up)
                        sp.dma_start(kS[HP:P, p], qkT[0:HP, p, 1]).then_inc(*swapped.up)

                def back(r, side, k):
                    for i in range(SLOT_N):
                        side(i)
                        if i == 3 and not k == 0:
                            end(r - 1)

                def end(r):
                    sp.wait_ge(*out_made(r))
                    sp.dma_start(a["mid" if first else "out"][r.at].rearrange("(t p) n -> p t n", p=P), xo[:]).then_inc(*out_done.up)

                front_back(sp, NB, run_front(step, ahead["sp"]), back)
                end(Round(NB // 2 - 1, 1))
                sp.wait_ge(*out_done(NB - 1))

            @block.gpsimd
            def _(pool):
                nc.gpsimd.memset(onesf[:], 1.0).then_inc(*ones_set.up)
                pool.wait_ge(*const_in(0))

                def step(r, p, k, s):
                    if s == "x" and first:
                        if k is None or k >= 1:
                            pool.wait_ge(*x_made(r - 1))
                            pool.wait_ge(*gathered(r - 1))
                        cols = bass.ds(r.at * TILES * TOPK, TILES * TOPK)
                        nc.gpsimd.tensor_copy(idx[:], a["slot_of"][:, cols]).then_inc(*idx_set.up)
                        nc.gpsimd.tensor_copy(gcur[:], a["gate_of"][:, cols]).then_inc(*idx_set.up)
                        pool.wait_ge(*idx_set(r))
                        settle(pool)
                        for t in range(TILES):
                            for c in range(TOPK):
                                pool.indirect_dma_start(gy[:, t, c, :], None, a["expert_out"],
                                                        bass.IndirectOffsetOnAxis(ap=idx[:, t * TOPK + c:t * TOPK + c + 1], axis=0),
                                                        bounds_check=NE * CAP - 1, oob_is_err=False).then_inc(*gathered.up)
                    elif s == "x1":
                        c_ = Chain(pool, x_part, r)
                        pool.wait_ge(*gathered(r))
                        c_.link(nc.gpsimd.tensor_tensor(gy[:], gy[:], over(gcur[:], [TOPK, TILES], [1, TOPK], [0, D]), ALU.mult))
                        pool.wait_ge(*x_in(r))
                        if k is None:
                            pool.wait_ge(*out_made(r - 2))
                        c_.inc(nc.gpsimd.tensor_tensor(x[:, p], gy[:, :, 0, :], h32, ALU.add))
                        c_.end()
                    elif s == "wpi":
                        pool.wait_ge(*pi(r, 9))
                        ww = w.rearrange("p t (h d) -> p t h d", d=DB)
                        nc.gpsimd.tensor_tensor(ww, ww, over(pw[:, 0, D:], [PW, TILES], [1, HB], [0, DB]), ALU.mult).then_inc(*w_pi.up)
                    elif s in ("h", "bh"):
                        pool.wait_ge(*(h_hi if s == "h" else bh_hi)(r))
                        nc.gpsimd.tensor_tensor(h[:, 1], h32, h[:, 0], ALU.subtract).then_inc(*(h_lo if s == "h" else bh_lo).up)
                    if s == "bh":
                        nc.gpsimd.tensor_tensor(x2[:], x2[:], over(bbout[:], [0, TILES], [1, D]), ALU.add).then_inc(*xb_set.up)
                    elif s[:5] == "ropeA":
                        t = int(s[5:])
                        pool.wait_ge(*read["act"](r, fl.read(f"k{t}")))
                        if t:
                            pool.wait_ge(*rope(r, t))
                        elif k is None or k >= 1:
                            pool.wait_ge(*rope(r - 1))
                        x2d = raw[:].rearrange("p (h d) -> p h d", d=HP)[:, :, 0:ROT]
                        nc.gpsimd.tensor_tensor(rc[:].rearrange("p h (s d) -> p h s d", s=2), x2d.rearrange("p h (s d) -> p h s d", s=2)[:, :, ::-1, :],
                                                over(sind[:, t, :], [0, 2 * NH], [HALF, 2], [1, HALF]), ALU.mult).then_inc(*rope_b.up)
                    elif s[:5] == "ropeB":
                        t = int(s[5:])
                        pool.wait_ge(*qk_hi(r, t + 1))
                        nc.gpsimd.tensor_tensor(qk2[:, t % 2, :, 1, :], raw[:].rearrange("p (h d) -> p h d", d=HP), qk2[:, t % 2, :, 0, :],
                                                ALU.subtract).then_inc(*qk_lo.up)

                def end(r, g, part, k):
                    if part == 0:
                        pool.wait_ge(*av_hi(r, g + 1))
                        nc.gpsimd.tensor_tensor(av[:, 1], av32[:], av[:, 0], ALU.subtract).then_inc(*av_lo.up)

                def back(r, side, k):
                    for i in range(SLOT_N):
                        for g, part, ago in due(i, k):
                            end(r - ago, g, part, k)
                        side(i)

                front_back(pool, NB, run_front(step, ahead["pool"]), back)
                end(Round(NB // 2 - 1, 1), TILES - 1, 1, None)
                end(Round(NB // 2 - 1, 1), TILES - 1, 2, None)

            @block.tensor
            def _(pe):
                pe.wait_ge(*const_in(0))
                pe.wait_ge(*ones_set(0))
                pe.wait_ge(*split(0))

                def begin(r, k, name, after=None):
                    was, ago = fl.before(name)
                    eng = fl.reader[was]
                    if after and fl.reader[after] == eng:
                        if ago or fl.index[after] > fl.index[was]:
                            was, ago = after, 0
                    elif after:
                        pe.wait_ge(*read[fl.reader[after]](r, fl.read(after)))
                    if not (ago and k == 0):
                        pe.wait_ge(*read[eng](r - ago, fl.read(was)))
                    return fl.bank(name)

                def products(to, pairs):
                    for n, (l, m) in enumerate(pairs):
                        ins = nc.tensor.matmul(to, l, m, start=n == 0, stop=n == len(pairs) - 1)
                    return ins

                parts = lambda l, m: [(l(i), m(j)) for i, j in ((0, 0), (0, 1), (1, 0))]

                def step(r, p, k, s):
                    if s not in fl.index:
                        return
                    if s in ("hT0", "hT1", "bT0", "bT1"):
                        c = int(s[2])
                        if c == 0:
                            pe.wait_ge(*(h_lo if s[0] == "h" else bh_lo)(r))
                        b = begin(r, k, s)
                        for j in range(2):
                            for t in range(TILES):
                                ins = nc.tensor.transpose(ps16[b][:, (j * TILES + t) * P:(j * TILES + t + 1) * P], h[:, j, t, c * P:(c + 1) * P], ident16[:])
                    elif s == "score":
                        b = begin(r, k, s, after="hT1")
                        ins = products(ps[b][0:NH, :], [q for c in range(KC) for q in parts(lambda i: mrw[:, i, c, :], lambda j: hT[:, c, j, :])])
                    elif s[0] in "qkv" and len(s) == 2:
                        t, j = int(s[1]), "qkv".index(s[0])
                        b = begin(r, k, s)
                        ins = products(ps[b][:], [q for c in range(KC) for q in parts(
                            lambda i: hT[:, c, i, t * P:(t + 1) * P], lambda i: dwqkv[:, i, c, j * HW:(j + 1) * HW])])
                    elif s[0:2] in ("qT", "kT"):
                        t, j = int(s[2]), "qk".index(s[0])
                        pe.wait_ge(*qk_lo(r, t + 1))
                        b = begin(r, k, s)
                        for n in range(NH):
                            ins = nc.tensor.transpose(ps16[b][:, n * P:(n + 1) * P], qk2[:, t % 2, j * NH + n].rearrange("p s d -> p (s d)"), ident16[:])
                    elif s == "sel":
                        pe.wait_ge(*pick(r))
                        b = begin(r, k, s)
                        settle(pe)
                        for j, src in enumerate((selT, scT)):
                            for t in range(TILES):
                                ins = nc.tensor.transpose(ps[b][:, (j * TILES + t) * NH:(j * TILES + t + 1) * NH],
                                                          src[:, t * P:(t + 1) * P], ident[0:NH, 0:NH])
                    elif s[:2] == "xg":
                        c = int(s[2])
                        pe.wait_ge(*g_set(r))
                        b = begin(r, k, s)
                        ins = products(ps[b][:], [(h[:, i, t, c * P:(c + 1) * P], G[:, t, :]) for t in range(TILES) for i in range(2)])
                    elif s == "aux":
                        b = begin(r, k, s, after="sel")
                        for m in range(PAIRS):
                            ins = products(ps[b][:, m * 2 * TW:(m + 1) * 2 * TW],
                                           [(G[:, t, m * P:(m + 1) * P], tb[:, t].rearrange("p s n -> p (s n)")) for t in range(TILES)])
                    elif s[:2] == "mq" and s != "mqT":
                        g = int(s[2])
                        b = begin(r, k, s, after="xg1")
                        for n in range(4 * g, 4 * g + 4):
                            q, m = n % 2 * SLOTS, n // 2 % 2
                            ins = products(ps[b][q:q + SLOTS, m * 192:(m + 1) * 192], [z for c in range(KC) for z in parts(
                                lambda i: xgT[:, c, i, n * SLOTS:(n + 1) * SLOTS], lambda i: mwqkv[:, i, c, n * 192:(n + 1) * 192])])
                    elif s in ("mqT", "mkT"):
                        j = "qk".index(s[1])
                        pe.wait_ge(*mq_lo(r))
                        b = begin(r, k, s)
                        settle(pe)
                        for i in range(2):
                            for m in range(PAIRS):
                                ins = nc.tensor.transpose(ps16[b][0:HP, (i * PAIRS + m) * P:(i * PAIRS + m + 1) * P], mq2[:, i, m, j * HP:(j + 1) * HP], ident16[:])
                    elif s == "ms":
                        b = begin(r, k, s, after="mkT")
                        for m in range(PAIRS):
                            cols = slice(m * P, (m + 1) * P)
                            ins = products(ps[b][:, cols], parts(lambda i: mqT[:, 0, i, cols], lambda i: mqT[:, 1, i, cols]) + [(identb[:], causal2[:])])
                    elif s == "mpT":
                        b = begin(r, k, s, after="ms")
                        for m in range(PAIRS):
                            ins = nc.tensor.transpose(ps[b][:, m * P:(m + 1) * P], mp[:, m, :], ident[:])
                    elif s == "am":
                        b = begin(r, k, s, after="mpT")
                        for n in range(NH):
                            q, m = n % 2 * SLOTS, n // 2
                            ins = products(ps[b][q:q + HP, m * SLOTS:(m + 1) * SLOTS],
                                           parts(lambda i: mq2[:, i, m, 2 * HP:3 * HP], lambda i: mpT[:, i, m, q:q + SLOTS]))
                    elif s[:2] == "bm":
                        g = int(s[2])
                        b = begin(r, k, s, after="am")
                        settle(pe)
                        for n in range(4 * g, 4 * g + 4):
                            q, m = n % 2 * SLOTS, n // 2
                            ins = products(ps[b][q:q + SLOTS, m % 2 * D:(m % 2 + 1) * D],
                                           parts(lambda i: am[q:q + HP, i, m * SLOTS:(m + 1) * SLOTS], lambda i: mwo[q:q + HP, i, m, :]))
                    elif s[:2] == "gt":
                        g = int(s[2])
                        b = begin(r, k, s)
                        for m in range(2):
                            for t in range(TILES):
                                ins = nc.tensor.transpose(ps16[b][:, (m * TILES + t) * P:(m * TILES + t + 1) * P],
                                                          G[:, t, (2 * g + m) * P:(2 * g + m + 1) * P], ident16[:])
                    elif s in ("bw0", "bw1"):
                        g = int(s[2])
                        b = begin(r, k, s, after="bT1")
                        for t in (2 * g, 2 * g + 1):
                            ins = products(ps[b][:, t % 2 * D:(t % 2 + 1) * D], [z for c in range(KC) for z in parts(
                                lambda i: hT[:, c, i, t * P:(t + 1) * P], lambda i: bw[:, i, c, :])])
                    elif s == "bss":
                        b = begin(r, k, s, after="bw1")
                        ins = products(ps[b][:, 0:D], [(onesf[:], w2[:, t, :]) for t in range(TILES)])
                    elif s == "bdot":
                        pe.wait_ge(*pi(r))
                        b = begin(r, k, s)
                        ins = products(ps[b][:, 0:PW], [(onesf[:], pw[:, t, :]) for t in range(TILES)])
                    elif s in ("oT0", "oT1"):
                        c = int(s[2])
                        pe.wait_ge(*res(r))
                        b = begin(r, k, s)
                        for t in range(TILES):
                            ins = nc.tensor.transpose(ps[b][:, t * P:(t + 1) * P], w[:, t, c * P:(c + 1) * P], ident[:])
                    elif s in ("bo0", "bo1"):
                        g = int(s[2])
                        b = begin(r, k, s, after="oT1")
                        for t in (2 * g, 2 * g + 1):
                            ins = products(ps[b][:, t % 2 * D:(t % 2 + 1) * D], [z for c in range(KC) for z in parts(
                                lambda i: hT[:, c, i, t * P:(t + 1) * P], lambda i: bwout[:, i, c, :])])
                    ins.then_inc(*filled.up)

                def end(r, g, part, k):
                    if part == 1:
                        pe.wait_ge(*av_lo(r, g + 1))
                        if g:
                            pe.wait_ge(*out_made(r, g))
                        elif k is None or k >= 1:
                            pe.wait_ge(*out_made(r - 1))
                        for s_ in range(2):
                            for m in range(PAIRS):
                                ins = nc.tensor.transpose(ps16[5][:, (s_ * PAIRS + m) * P:(s_ * PAIRS + m + 1) * P], av[:, s_, m * P:(m + 1) * P], ident16[:])
                        ins.then_inc(*av_flip.up)
                    elif part == 2:
                        qt = QORDER[g]
                        pe.wait_ge(*read["act"](r, max(fl.read("gt0"), fl.read("gt1"))))
                        pe.wait_ge(*read["dve"](r, max(fl.read("bm0"), fl.read("bm1"))))
                        pe.wait_ge(*avT_set(r, g + 1))
                        ins = products(ps[5][:, 0:D], [(GT[:, m, qt * P:(qt + 1) * P], bm[:, i_, m, :]) for m in range(PAIRS) for i_ in range(2)]
                                       + [z for m in range(PAIRS) for z in parts(lambda i_: avT[:, i_, m, :], lambda i_: dwo[:, i_, m, :])])
                        ins.then_inc(*o_ps.up)

                def scores(r, k, i):
                    qt, n = item(i)
                    nk = (qt + 1) * P
                    if i >= 2:
                        pe.wait_ge(*s_exp(r, i - 1))
                    elif k is None or k >= 1:
                        pe.wait_ge(*s_exp(r - 1))
                    p, to = r.parity, ps[i % 2]
                    qs = qkT[:, p, 0, n, qt * P:(qt + 1) * P]
                    nc.tensor.matmul(to[:, 0:nk], qs, qkT[:, p, 1, n, 0:nk], start=True, stop=False)
                    nc.tensor.matmul(to[:, 0:nk], qs, kS[:, p, n, 0:nk], start=False, stop=False)
                    nc.tensor.matmul(to[:, nk - P:nk], identb[:], causal[:], start=False, stop=True).then_inc(*s_ps.up)

                def back(r, side, k):
                    p = r.parity
                    pe.wait_ge(*swapped(r))
                    pe.wait_ge(*read["act"](r, fl.read(f"kT{TILES - 1}")))
                    pe.wait_ge(*read["dve"](r, fl.read(f"v{TILES - 1}")))
                    scores(r, k, 0)
                    for i in range(SLOT_N):
                        if 1 <= i <= NI:
                            j = i - 1
                            qt, n = item(j)
                            pe.wait_ge(*s_exp(r, j + 1))
                            if j >= 2:
                                pe.wait_ge(*p_lo(r, j - 1))
                            elif k is None or k >= 1:
                                pe.wait_ge(*p_lo(r - 1))
                            for c in range(qt + 1):
                                ins = nc.tensor.transpose(ps[2 + j % 2][:, c * P:(c + 1) * P], prob[:, j % 2, c * P:(c + 1) * P], ident[:])
                            ins.then_inc(*p_flip.up)
                        if AV_LAG <= i < NI + AV_LAG:
                            j = i - AV_LAG
                            qt, n = item(j)
                            pe.wait_ge(*p_lo(r, j + 1))
                            if n == 0 and j:
                                pe.wait_ge(*av_set(r, 2 * (j // NH)))
                            elif n == 0 and (k is None or k >= 1):
                                pe.wait_ge(*av_set(r - 1, 2 * TILES))
                            ins = products(ps[4][:, n * HP:(n + 1) * HP], [z for c in range(qt + 1) for z in parts(
                                lambda i_: pT[:, j % 3, i_, c * P:(c + 1) * P], lambda i_: v[:, p, i_, c, n * HP:(n + 1) * HP])])
                            ins.then_inc(*av_ps.up)
                        if i + 1 < NI:
                            scores(r, k, i + 1)
                        for g, part, ago in due(i, k):
                            end(r - ago, g, part, k)
                        for s in own["pe"].get(i, ()):
                            step(r, p, k, s)
                        side(i)

                front_back(pe, NB, run_front(step, ahead["pe"]), back)
                end(Round(NB // 2 - 1, 1), TILES - 1, 1, None)
                end(Round(NB // 2 - 1, 1), TILES - 1, 2, None)

            @block.scalar
            def _(act):
                def copy(dst, src, up, scale=1.0):
                    nc.scalar.activation(dst, src, ACT.Copy, scale=scale).then_inc(*up.up)

                def step(r, p, k, s):
                    if s in by_scalar or s in HI:
                        act.wait_ge(*filled(r, fl.filled(s)))
                        b = fl.bank(s)
                    last = read["act"]
                    if s in ("h", "bh"):
                        act.wait_ge(*(ln if s == "h" else b_ln)(r))
                        if s == "h" and not first:
                            act.wait_ge(*filled(r, max(fl.filled("bT0"), fl.filled("bT1"))))
                        elif k is None or k >= 1:
                            act.wait_ge(*filled(r - 1, max(fl.filled(f) for f in ("xg0", "xg1", "hT0", "hT1"))))
                        copy(h[:, 0], h32, h_hi if s == "h" else bh_hi)
                    elif s in ("hT0", "hT1", "bT0", "bT1"):
                        copy(hT[:, int(s[2])], ps16[b].rearrange("p (s n) -> p s n", s=2), last)
                    elif s == "score":
                        if k is None or k >= 1:
                            act.wait_ge(*pick(r - 1))
                        copy(scT[:], ps[b][0:NH, :], last, 1 / W_UP)
                    elif s[0] in "qk" and len(s) == 2:
                        t, j = int(s[1]), "qk".index(s[0])
                        if t:
                            act.wait_ge(*qk_lo(r, t))
                        elif k is None or k >= 1:
                            act.wait_ge(*qk_lo(r - 1))
                        copy(raw[:, j * HW:(j + 1) * HW], ps[b][:], last, 1 / W_UP)
                    elif s[0] == "v":
                        if k is None:
                            act.wait_ge(*av_ps(r - 2))
                        copy(v[:, p, 0, int(s[1]), :], ps[b][:], hi, 1 / W_UP)
                    elif s[:5] == "ropeB":
                        t = int(s[5:])
                        act.wait_ge(*rope(r, t + 1))
                        if t >= 2:
                            act.wait_ge(*filled(r, fl.filled(f"kT{t - 2}")))
                        elif k is None or k >= 1:
                            act.wait_ge(*filled(r - 1, fl.filled(f"kT{TILES - 2 + t}")))
                        copy(qk2[:, t % 2, :, 0, :], raw[:].rearrange("p (h d) -> p h d", d=HP), qk_hi)
                    elif s[0:2] in ("qT", "kT"):
                        t, j = int(s[2]), "qk".index(s[0])
                        if k is None:
                            act.wait_ge(*s_ps(r - 2))
                        copy(qkT[:, p, j, :, t * P:(t + 1) * P], ps16[b].rearrange("p (n q) -> p n q", n=NH), last)
                    elif s == "sel":
                        n4 = TILES * NH
                        if k is None or k >= 1:
                            act.wait_ge(*g_set(r - 1))
                        copy(sel[:], ps[b][:, 0:n4].rearrange("p (t n) -> p t n", n=NH), hi)
                        copy(tb[:, :, 0, ROT:], ps[b][:, n4:2 * n4].rearrange("p (t n) -> p t n", n=NH), hi)
                    elif s in ("xg0", "xg1"):
                        copy(xgT[:, int(s[2]), 0, :], ps[b][:], hi)
                    elif s == "aux":
                        act.wait_ge(*aux_step(r))
                        if k is None or k >= 1:
                            act.wait_ge(*bm_step(r - 1, 1))
                        nc.scalar.activation(gex[:], gsc[:], ACT.Exp).then_inc(*gate_exp.up)
                    elif s in ("mq0", "mq1"):
                        g = int(s[2])
                        copy(mq[:, 2 * g:2 * g + 2, :], ps[b][:, 0:2 * 192].rearrange("p (m n) -> p m n", m=2), last, 1 / W_UP)
                    elif s == "mrope":
                        act.wait_ge(*mrope(r))
                        if k is None or k >= 1:
                            act.wait_ge(*filled(r - 1, fl.filled("am")))
                        copy(mq2[:, 0], mq, mq_hi)
                    elif s in ("mqT", "mkT"):
                        copy(mqT[:, "qk".index(s[1])], ps16[b][0:HP, :].rearrange("p (s n) -> p s n", s=2), last)
                    elif s == "ms":
                        act.wait_ge(*m_max(r))
                        if k is None or k >= 1:
                            act.wait_ge(*bm_step(r - 1, 2))
                        for m in range(PAIRS):
                            nc.scalar.activation(mp[:, m, :], ps[b][:, m * P:(m + 1) * P], ACT.Exp, bias=mmax[:, m:m + 1],
                                                 accum_out=msum[:, m:m + 1]).then_inc(*(last if m == PAIRS - 1 else m_exp).up)
                    elif s == "mpT":
                        copy(mpT[:, 0], ps[b][:].rearrange("p (m n) -> p m n", m=PAIRS), hi)
                    elif s == "am":
                        copy(am[:, 0], ps[b][:, 0:PAIRS * SLOTS], hi)
                    elif s[:2] == "gt":
                        g = int(s[2])
                        if k is None or k >= 1:
                            act.wait_ge(*o_ps(r - 1))
                        copy(GT[:, 2 * g:2 * g + 2, :], ps16[b].rearrange("p (m n) -> p m n", m=2), last)
                    elif s in ("bw0", "bw1"):
                        g = int(s[2])
                        src = ps[b][:].rearrange("p (t n) -> p t n", n=D)
                        copy(w[:, 2 * g:2 * g + 2, :], src, hi, 1 / W_UP)
                        nc.scalar.activation(w2[:, 2 * g:2 * g + 2, :], src, ACT.Square, scale=1 / W_UP).then_inc(*last.up)
                    elif s == "bexp":
                        act.wait_ge(*pi(r, 6))
                        nc.scalar.activation(bl[:], bl[:], ACT.Exp).then_inc(*pi_exp.up)
                    elif s in ("oT0", "oT1"):
                        copy(hT[:, int(s[2]), 0], ps[b][:], hi)

                def end(r, g, part, k):
                    if part == 0:
                        act.wait_ge(*av_set(r, 2 * g + 2))
                        if g:
                            act.wait_ge(*av_flip(r, g))
                        elif k is None or k >= 1:
                            act.wait_ge(*av_flip(r - 1))
                        copy(av[:, 0], av32[:], av_hi)
                    elif part == 1:
                        act.wait_ge(*av_flip(r, g + 1))
                        if g:
                            act.wait_ge(*o_ps(r, g))
                        elif k is None or k >= 1:
                            act.wait_ge(*o_ps(r - 1))
                        copy(avT[:], ps16[5].rearrange("p (s m n) -> p s m n", s=2, m=PAIRS), avT_set)

                def back(r, side, k):
                    for i in range(SLOT_N):
                        if i < NI:
                            qt, n = item(i)
                            nk = (qt + 1) * P
                            act.wait_ge(*s_max(r, i + 1))
                            if i >= 2:
                                act.wait_ge(*p_flip(r, i - 1))
                            elif k is None or k >= 1:
                                act.wait_ge(*p_flip(r - 1))
                            if i == 0 and (k is None or k >= 1):
                                act.wait_ge(*av_set(r - 1))
                            nc.scalar.activation(prob[:, i % 2, 0:nk], ps[i % 2][:, 0:nk], ACT.Exp, bias=nmax[:, i % 4:i % 4 + 1],
                                                 accum_out=rsum[:, qt * NH + n:qt * NH + n + 1]).then_inc(*s_exp.up)
                        if 1 <= i <= NI:
                            j = i - 1
                            nk = (item(j)[0] + 1) * P
                            act.wait_ge(*p_flip(r, j + 1))
                            if j >= 3:
                                act.wait_ge(*av_ps(r, j - 2))
                            elif k is None or k >= 1:
                                act.wait_ge(*av_ps(r - 1))
                            copy(pT[:, j % 3, 0, 0:nk], ps[2 + j % 2][:, 0:nk], p_hi)
                        for g, part, ago in due(i, k):
                            end(r - ago, g, part, k)
                        for s in own["act"].get(i, ()):
                            step(r, r.parity, k, s)
                        side(i)

                front_back(act, NB, run_front(step, ahead["act"]), back)
                end(Round(NB // 2 - 1, 1), TILES - 1, 1, None)
                end(Round(NB // 2 - 1, 1), TILES - 1, 2, None)

            @block.vector
            def _(dve):
                V = nc.vector
                dve.wait_ge(*const_in(0))
                dve.wait_ge(*ones_set(0))
                s0 = Chain(dve, split, 0)
                for src, name, to, n in chunked:
                    src = src.rearrange("p (k n) -> p k n", n=n)
                    if name == "dwqkv":
                        s0.link(V.tensor_scalar(src[:, :, 0:HW], src[:, :, 0:HW], SCALE, None, ALU.mult))
                    if name == "mwqkv":
                        for c in range(KC):
                            qs = src[:, c, :].rearrange("p (h n) -> p h n", n=3 * HP)[:, :, 0:HP]
                            s0.inc(V.tensor_scalar(qs, qs, SCALE, None, ALU.mult))
                        s0.sync()
                    s0.link(V.tensor_scalar(to[:, 0], src, W_UP, None, ALU.mult))
                    s0.inc(V.scalar_tensor_tensor(to[:, 1], src, W_UP, to[:, 0], ALU.mult, ALU.subtract))
                s0.link(V.tensor_copy(tb[:, :, 0, 0:ROT], tb32[:]))
                s0.inc(V.tensor_tensor(tb[:, :, 1, 0:ROT], tb32[:], tb[:, :, 0, 0:ROT], ALU.subtract))
                s0.inc(V.memset(m8[:], 0.0))
                s0.end()
                dve.wait_ge(*split(0))

                def layernorm(part, up, r, src):
                    if part == "A":
                        c = open_["ln"] = Chain(dve, up, r)
                        for t in range(TILES):
                            c.inc(V.bn_stats(stats[:, t, :], src[:, t, :]))
                        c.sync()
                        settle(dve)
                        for t in range(TILES):
                            c.inc(V.bn_aggr(mv[:, t, :], stats[:, t, :]))
                        c.sync()
                        c.link(V.tensor_scalar(ve[:], mv[:, :, 1], LN_EPS, None, ALU.add))
                        return
                    c = open_["ln"]
                    if part in "BC":
                        rsqrt(nc, c, rs[:], ve[:], rt[:], "BC".index(part))
                    else:
                        for t in range(TILES):
                            c.inc(V.tensor_scalar(h32[:, t, :], src[:, t, :], mv[:, t, 0:1], rs[:, t:t + 1], ALU.subtract, ALU.mult))
                        c.end()

                heads = lambda z: z.rearrange("p t (h d) -> p t h d", d=DB)
                last = read["dve"]
                open_ = {}

                def low(r, s, to, src, high, n_hi, op_scale=None):
                    dve.wait_ge(*hi(r, n_hi))
                    if op_scale is None:
                        V.tensor_tensor(to, src, high, ALU.subtract).then_inc(*last.up)
                    else:
                        V.scalar_tensor_tensor(to, src, op_scale, high, ALU.mult, ALU.subtract).then_inc(*last.up)

                def step(r, p, k, s):
                    if fl.reader.get(s) == "dve" or s == "ms":
                        dve.wait_ge(*filled(r, fl.filled(s)))
                        b = fl.bank(s)
                    if s == "x1b":
                        dve.wait_ge(*x_part(r))
                        V.tensor_tensor(x[:, p], x[:, p], gy[:, :, 1, :], ALU.add).then_inc(*x_made.up)
                    elif s[:4] == "b_ln":
                        if s[4] == "A":
                            dve.wait_ge(*x_in(r))
                        layernorm(s[4], b_ln, r, x2)
                    elif s[:2] == "ln":
                        if s[2] == "A":
                            dve.wait_ge(*x_ready(r))
                        if s[2] == "D" and not first:
                            dve.wait_ge(*bh_lo(r))
                        layernorm(s[2], ln, r, x[:, p])
                    elif s[:3] == "top":
                        i = int(s[3])
                        if i == 0:
                            open_["pick"] = Chain(dve, pick, r)
                            dve.wait_ge(*read["act"](r, fl.read("score")))
                        c_ = open_["pick"]
                        src = scT[:] if i == 0 else wk[:]
                        settle(dve)
                        c_.link(V.max(m8[:], src))
                        settle(dve)
                        c_.link(V.match_replace(wk[:], m8[:], src, NEG))
                    elif s[:4] == "rank":
                        c_ = open_["pick"]
                        if s == "rank0":
                            if k is None or k >= 1:
                                dve.wait_ge(*filled(r - 1, fl.filled("sel")))
                            c_.link(V.tensor_tensor(wk[:], wk[:], scT[:], ALU.not_equal))
                        elif s == "rank1":
                            c_.link(V.tensor_tensor_scan(selT[:], over(onesf[0:NH, 0:1], [0, NT]), wk[:], 0.0, ALU.mult, ALU.add))
                        else:
                            c_.link(V.tensor_tensor(selT[:], wk[:], selT[:], ALU.mult))
                            c_.end()
                    elif s[0] == "v" and len(s) == 2:
                        t = int(s[1])
                        low(r, s, v[:, p, 1, t, :], ps[b][:], v[:, p, 0, t, :], HN[s], 1 / W_UP)
                    elif s[:4] == "rope":
                        t = int(s[5:])
                        x2d = raw[:].rearrange("p (h d) -> p h d", d=HP)[:, :, 0:ROT]
                        if s[4] == "A":
                            dve.wait_ge(*read["act"](r, fl.read(f"k{t}")))
                            V.tensor_tensor(ra[:], x2d, over(cosd[:, t, :], [0, 2 * NH], [1, ROT]), ALU.mult).then_inc(*rope_a.up)
                        else:
                            dve.wait_ge(*rope_a(r, t + 1))
                            dve.wait_ge(*rope_b(r, t + 1))
                            V.tensor_tensor(x2d, ra[:], rc[:], ALU.add).then_inc(*rope.up)
                    elif s == "sel":
                        low(r, s, tb[:, :, 1, ROT:], ps[b][:, TILES * NH:2 * TILES * NH].rearrange("p (t n) -> p t n", n=NH), tb[:, :, 0, ROT:], HN[s])
                    elif s[0] == "G":
                        t = int(s[1])
                        V.tensor_tensor(G[:, t, :].rearrange("p (n k) -> p n k", k=SLOTS), over(slot1[:], [0, NH], [1, SLOTS]),
                                        over(sel[:, t, :], [1, NH], [0, SLOTS]), ALU.is_equal).then_inc(*g_set.up)
                    elif s in ("xg0", "xg1"):
                        c = int(s[2])
                        low(r, s, xgT[:, c, 1, :], ps[b][:], xgT[:, c, 0, :], HN[s])
                    elif s == "aux":
                        sums = ps[b][:, 0:PAIRS * 2 * TW].rearrange("p (m s n) -> p m s n", m=PAIRS, s=2)
                        V.tensor_copy(aux[:].rearrange("p (m n) -> p m n", m=PAIRS), sums[:, :, 0, :]).then_inc(*aux_hi.up)
                        dve.wait_ge(*aux_hi(r))
                        V.tensor_tensor(aux[:].rearrange("p (m n) -> p m n", m=PAIRS), aux[:].rearrange("p (m n) -> p m n", m=PAIRS), sums[:, :, 1, :],
                                        ALU.add).then_inc(*last.up)
                        dve.wait_ge(*last(r, fl.read("aux")))
                        for q in range(2):
                            V.tensor_scalar(gsc[q * SLOTS:(q + 1) * SLOTS, :], over(aux[q * SLOTS:(q + 1) * SLOTS, ROT + q:ROT + q + 1], [TW + 2, PAIRS]),
                                            -1.0, 80.0, ALU.mult, ALU.min).then_inc(*aux_step.up)
                    elif s == "mrope":
                        c_ = Chain(dve, mrope, r)
                        dve.wait_ge(*read["act"](r, fl.read("mq1")))
                        qk_ = mq[:, :, 0:2 * HP].rearrange("p m (j d) -> p m j d", j=2)
                        x1, x2_ = qk_[:, :, :, 0:HALF], qk_[:, :, :, HALF:ROT]
                        cc, ss = (over(aux[:, o:o + 1], [TW, PAIRS], [0, 2], [1, HALF]) for o in (0, HALF))
                        c_.inc(V.tensor_tensor(r4[:, 0], x1, cc, ALU.mult))
                        c_.inc(V.tensor_tensor(r4[:, 1], x2_, ss, ALU.mult))
                        c_.inc(V.tensor_tensor(r4[:, 2], x1, ss, ALU.mult))
                        c_.link(V.tensor_tensor(r4[:, 3], x2_, cc, ALU.mult))
                        c_.inc(V.tensor_tensor(x1, r4[:, 0], r4[:, 1], ALU.subtract))
                        c_.inc(V.tensor_tensor(x2_, r4[:, 2], r4[:, 3], ALU.add))
                        c_.end()
                    elif s == "mlow":
                        dve.wait_ge(*mq_hi(r))
                        V.tensor_tensor(mq2[:, 1], mq, mq2[:, 0], ALU.subtract).then_inc(*mq_lo.up)
                    elif s == "ms":
                        V.tensor_reduce(mmax[:], ps[b][:].rearrange("p (m n) -> p m n", m=PAIRS), AX, ALU.max, negate=True).then_inc(*m_max.up)
                    elif s == "mpT":
                        low(r, s, mpT[:, 1], ps[b][:].rearrange("p (m n) -> p m n", m=PAIRS), mpT[:, 0], HN[s])
                    elif s == "am":
                        low(r, s, am[:, 1], ps[b][:, 0:PAIRS * SLOTS], am[:, 0], HN[s])
                    elif s in ("bm0", "bm1"):
                        g = int(s[2])
                        if g == 0:
                            open_["bm"] = c_ = Chain(dve, bm_step, r)
                            dve.wait_ge(*gate_exp(r))
                            dve.wait_ge(*read["act"](r, fl.read("ms")))
                            c_.link(V.tensor_scalar(gr[:], gex[:], 1.0, None, ALU.add))
                            c_.link(V.tensor_tensor(gr[:], gr[:], msum[:], ALU.mult))
                            c_.link(V.reciprocal(gr[:], gr[:]))
                            if k is None or k >= 1:
                                dve.wait_ge(*o_ps(r - 1))
                        c_ = open_["bm"]
                        for m in (2 * g, 2 * g + 1):
                            src = ps[b][:, m % 2 * D:(m % 2 + 1) * D]
                            c_.inc(V.tensor_scalar(bm[:, 0, m, :], src, gr[:, m:m + 1], None, ALU.mult))
                        c_.sync()
                        for m in (2 * g, 2 * g + 1):
                            src = ps[b][:, m % 2 * D:(m % 2 + 1) * D]
                            ins = V.scalar_tensor_tensor(bm[:, 1, m, :], src, gr[:, m:m + 1], bm[:, 0, m, :], ALU.mult, ALU.subtract)
                            ins.then_inc(*last.up) if m % 2 else c_.inc(ins)
                    elif s == "bss":
                        c_ = open_["pi"] = Chain(dve, pi, r)
                        V.tensor_scalar(inv[:], ps[b][:, 0:D], 1e-24, None, ALU.max).then_inc(*last.up)
                        dve.wait_ge(*last(r, fl.read("bss")))
                        c_.link(V.reciprocal(inv[:], inv[:]))
                    elif s == "bnorm":
                        c_ = open_["pi"]
                        c_.link(V.tensor_tensor(pw[:, :, 0:D], w2, over(inv[:], [0, TILES], [1, D]), ALU.mult))
                    elif s == "blog":
                        c_ = open_["pi"]
                        c_.link(V.tensor_reduce(bl[:], heads(pw[:, :, 0:D]), AX, ALU.add))
                        c_.link(V.tensor_tensor(bl[:], bl[:], over(btemp[:], [0, TILES], [1, HB]), ALU.mult))
                        c_.link(V.tensor_reduce(bmx[:], bl[:], AX, ALU.max))
                        c_.link(V.tensor_tensor(bl[:], bl[:], over(bmx[:], [1, TILES], [0, HB]), ALU.subtract))
                    elif s == "bpi":
                        c_ = open_["pi"]
                        dve.wait_ge(*pi_exp(r))
                        c_.link(V.tensor_reduce(bsm[:], bl[:], AX, ALU.add))
                        c_.link(V.reciprocal(bsm[:], bsm[:]))
                        c_.link(V.tensor_tensor(pw[:, :, D:], bl[:], over(bsm[:], [1, TILES], [0, HB]), ALU.mult))
                    elif s == "bpiw":
                        c_ = open_["pi"]
                        c_.link(V.tensor_tensor(heads(pw[:, :, 0:D]), heads(w2), over(pw[:, 0, D:], [PW, TILES], [1, HB], [0, DB]), ALU.mult))
                        c_.end()
                    elif s == "bdot":
                        V.tensor_copy(dot, ps[b][:, 0:PW]).then_inc(*last.up)
                    elif s == "res":
                        c_ = open_["res"] = Chain(dve, res, r)
                        dve.wait_ge(*last(r, fl.read("bdot")))
                        c_.link(V.tensor_scalar(bden[:], dot[:, D:PW], 1e-8, None, ALU.add))
                        c_.link(V.reciprocal(bden[:], bden[:]))
                        c_.link(V.tensor_tensor(attn[:].rearrange("p (h d) -> p h d", d=DB), dot[:, 0:D].rearrange("p (h d) -> p h d", d=DB),
                                                over(bden[:], [1, HB], [0, DB]), ALU.mult))
                        c_.link(V.tensor_scalar(attn[:], attn[:], 1.0, None, ALU.add))
                        c_.link(V.reciprocal(attn[:], attn[:]))
                    elif s == "resw":
                        c_ = open_["res"]
                        dve.wait_ge(*w_pi(r))
                        c_.link(V.scalar_tensor_tensor(w, w, -1.0, over(attn[:], [0, TILES], [1, D]), ALU.mult, ALU.mult))
                        c_.end()
                    elif s in ("oT0", "oT1"):
                        c = int(s[2])
                        low(r, s, hT[:, c, 1], ps[b][:], hT[:, c, 0], HN[s])
                    elif s in ("bo0", "bo1"):
                        g = int(s[2])
                        dve.wait_ge(*xb_set(r))
                        if k is None and g == 0:
                            dve.wait_ge(*out_made(r - 2))
                        src = ps[b][:].rearrange("p (t n) -> p t n", n=D)
                        V.scalar_tensor_tensor(x[:, p, 2 * g:2 * g + 2, :], src, 1 / W_UP, x2[:, 2 * g:2 * g + 2, :], ALU.mult, ALU.add).then_inc(*last.up)

                def end(r, g, part, k):
                    if part == 0:
                        qt = QORDER[g]
                        dve.wait_ge(*s_exp(r, (g + 1) * NH))
                        V.reciprocal(rinv[:], rsum[:, qt * NH:(qt + 1) * NH]).then_inc(*av_set.up)
                        dve.wait_ge(*av_set(r, 2 * g + 1))
                        dve.wait_ge(*av_ps(r, (g + 1) * NH))
                        if g:
                            dve.wait_ge(*av_lo(r, g))
                        elif k is None or k >= 1:
                            dve.wait_ge(*av_lo(r - 1))
                        V.tensor_tensor(av32[:].rearrange("p (n d) -> p n d", d=HP), ps[4][:].rearrange("p (n d) -> p n d", d=HP),
                                        over(rinv[:], [1, NH], [0, HP]), ALU.mult).then_inc(*av_set.up)
                    elif part == 2:
                        qt = QORDER[g]
                        dve.wait_ge(*o_ps(r, g + 1))
                        if g == 0 and (k is None or k >= 1):
                            dve.wait_ge(*out_done(r - 1))
                        V.scalar_tensor_tensor(xo[:, qt, :], ps[5][:, 0:D], 1 / W_UP, x[:, r.parity, qt, :], ALU.mult, ALU.add).then_inc(*out_made.up)

                def maxima(r, k, i):
                    nk = (item(i)[0] + 1) * P
                    dve.wait_ge(*s_ps(r, i + 1))
                    if i >= 4:
                        dve.wait_ge(*s_exp(r, i - 3))
                    elif k is None or k >= 1:
                        dve.wait_ge(*s_exp(r - 1))
                    V.tensor_reduce(nmax[:, i % 4:i % 4 + 1], ps[i % 2][:, 0:nk], AX, ALU.max, negate=True).then_inc(*s_max.up)

                def back(r, side, k):
                    p = r.parity
                    maxima(r, k, 0)
                    for i in range(SLOT_N):
                        if 2 <= i <= NI + 1:
                            j = i - 2
                            nk = (item(j)[0] + 1) * P
                            dve.wait_ge(*p_hi(r, j + 1))
                            V.tensor_tensor(pT[:, j % 3, 1, 0:nk], ps[2 + j % 2][:, 0:nk], pT[:, j % 3, 0, 0:nk], ALU.subtract).then_inc(*p_lo.up)
                        for g, part, ago in due(i, k):
                            end(r - ago, g, part, k)
                        if i + 1 < NI:
                            maxima(r, k, i + 1)
                        for s in own["dve"].get(i, ()):
                            step(r, p, k, s)
                        side(i)

                front_back(dve, NB, run_front(step, ahead["dve"]), back)
                end(Round(NB // 2 - 1, 1), TILES - 1, 1, None)
                end(Round(NB // 2 - 1, 1), TILES - 1, 2, None)


def hybrid_block_program(nc, a):
    a["resid"] = nc.dram_tensor("resid", (NB, NT, D), F32, kind="Internal").ap()
    a["dispatched"] = nc.dram_tensor("dispatched", (NE * CAP, D), F32, kind="Internal").ap()
    a["expert_out"] = nc.dram_tensor("expert_out", (NE * CAP, D), F32, kind="Internal").ap()
    a["mid"] = nc.dram_tensor("mid", (NB, NT, D), F32, kind="Internal").ap()
    with ExitStack() as ctx:
        a["lasting"] = ctx
        a["slot_of"] = ctx.enter_context(nc.sbuf_tensor("slot_of", [P, NB * TILES * TOPK], U32))
        a["gate_of"] = ctx.enter_context(nc.sbuf_tensor("gate_of", [P, NB * TILES * TOPK], F32))
        attention_a_stage(nc, a)
        expert_stage(nc, a)
        a["mixing"] = mixing_weights(nc, ctx)
        mixing_stage(nc, a, True)
        mixing_stage(nc, a, False)


def host_layout(inputs):
    f = np.float32
    inp = {k: np.ascontiguousarray(np.asarray(v)) for k, v in inputs.items()}
    rep = lambda v: np.ascontiguousarray(np.broadcast_to(v.reshape(1, -1), (P, v.size)))
    A = "L0_attn_a_"
    d = {
        "x": inp[A + "x"],
        "wqkvg": np.concatenate([inp[A + w] for w in ("Wq", "Wk", "Wv", "Wg")], axis=1),
        "wo": inp[A + "Wo"], "rw": inp[A + "router_W"],
        "s1": np.ascontiguousarray(inp[A + "norm1_scale"].reshape(KC, P).T),
        "s2b": rep(inp[A + "norm2_scale"]),
        "bqkvg": rep(np.concatenate([inp[A + b] for b in ("bq", "bk", "bv", "bg")])),
        "bo": rep(inp[A + "bo"]), "rb": rep(inp[A + "router_b"]),
        "w1": inp[A + "W1"], "w2": inp[A + "W2"],
        "b1": np.ascontiguousarray(inp[A + "b1"].reshape(NE, MC, P).transpose(2, 0, 1)),
        "b2": rep(inp[A + "b2"]).reshape(P, NE, D),
        "bw": np.ascontiguousarray(inp["L0_attn_b_Wqkv"].T), "bwout": np.ascontiguousarray(inp["L0_attn_b_Wout"].T),
        "btemp": rep(inp["L0_attn_b_temp"]), "bbout": rep(inp["L0_attn_b_bout"]),
        "mrw": inp["L0_ffn_mosa_router_w"],
        "mwqkv": inp["L0_ffn_mosa_wqkv"].reshape(D, NH * 3 * HP),
        "mwo": inp["L0_ffn_mosa_wo"],
        "dwqkv": np.ascontiguousarray(inp["L0_ffn_dense_wqkv"].reshape(D, NH, 3, HP).transpose(0, 2, 1, 3)).reshape(D, 3 * NH * HP),
        "dwo": inp["L0_ffn_dense_wo"],
    }
    pos = np.arange(NT, dtype=f).reshape(TILES, P).T
    half = DA // 2
    inv = (f(1.0) / np.power(f(10000.0), np.arange(half, dtype=f) / f(half))).astype(f)
    ang = pos[..., None] * inv
    sin, cos = np.sin(ang).astype(f), np.cos(ang).astype(f)
    d["cosa"] = np.concatenate([cos, cos], axis=-1)
    d["sina"] = np.concatenate([-sin, sin], axis=-1)
    half = ROT // 2
    inv = np.power(f(10000.0), -np.arange(half, dtype=f) / f(half)).astype(f)
    ang = pos[..., None] * inv
    sin, cos = np.sin(ang).astype(f), np.cos(ang).astype(f)
    d["cosd"] = np.concatenate([cos, cos], axis=-1)
    d["sind"] = np.concatenate([-sin, sin], axis=-1)
    d["rope_rows"] = np.concatenate([cos, sin], axis=-1)
    part = np.arange(P)
    d["ident"] = np.eye(P, dtype=f)
    d["bd"] = np.ascontiguousarray(np.tile((part[:, None] // DA == np.arange(GRP)[None, :]).astype(f)[:, None, :, None], (1, 2, 1, VA)).reshape(P, -1))
    bf = mybir.dt.np(BF16)
    d["before"] = (part[:, None] < part[None, :]).astype(f).astype(bf)
    d["iota8"] = np.ascontiguousarray(np.broadcast_to(np.arange(NE, dtype=f), (P, TOPK, NE)))
    d["ident16"] = np.eye(P, dtype=mybir.dt.np(F16))
    d["identb"] = np.eye(P, dtype=f).astype(bf)
    d["causal"] = np.where(part[:, None] >= part[None, :], 0.0, NEG).astype(bf)
    d["causal_pair"] = np.where((part[:, None] >= part[None, :]) & (part[:, None] // SLOTS == part[None, :] // SLOTS), 0.0, NEG).astype(bf)
    d["slot1"] = np.ascontiguousarray(np.broadcast_to(np.arange(1, SLOTS + 1, dtype=f), (P, SLOTS)))
    return {k: np.ascontiguousarray(v) for k, v in d.items()}


def kernel(**inputs):
    import concourse.bacc as bacc
    from concourse.bass_utils import run_bass_kernel_spmd

    nc = bacc.Bacc("TRN2", target_bir_lowering=False, num_devices=1)
    arrays = host_layout(inputs)
    a = {name: nc.dram_tensor(name, v.shape, mybir.dt.from_np(v.dtype), kind="ExternalInput").ap() for name, v in arrays.items()}
    a["out"] = nc.dram_tensor("out", (NB, NT, D), F32, kind="ExternalOutput").ap()
    hybrid_block_program(nc, a)
    got = run_bass_kernel_spmd(nc, [arrays], core_ids=[0])
    return got.results[0]["out"]
```
